# Optimizing a Trainium2 kernel written in Bass

```python
import numpy as np
import jax
import jax.numpy as jnp

def _softmax(x, axis=-1):
    return jax.nn.softmax(x, axis=axis)

def _gelu(x):
    return jax.nn.gelu(x, approximate=True)

def _silu(x):
    return jax.nn.silu(x)

def _sigmoid(x):
    return jax.nn.sigmoid(x)

def _layernorm(x, axis=-1, eps=1e-05):
    m = jnp.mean(x, axis=axis, keepdims=True)
    v = jnp.var(x, axis=axis, keepdims=True)
    return (x - m) / jnp.sqrt(v + eps)

def _scatter_add(tgt, idx, src, axis=0):
    return tgt.at[idx].add(src)

def _segment_sum(src, seg, n):
    return jax.ops.segment_sum(src, seg, n)
kernel_name = 'mk_gnn_resnorm_d2_gnn_r32_6e8c11'

def setup_inputs(seed: int=0):
    np.random.seed(seed)
    _w = jnp.asarray

    def _rec_inputs():
        import jax
        import jax.numpy as jnp
        _gk = jax.random.key(seed)
        x = -0.000202 + 1 * jax.random.normal(jax.random.fold_in(_gk, 1), (50000, 128), jnp.float32)
        src = jax.random.randint(jax.random.fold_in(_gk, 2), (50000,), 0, 50000, jnp.int32)
        dst = jax.random.randint(jax.random.fold_in(_gk, 3), (50000,), 0, 50000, jnp.int32)
        _o = jnp.argsort(dst, stable=True)
        src = src[_o]
        dst = dst[_o]
        edge_attr_128 = -5.16925e-05 + 1.00005 * jax.random.normal(jax.random.fold_in(_gk, 12), (50000, 128), jnp.float32)
        edge_attr_64 = 0.000189758 + 1.00013 * jax.random.normal(jax.random.fold_in(_gk, 13), (50000, 64), jnp.float32)
        return (x, src, dst, edge_attr_128, edge_attr_64)
    x, src, dst, edge_attr_128, edge_attr_64 = _rec_inputs()

    def _L0_gnn_setup():
        import jax, jax.numpy as jnp
        import numpy as np
        N_NODES = 50000
        N_EDGES = 25000
        C = 128
        D = 64
        Z_DIM = 2 * C + D
        EPS = 1e-05
        key = jax.random.key(seed)
        ks = jax.random.split(key, 8)
        x = jax.random.normal(ks[0], (N_NODES, C), dtype=jnp.float32)
        edge_index = jax.random.randint(ks[1], (2, N_EDGES), 0, N_NODES, dtype=jnp.int64)
        edge_attr = jax.random.normal(ks[2], (N_EDGES, D), dtype=jnp.float32)
        scale = 1.0 / np.sqrt(Z_DIM)
        W_f = jax.random.normal(ks[3], (C, Z_DIM), dtype=jnp.float32) * scale
        b_f = jnp.zeros((C,), dtype=jnp.float32)
        W_s = jax.random.normal(ks[4], (C, Z_DIM), dtype=jnp.float32) * scale
        b_s = jnp.zeros((C,), dtype=jnp.float32)
        gamma = jnp.ones((C,), dtype=jnp.float32)
        beta = jnp.zeros((C,), dtype=jnp.float32)
        return {'x': x, 'edge_index': edge_index, 'edge_attr': edge_attr, 'W_f': W_f, 'b_f': b_f, 'W_s': W_s, 'b_s': b_s, 'gamma': gamma, 'beta': beta}
    _L0_gnn_all = _L0_gnn_setup()
    _L0_gnn_in = {k: v for k, v in _L0_gnn_all.items() if k in ('W_f', 'b_f', 'W_s', 'b_s', 'gamma', 'beta')}
    del _L0_gnn_all

    def _L1_gnn_setup():
        import jax, jax.numpy as jnp
        import numpy as np
        N_NODES = 50000
        N_EDGES = 25000
        D = 128
        L = 3
        BN_EPS = 1e-05

        def _bn(h, gamma, beta):
            m = h.mean(axis=0)
            v = h.var(axis=0)
            return gamma * (h - m) * jax.lax.rsqrt(v + BN_EPS) + beta
        key = jax.random.key(seed)
        ks = jax.random.split(key, 12)
        x = jax.random.normal(ks[0], (N_NODES, D), dtype=jnp.float32)
        edge_index = jax.random.randint(ks[1], (2, N_EDGES), 0, N_NODES, dtype=jnp.int64)
        edge_attr = jax.random.normal(ks[2], (N_EDGES, D), dtype=jnp.float32)
        batch = jnp.zeros((N_NODES,), dtype=jnp.int64)
        s = 1.0 / np.sqrt(D)
        W1 = jax.random.uniform(ks[3], (L, D, D), jnp.float32, -s, s)
        b1 = jax.random.uniform(ks[4], (L, D), jnp.float32, -s, s)
        g_mlp = jnp.ones((L, D), jnp.float32)
        be_mlp = jnp.zeros((L, D), jnp.float32)
        W2 = jax.random.uniform(ks[5], (L, D, D), jnp.float32, -s, s)
        b2 = jax.random.uniform(ks[6], (L, D), jnp.float32, -s, s)
        g_out = jnp.ones((L, D), jnp.float32)
        be_out = jnp.zeros((L, D), jnp.float32)
        return {'x': x, 'edge_index': edge_index, 'edge_attr': edge_attr, 'batch': batch, 'W1': W1, 'b1': b1, 'g_mlp': g_mlp, 'be_mlp': be_mlp, 'W2': W2, 'b2': b2, 'g_out': g_out, 'be_out': be_out}
    _L1_gnn_all = _L1_gnn_setup()
    _L1_gnn_in = {k: v for k, v in _L1_gnn_all.items() if k in ('W1', 'b1', 'g_mlp', 'be_mlp', 'W2', 'b2', 'g_out', 'be_out')}
    del _L1_gnn_all
    return {'x': x, 'src': src, 'dst': dst, 'edge_attr_128': edge_attr_128, 'edge_attr_64': edge_attr_64, 'L0_gnn_W_f': _L0_gnn_in['W_f'], 'L0_gnn_b_f': _L0_gnn_in['b_f'], 'L0_gnn_W_s': _L0_gnn_in['W_s'], 'L0_gnn_b_s': _L0_gnn_in['b_s'], 'L0_gnn_gamma': _L0_gnn_in['gamma'], 'L0_gnn_beta': _L0_gnn_in['beta'], 'L1_gnn_W1': _L1_gnn_in['W1'], 'L1_gnn_b1': _L1_gnn_in['b1'], 'L1_gnn_g_mlp': _L1_gnn_in['g_mlp'], 'L1_gnn_be_mlp': _L1_gnn_in['be_mlp'], 'L1_gnn_W2': _L1_gnn_in['W2'], 'L1_gnn_b2': _L1_gnn_in['b2'], 'L1_gnn_g_out': _L1_gnn_in['g_out'], 'L1_gnn_be_out': _L1_gnn_in['be_out']}

def reference(x, src, dst, edge_attr_128, edge_attr_64, L0_gnn_W_f, L0_gnn_b_f, L0_gnn_W_s, L0_gnn_b_s, L0_gnn_gamma, L0_gnn_beta, L1_gnn_W1, L1_gnn_b1, L1_gnn_g_mlp, L1_gnn_be_mlp, L1_gnn_W2, L1_gnn_b2, L1_gnn_g_out, L1_gnn_be_out):
    import jax
    import jax.numpy as jnp

    def _L0_gnn_ref(x, edge_index, edge_attr, W_f, b_f, W_s, b_s, gamma, beta):
        import jax, jax.numpy as jnp
        import numpy as np
        N_NODES = 50000
        N_EDGES = 25000
        C = 128
        D = 64
        Z_DIM = 2 * C + D
        EPS = 1e-05
        src = edge_index[0]
        dst = edge_index[1]
        z = jnp.concatenate([x[dst], x[src], edge_attr], axis=-1)
        gate = jax.nn.sigmoid(z @ W_f.T + b_f)
        val = jax.nn.softplus(z @ W_s.T + b_s)
        msg = gate * val
        summed = jax.ops.segment_sum(msg, dst, num_segments=N_NODES)
        count = jax.ops.segment_sum(jnp.ones((msg.shape[0],), msg.dtype), dst, num_segments=N_NODES)
        mean_agg = summed / jnp.maximum(count, 1.0)[:, None]
        out = x + mean_agg
        mu = jnp.mean(out, axis=0)
        var = jnp.mean((out - mu) ** 2, axis=0)
        y = gamma * (out - mu) * jax.lax.rsqrt(var + EPS) + beta
        return y

    def _L1_gnn_ref(x, edge_index, edge_attr, batch, W1, b1, g_mlp, be_mlp, W2, b2, g_out, be_out):
        import jax, jax.numpy as jnp
        import numpy as np
        N_NODES = 50000
        N_EDGES = 25000
        D = 128
        L = 3
        BN_EPS = 1e-05

        def _bn(h, gamma, beta):
            m = h.mean(axis=0)
            v = h.var(axis=0)
            return gamma * (h - m) * jax.lax.rsqrt(v + BN_EPS) + beta
        src, dst = (edge_index[0], edge_index[1])
        for i in range(L):
            msg = jax.nn.relu(x[src] + edge_attr)
            aggr = jax.ops.segment_sum(msg, dst, num_segments=N_NODES)
            h = x + aggr
            h = h @ W1[i] + b1[i]
            h = jax.nn.relu(_bn(h, g_mlp[i], be_mlp[i]))
            h = h @ W2[i] + b2[i]
            h = _bn(h, g_out[i], be_out[i])
            if i != L - 1:
                h = jax.nn.relu(h)
            x = h
        return x
    edge_index = jnp.stack([src, dst])
    batch0 = jnp.zeros((50000,), jnp.int32)
    x = _layernorm(x + _L0_gnn_ref(x, edge_index, edge_attr_64, L0_gnn_W_f, L0_gnn_b_f, L0_gnn_W_s, L0_gnn_b_s, L0_gnn_gamma, L0_gnn_beta), axis=-1)
    x = _layernorm(x + _L1_gnn_ref(x, edge_index, edge_attr_128, batch0, L1_gnn_W1, L1_gnn_b1, L1_gnn_g_mlp, L1_gnn_be_mlp, L1_gnn_W2, L1_gnn_b2, L1_gnn_g_out, L1_gnn_be_out), axis=-1)
    return x

_drawn_inputs = setup_inputs


def setup_inputs(seed=0):
    import zlib

    import numpy as np

    out = dict(_drawn_inputs(seed))
    spreads = {'L0_gnn_b_f': (0.0, 0.8),
     'L0_gnn_b_s': (0.0, 0.8),
     'L0_gnn_gamma': (1.0, 0.2),
     'L0_gnn_beta': (0.0, 0.1),
     'L1_gnn_g_mlp': (1.0, 0.2),
     'L1_gnn_be_mlp': (0.0, 0.1),
     'L1_gnn_g_out': (1.0, 0.2),
     'L1_gnn_be_out': (0.0, 0.1)}
    factors = {'L1_gnn_b1': 8.0, 'L1_gnn_b2': 8.0}
    for name, (base, spread) in spreads.items():
        noise = np.random.default_rng([zlib.crc32(name.encode()), seed]).standard_normal(out[name].shape)
        drawn = base * np.exp(spread * noise) if base else spread * noise
        out[name] = jnp.asarray(drawn.astype(out[name].dtype))
    for name, factor in factors.items():
        out[name] = (out[name] * factor).astype(out[name].dtype)
    return out
```

```python
import concourse.bass as bass
from concourse import mybir
from contextlib import ExitStack, contextmanager

F32 = mybir.dt.float32
I32 = mybir.dt.int32
ALU = mybir.AluOpType
ACT = mybir.ActivationFunctionType

P = 128
N = 50000
E = 50000
C = 128
D0 = 64
LAYERS = 3
EPS = 1e-5
T = 6
BLOCK = T * P
HALF = BLOCK // 2
BLOCKS = N // BLOCK
PAIRS = BLOCKS // 2
TILES = N // P
TAIL = N - TILES * P
CHUNKS = 2 * BLOCKS + 1
BANK = 512
AGG = C + 4
AGG_ROWS = N + P

assert N == E and N == BLOCKS * BLOCK + TAIL and BLOCKS % 2 == 1 and TILES == BLOCKS * T


def sbuf(nc, name, shape, dt):
    return nc.sbuf_tensor(f"{name}_{nc.next_id()}", shape, dt)


def psum(nc, name, shape, dt):
    return nc.psum_tensor(f"{name}_{nc.next_id()}", shape, dt)


@contextmanager
def phase(nc, names):
    sems = [nc.alloc_semaphore(f"{n}_{nc.next_id()}") for n in names.split()]
    with nc.Block() as block:
        yield (block, *sems)
    nc.clear_and_free_semaphores(sems)
    nc.all_engine_barrier()


class Chain:

    def __init__(self, eng, sem, at, per):
        self.eng, self.sem, self.base, self.per, self.n = eng, sem, at * per, per, 0

    def mark(self, instruction):
        instruction.then_inc(self.sem, 1)
        self.n += 1

    def wait(self):
        self.eng.wait_ge(self.sem, self.base + self.n)

    def then(self, instruction):
        self.mark(instruction)
        self.wait()

    def end(self):
        assert self.n == self.per, (self.n, self.per)


def alone(eng):
    eng.nop(nofuse=True)


def over_blocks(eng, body):
    body(0, 0, 0, T, BLOCK)
    body(1, 1, 0, T, BLOCK)
    with eng.Fori(1, PAIRS) as pair:
        body(2 * pair, 0, pair, T, BLOCK)
        body(2 * pair + 1, 1, pair, T, BLOCK)
    body(BLOCKS - 1, 0, PAIRS, T, BLOCK)
    body(BLOCKS, 1, PAIRS, 1, TAIL)


def over_tiles(eng, body):
    with eng.Fori(0, TILES) as tile:
        body(tile, P)
    body(TILES, TAIL)


def first(b):
    return isinstance(b, int) and b < 2


def halves(columns):
    return [(0, 0, HALF), (1, HALF, HALF)] if columns == BLOCK else [(0, 0, columns)]


def feat_block(feat, b, columns):
    v = feat[:, bass.ds(b * BLOCK, columns)]
    return v.rearrange("p (a c) -> p a c", a=2) if columns == BLOCK else v


def banks(ps, columns):
    return ps[:, :, 0:HALF] if columns == BLOCK else ps[:, 0, 0:columns]


def tile_in_banks(ps, j, rows, width):
    return ps[0:rows, j // 3, (j % 3) * P:(j % 3) * P + width]


def node_block(dram, b, columns):
    rows = dram[bass.ds(b * BLOCK, columns), :]
    return rows.rearrange("(t p) c -> p t c", p=P) if columns == BLOCK else rows


def node_slot(buf, s, columns):
    return buf[:, s, :, :] if columns == BLOCK else buf[0:columns, s, 0, :]


def gnn_kernel(nc, x, src, dst, edge128, edge64, w_src, w_dst, w_edge, vectors, w1, w2, out):
    ctx = ExitStack()
    with ctx:
        keep = lambda name, shape, dt=F32: ctx.enter_context(sbuf(nc, name, shape, dt))
        feat = keep("feat", [P, N])
        ident = keep("ident", [P, P])
        lower = keep("lower", [P, P])
        src_ix = keep("src_ix", [P, TILES + 1], I32)
        dst_ix = keep("dst_ix", [P, TILES + 1], I32)
        dst_f = keep("dst_f", [P, TILES + 1])
        vecs = keep("vecs", [P, vectors.shape[1]])
        scale = keep("scale", [P, 2])
        table = nc.dram_tensor("table", [N, C], F32).ap()
        resid = nc.dram_tensor("resid", [N, C], F32).ap()
        agg0 = nc.dram_tensor("agg0", [AGG_ROWS, AGG], F32).ap()
        agg1 = nc.dram_tensor("agg1", [AGG_ROWS, C], F32).ap()

        GAMMA0, BETA0 = 0, 1
        B1, GM, BM, B2, GO, BO = (lambda l, k=k: 2 + 6 * l + k for k in range(6))

        load_constants(nc, src, dst, vectors, ident, lower, src_ix, dst_ix, dst_f, vecs)
        load_nodes(nc, x, feat, ident)
        scatter_messages(nc, x, edge64, (w_src, w_dst, w_edge), ident, lower, src_ix, dst_ix, dst_f, agg0)
        add_sums(nc, agg0, feat, ident, mean=True)
        norm_stats(nc, feat, vecs, scale, GAMMA0, BETA0)
        layer_norm(nc, feat, scale, ident, x, table, resid)
        for l in range(LAYERS):
            last = l == LAYERS - 1
            scatter_messages(nc, table, edge128, None, ident, lower, src_ix, dst_ix, dst_f, agg1)
            add_sums(nc, agg1, feat, ident, mean=False)
            first_product(nc, w1[l], feat, vecs, scale, B1(l), GM(l), BM(l))
            second_product(nc, w2[l], feat, vecs, scale, B2(l), GO(l), BO(l))
            if not last:
                write_table(nc, feat, scale, ident, table)
        layer_norm(nc, feat, scale, ident, resid, out, None)


def load_constants(nc, src, dst, vectors, ident, lower, src_ix, dst_ix, dst_f, vecs):
    groups = [(g, min(P, TILES - g)) for g in range(0, TILES, P)]
    with ExitStack() as ctx:
        raw = ctx.enter_context(sbuf(nc, "raw", [P, 2, len(groups) + 1, P], I32))
        rawf = ctx.enter_context(sbuf(nc, "rawf", [P, 2, len(groups) + 1, P], F32))
        ps = ctx.enter_context(psum(nc, "ps_ix", [P, 2, BANK], F32))
        with phase(nc, "zeroed ones_done loaded rawf_done turned copied dst_done") as \
                (block, zeroed, ones_done, loaded, rawf_done, turned, copied, dst_done):
            @block.sync
            def _(sp):
                sp.wait_ge(zeroed, 1)
                n = 0
                for k, a in enumerate((src, dst)):
                    for g, (first, tiles) in enumerate(groups):
                        sp.dma_start(raw[0:tiles, k, g, :],
                                     a[first * P:(first + tiles) * P].rearrange("(t p) -> t p", p=P)).then_inc(loaded, 16)
                    sp.dma_start(raw[0:1, k, len(groups), 0:TAIL],
                                 a[TILES * P:N].rearrange("(a p) -> a p", a=1)).then_inc(loaded, 16)
                    n += len(groups) + 1
                sp.dma_start(vecs[:, :], vectors).then_inc(loaded, 16)
                sp.wait_ge(loaded, 16 * (n + 1))

            @block.gpsimd
            def _(pool):
                pool.memset(ident[:, :], 0.0).then_inc(ones_done, 1)
                pool.memset(lower[:, :], 1.0).then_inc(ones_done, 1)
                pool.wait_ge(ones_done, 2)
                pool.affine_select(out=ident[:, :], in_=ident[:, :], compare_op=ALU.not_equal, fill=1.0,
                                   base=0, pattern=[[-1, P]], channel_multiplier=1).then_inc(ones_done, 1)
                pool.affine_select(out=lower[:, :], in_=lower[:, :], compare_op=ALU.is_gt, fill=0.0,
                                   base=0, pattern=[[-1, P]], channel_multiplier=1).then_inc(ones_done, 1)

            @block.vector
            def _(dve):
                dve.memset(raw[:, :, :, :], 0).then_inc(zeroed, 1)
                dve.wait_ge(loaded, 16 * (2 * (len(groups) + 1) + 1))
                dve.tensor_copy(rawf[:, :, :, :], raw[:, :, :, :]).then_inc(rawf_done, 1)
                dve.wait_ge(turned, 1)
                dve.tensor_copy(src_ix[:, :], ps[:, 0, 0:TILES + 1]).then_inc(copied, 1)
                dve.tensor_copy(dst_ix[:, :], ps[:, 1, 0:TILES + 1]).then_inc(copied, 1)
                dve.tensor_copy(dst_f[:, :], ps[:, 1, 0:TILES + 1]).then_inc(copied, 1)

            @block.tensor
            def _(pe):
                pe.wait_ge(rawf_done, 1)
                pe.wait_ge(ones_done, 4)
                for k in range(2):
                    for g, (first, tiles) in enumerate(groups + [(TILES, 1)]):
                        last = pe.transpose(ps[:, k, first:first + tiles], rawf[0:tiles, k, g, :], ident[0:tiles, 0:tiles])
                last.then_inc(turned, 1)


def load_nodes(nc, x, feat, ident):
    with ExitStack() as ctx:
        rows = ctx.enter_context(sbuf(nc, "rows", [P, 2, T, C], F32))
        ps = [ctx.enter_context(psum(nc, f"ps_turn{s}", [P, 2, BANK], F32)) for s in range(2)]
        with phase(nc, "rows0 rows1 rows_free turned turned_free") as (block, rows0, rows1, rows_free, turned, turned_free):
            rows_loaded = (rows0, rows1)

            @block.sync
            def _(sp):
                def load(b, s, use, tiles, columns):
                    sp.wait_ge(rows_free, b + 1)
                    alone(sp)
                    sp.dma_start(node_slot(rows, s, columns), node_block(x, b, columns)).then_inc(rows_loaded[s], 16)
                over_blocks(sp, load)

            @block.tensor
            def _(pe):
                pe.sem_inc(rows_free, 2)

                def turn(b, s, use, tiles, columns):
                    pe.wait_ge(turned_free, b + 1)
                    pe.wait_ge(rows_loaded[s], use * 16 + 16)
                    n = P if columns == BLOCK else columns
                    for j in range(tiles):
                        last = pe.transpose(tile_in_banks(ps[s], j, P, n), rows[0:n, s, j, :], ident[0:n, 0:n])
                    last.then_inc(turned, 1)
                    pe.wait_ge(turned, b + 1)
                    pe.sem_inc(rows_free, 1)
                over_blocks(pe, turn)

            @block.scalar
            def _(act):
                act.sem_inc(turned_free, 2)

                def store(b, s, use, tiles, columns):
                    act.wait_ge(turned, b + 1)
                    alone(act)
                    act.activation(feat_block(feat, b, columns), banks(ps[s], columns), ACT.Copy).then_inc(turned_free, 1)
                over_blocks(act, store)


def zero_rows(nc, agg):
    rows, width = agg.shape
    words = rows * width // 16
    piece = 1
    for k in range(1, 3001):
        if words % k == 0:
            piece = k
    flat = agg.rearrange("r w -> (r w)").rearrange("(a n) -> a n", a=16)
    with ExitStack() as ctx:
        zeros = ctx.enter_context(sbuf(nc, "zeros", [16, piece], F32))
        with phase(nc, "zeros_set zeroed") as (block, zeros_set, zeroed):
            @block.vector
            def _(dve):
                dve.memset(zeros[:, :], 0.0).then_inc(zeros_set, 1)

            @block.sync
            def _(sp):
                sp.wait_ge(zeros_set, 1)
                with sp.Fori(0, words // piece) as k:
                    sp.dma_start(flat[:, bass.ds(k * piece, piece)], zeros[:, :]).then_inc(zeroed, 16)
                sp.wait_ge(zeroed, words // piece * 16)


def scatter_messages(nc, table, edges, gates, ident, lower, src_ix, dst_ix, dst_f, agg):
    zero_rows(nc, agg)
    width = agg.shape[1]
    d = edges.shape[1]
    spare = [N + 0, 1]
    with ExitStack() as ctx:
        sb = lambda name, shape, dt=F32: ctx.enter_context(sbuf(nc, name, shape, dt))
        six, dix, gix = (sb(n, [P, 1], I32) for n in ("six", "dix", "gix"))
        ds_, place, low, to, tof = (sb(n, [P, 1]) for n in ("dst_here", "place", "low", "to", "tof"))
        same, tmp = sb("same", [P, P]), sb("tmp", [P, P])
        xs, ed, msg, total = sb("xs", [P, C]), sb("ed", [P, d]), sb("msg", [P, width]), sb("total", [P, width])
        if gates:
            xd, tT = sb("xd", [P, C]), sb("tT", [P, 3, P])
            weights = sb("gate_w", [P, 3, 2 * C])
            e1, e2 = sb("e1", [P, C]), sb("e2", [P, C])
        ps_d = ctx.enter_context(psum(nc, "ps_dst", [P, BANK], F32))
        ps_m = ctx.enter_context(psum(nc, "ps_total", [P, BANK], F32))
        ps_t = ctx.enter_context(psum(nc, "ps_turned", [P, 3, P], F32))
        ps_z = ctx.enter_context(psum(nc, "ps_z", [P, 2 * C], F32))
        names = "ready wloaded indexed dst_turned edge_loaded gathered added index_made msg_made summed total_made turned turned_copied gated gate_vals vec"
        with phase(nc, names) as (block, ready, wloaded, indexed, dst_turned, edge_loaded, gathered, added, index_made,
                                  msg_made, summed, total_made, turned, turned_copied, gated, gate_vals, vec):
            @block.sync
            def _(sp):
                if gates:
                    sp.dma_start(weights[:, 0, :], gates[0]).then_inc(wloaded, 16)
                    sp.dma_start(weights[:, 1, :], gates[1]).then_inc(wloaded, 16)
                    sp.dma_start(weights[0:D0 + 1, 2, :], gates[2]).then_inc(wloaded, 16)

                def load(t, rows):
                    sp.wait_ge(indexed, t + 1)
                    alone(sp)
                    sp.dma_start(ed[0:rows, :], edges[bass.ds(t * P, rows), :]).then_inc(edge_loaded, 16)
                over_tiles(sp, load)

            @block.gpsimd
            def _(pool):
                pool.iota(gix[:, :], [[0, 1]], base=N, channel_multiplier=1).then_inc(ready, 1)

                def tile(t, rows):
                    pool.wait_ge(indexed, t + 1)
                    alone(pool)
                    pool.indirect_dma_start(xs[0:rows, :], None, table,
                                            bass.IndirectOffsetOnAxis(ap=six[0:rows, 0:1], axis=0)).then_inc(gathered, 16)
                    if gates:
                        pool.indirect_dma_start(xd[0:rows, :], None, table,
                                                bass.IndirectOffsetOnAxis(ap=dix[0:rows, 0:1], axis=0)).then_inc(gathered, 16)
                    pool.wait_ge(total_made, t + 1)
                    alone(pool)
                    pool.indirect_dma_start(agg, bass.IndirectOffsetOnAxis(ap=dix[0:rows, 0:1], axis=0),
                                            total[0:rows, :], None, compute_op=ALU.add).then_inc(added, 16)
                over_tiles(pool, tile)

            @block.tensor
            def _(pe):
                if gates:
                    pe.wait_ge(wloaded, 48)

                def tile(t, rows):
                    pe.wait_ge(indexed, t + 1)
                    pe.transpose(ps_d[0:rows, 0:rows], ds_[0:rows, 0:1].to_broadcast([rows, rows]),
                                 ident[0:rows, 0:rows]).then_inc(dst_turned, 1)
                    if gates:
                        pe.wait_ge(gathered, 32 * t + 32)
                        pe.wait_ge(edge_loaded, 16 * t + 16)
                        pe.transpose(ps_t[:, 0, 0:rows], xs[0:rows, :], ident[0:rows, 0:rows])
                        pe.transpose(ps_t[:, 1, 0:rows], xd[0:rows, :], ident[0:rows, 0:rows])
                        pe.transpose(ps_t[0:D0, 2, 0:rows], ed[0:rows, :], ident[0:rows, 0:rows]).then_inc(turned, 1)
                        pe.wait_ge(turned_copied, t + 1)
                        pe.matmul(ps_z[0:rows, :], tT[:, 0, 0:rows], weights[:, 0, :], start=True, stop=False)
                        pe.matmul(ps_z[0:rows, :], tT[:, 1, 0:rows], weights[:, 1, :], start=False, stop=False)
                        pe.matmul(ps_z[0:rows, :], tT[0:D0 + 1, 2, 0:rows], weights[0:D0 + 1, 2, :],
                                  start=False, stop=True).then_inc(gated, 1)
                    pe.wait_ge(msg_made, t + 1)
                    pe.matmul(ps_m[0:rows, 0:width], same[0:rows, 0:rows], msg[0:rows, :],
                              start=True, stop=True).then_inc(summed, 1)
                over_tiles(pe, tile)

            if gates:
                @block.scalar
                def _(act):
                    def tile(t, rows):
                        act.wait_ge(turned, t + 1)
                        act.activation(tT[:, 0:2, 0:rows], ps_t[:, 0:2, 0:rows], ACT.Copy)
                        act.activation(tT[0:D0, 2, 0:rows], ps_t[0:D0, 2, 0:rows], ACT.Copy).then_inc(turned_copied, 1)
                        act.wait_ge(gated, t + 1)
                        act.activation(e1[0:rows, :], ps_z[0:rows, 0:C], ACT.Exp, scale=-1.0)
                        act.activation(e2[0:rows, :], ps_z[0:rows, C:2 * C], ACT.Abs).then_inc(gate_vals, 1)
                        act.wait_ge(gate_vals, 3 * t + 1)
                        act.activation(e2[0:rows, :], e2[0:rows, :], ACT.Exp, scale=-1.0).then_inc(gate_vals, 1)
                        act.wait_ge(gate_vals, 3 * t + 2)
                        act.activation(e2[0:rows, :], e2[0:rows, :], ACT.Ln, bias=1.0).then_inc(gate_vals, 1)
                    over_tiles(act, tile)

            @block.vector
            def _(dve):
                dve.wait_ge(ready, 1)
                dve.tensor_copy(place[:, :], gix[:, :]).then_inc(ready, 1)
                dve.wait_ge(ready, 2)
                if gates:
                    dve.memset(tT[D0:D0 + 1, 2, :], 1.0)
                    dve.memset(msg[:, C:AGG], 1.0).then_inc(ready, 1)
                    dve.wait_ge(ready, 3)

                def tile(t, rows):
                    ch = Chain(dve, vec, t, 7 if gates else 6)
                    r = slice(0, rows)
                    dve.tensor_copy(six[r, :], src_ix[r, bass.ds(t, 1)])
                    dve.tensor_copy(dix[r, :], dst_ix[r, bass.ds(t, 1)])
                    dve.tensor_copy(ds_[r, :], dst_f[r, bass.ds(t, 1)]).then_inc(indexed, 1)
                    dve.wait_ge(dst_turned, t + 1)
                    dve.wait_ge(indexed, t + 1)
                    ch.then(dve.tensor_scalar(same[r, r], ps_d[r, r], ds_[r, 0:1], None, ALU.is_equal))
                    ch.then(dve.tensor_tensor_reduce(out=tmp[r, r], in0=same[r, r], in1=lower[r, r], scale=1.0, scalar=0.0,
                                                     op0=ALU.mult, op1=ALU.add, accum_out=low[r, :]))
                    ch.then(dve.tensor_tensor(to[r, :], place[r, :], ds_[r, :], ALU.subtract))
                    ch.then(dve.scalar_tensor_tensor(out=tof[r, :], in0=low[r, :], scalar=0.0, in1=to[r, :],
                                                     op0=ALU.is_gt, op1=ALU.mult))
                    if gates:
                        dve.wait_ge(gate_vals, 3 * t + 3)
                        ch.then(dve.scalar_tensor_tensor(out=e2[r, :], in0=ps_z[r, C:2 * C], scalar=0.0, in1=e2[r, :],
                                                         op0=ALU.max, op1=ALU.add))
                        ch.then(dve.tensor_scalar(e1[r, :], e1[r, :], 1.0, None, ALU.add))
                        ch.then(dve.reciprocal(e1[r, :], e1[r, :]))
                        dve.tensor_tensor(msg[r, 0:C], e2[r, :], e1[r, :], ALU.mult).then_inc(msg_made, 1)
                    else:
                        dve.wait_ge(gathered, 16 * t + 16)
                        dve.wait_ge(edge_loaded, 16 * t + 16)
                        ch.then(dve.tensor_tensor(tmp[r, 0:C], xs[r, :], ed[r, :], ALU.add))
                        ch.mark(dve.tensor_scalar(msg[r, :], tmp[r, 0:C], 0.0, None, ALU.max))
                        ch.wait()
                        dve.sem_inc(msg_made, 1)
                    dve.wait_ge(summed, t + 1)
                    dve.tensor_copy(total[r, :], ps_m[r, 0:width])
                    dve.tensor_tensor(dix[r, :], tof[r, :], ds_[r, :], ALU.add).then_inc(total_made, 1)
                    dve.wait_ge(added, 16 * t + 16)
                    ch.end()
                over_tiles(dve, tile)


def add_sums(nc, agg, feat, ident, mean):
    width = agg.shape[1]
    with ExitStack() as ctx:
        sb = lambda name, shape, dt=F32: ctx.enter_context(sbuf(nc, name, shape, dt))
        rows_ = sb("sum_rows", [P, width])
        cnt, rec = sb("cnt", [P, 1]), sb("rec", [P, 1])
        ps = ctx.enter_context(psum(nc, "ps_sums", [P, P], F32))
        with phase(nc, "loaded scaled turned added vec") as (block, loaded, scaled, turned, added, vec):
            @block.sync
            def _(sp):
                sp.sem_inc(added, 1)

                def load(t, rows):
                    sp.wait_ge(added, t + 1)
                    alone(sp)
                    sp.dma_start(rows_[0:rows, :], agg[bass.ds(t * P, rows), :]).then_inc(loaded, 16)
                over_tiles(sp, load)

            @block.tensor
            def _(pe):
                def tile(t, rows):
                    pe.wait_ge(scaled, t + 1)
                    pe.transpose(ps[:, 0:rows], rows_[0:rows, 0:C], ident[0:rows, 0:rows]).then_inc(turned, 1)
                over_tiles(pe, tile)

            @block.vector
            def _(dve):
                def tile(t, rows):
                    r = slice(0, rows)
                    dve.wait_ge(loaded, 16 * t + 16)
                    if mean:
                        ch = Chain(dve, vec, t, 3)
                        ch.then(dve.tensor_scalar(cnt[r, :], rows_[r, C:C + 1], 1.0, None, ALU.max))
                        ch.then(dve.reciprocal(rec[r, :], cnt[r, :]))
                        ch.then(dve.tensor_scalar(rows_[r, 0:C], rows_[r, 0:C], rec[r, 0:1], None, ALU.mult))
                        ch.end()
                    dve.sem_inc(scaled, 1)
                    dve.wait_ge(turned, t + 1)
                    here = feat[:, bass.ds(t * P, rows)]
                    dve.tensor_tensor(here, here, ps[:, 0:rows], ALU.add).then_inc(added, 1)
                over_tiles(dve, tile)


def batch_scale(dve, act_sem, var_sem, chain, stats, mv, scale, vecs, gamma, beta, bias=None):
    chain.then(dve.bn_aggr(mv[:, 0:2], stats[:, :, :].rearrange("p a b -> p (a b)")))
    dve.tensor_scalar(mv[:, 1:2], mv[:, 1:2], EPS, None, ALU.add).then_inc(var_sem, 1)
    dve.wait_ge(act_sem, 1)
    chain.then(dve.reciprocal(mv[:, 3:4], mv[:, 2:3]))
    chain.then(dve.tensor_tensor(scale[:, 0:1], mv[:, 3:4], vecs[:, gamma:gamma + 1], ALU.mult))
    if bias is not None:
        chain.then(dve.tensor_tensor(mv[:, 0:1], mv[:, 0:1], vecs[:, bias:bias + 1], ALU.add))
    chain.then(dve.tensor_tensor(mv[:, 3:4], mv[:, 0:1], scale[:, 0:1], ALU.mult))
    dve.tensor_tensor(scale[:, 1:2], vecs[:, beta:beta + 1], mv[:, 3:4], ALU.subtract)


def root_of(act, act_sem, var_sem, mv):
    act.wait_ge(var_sem, 1)
    act.activation(mv[:, 2:3], mv[:, 1:2], ACT.Sqrt).then_inc(act_sem, 1)


def norm_stats(nc, feat, vecs, scale, gamma, beta):
    with ExitStack() as ctx:
        stats = ctx.enter_context(sbuf(nc, "stats", [P, CHUNKS, 6], F32))
        mv = ctx.enter_context(sbuf(nc, "mv", [P, 4], F32))
        with phase(nc, "taken root var vec") as (block, taken, root, var, vec):
            @block.vector
            def _(dve):
                def take(b, s, use, tiles, columns):
                    for c, at, w in halves(columns):
                        dve.bn_stats(stats[:, bass.ds(2 * b + c, 1), :].rearrange("p a b -> p (a b)"),
                                     feat[:, bass.ds(b * BLOCK + at, w)]).then_inc(taken, 1)
                over_blocks(dve, take)
                dve.wait_ge(taken, CHUNKS)
                batch_scale(dve, root, var, Chain(dve, vec, 0, 4), stats, mv, scale, vecs, gamma, beta)

            @block.scalar
            def _(act):
                root_of(act, root, var, mv)


def first_product(nc, w, feat, vecs, scale, bias, gamma, beta):
    with ExitStack() as ctx:
        stats = ctx.enter_context(sbuf(nc, "stats", [P, CHUNKS, 6], F32))
        mv = ctx.enter_context(sbuf(nc, "mv", [P, 4], F32))
        w_sb = ctx.enter_context(sbuf(nc, "w_sb", [P, C], F32))
        ps = [ctx.enter_context(psum(nc, f"ps_h{s}", [P, 2, BANK], F32)) for s in range(2)]
        with phase(nc, "w_loaded product taken stored root var vec") as (block, w_loaded, product, taken, stored, root, var, vec):
            @block.sync
            def _(sp):
                sp.dma_start(w_sb[:, :], w).then_inc(w_loaded, 16)

            @block.tensor
            def _(pe):
                pe.wait_ge(w_loaded, 16)

                def multiply(b, s, use, tiles, columns):
                    pe.wait_ge(stored, b + 1)
                    for c, at, n in halves(columns):
                        last = pe.matmul(ps[s][:, c, 0:n], w_sb[:, :], feat[:, bass.ds(b * BLOCK + at, n)], start=True, stop=True)
                    last.then_inc(product, 1)
                over_blocks(pe, multiply)

            @block.scalar
            def _(act):
                act.sem_inc(stored, 2)

                def store(b, s, use, tiles, columns):
                    act.wait_ge(product, b + 1)
                    alone(act)
                    act.activation(feat_block(feat, b, columns), banks(ps[s], columns), ACT.Identity,
                                   bias=vecs[:, bias:bias + 1]).then_inc(stored, 1)
                over_blocks(act, store)
                root_of(act, root, var, mv)

            @block.vector
            def _(dve):
                def take(b, s, use, tiles, columns):
                    dve.wait_ge(stored, b + 3)
                    alone(dve)
                    for c, at, n in halves(columns):
                        last = dve.bn_stats(stats[:, bass.ds(2 * b + c, 1), :].rearrange("p a b -> p (a b)"),
                                            feat[:, bass.ds(b * BLOCK + at, n)])
                    last.then_inc(taken, 1)
                over_blocks(dve, take)
                dve.wait_ge(taken, BLOCKS + 1)
                batch_scale(dve, root, var, Chain(dve, vec, 0, 4), stats, mv, scale, vecs, gamma, beta)


def second_product(nc, w, feat, vecs, scale, bias, gamma, beta):
    with ExitStack() as ctx:
        stats = ctx.enter_context(sbuf(nc, "stats", [P, CHUNKS, 6], F32))
        mv = ctx.enter_context(sbuf(nc, "mv", [P, 4], F32))
        w_sb = ctx.enter_context(sbuf(nc, "w_sb", [P, C], F32))
        hidden = ctx.enter_context(sbuf(nc, "hidden", [P, 2, BLOCK], F32))
        ps = [ctx.enter_context(psum(nc, f"ps_h{s}", [P, 2, BANK], F32)) for s in range(2)]
        with phase(nc, "w_loaded made product used root var vec") as (block, w_loaded, made, product, used, root, var, vec):
            @block.sync
            def _(sp):
                sp.dma_start(w_sb[:, :], w).then_inc(w_loaded, 16)

            @block.scalar
            def _(act):
                def make(b, s, use, tiles, columns):
                    act.wait_ge(product, b + 1)
                    alone(act)
                    act.activation(hidden[:, s, 0:columns], feat[:, bass.ds(b * BLOCK, columns)], ACT.Relu,
                                   bias=scale[:, 1:2], scale=scale[:, 0:1]).then_inc(made, 1)
                over_blocks(act, make)
                root_of(act, root, var, mv)

            @block.tensor
            def _(pe):
                pe.wait_ge(w_loaded, 16)
                pe.sem_inc(product, 2)

                def multiply(b, s, use, tiles, columns):
                    pe.wait_ge(used, b + 1)
                    pe.wait_ge(made, b + 1)
                    for c, at, n in halves(columns):
                        last = pe.matmul(ps[s][:, c, 0:n], w_sb[:, :], hidden[:, s, at:at + n], start=True, stop=True)
                    last.then_inc(product, 1)
                over_blocks(pe, multiply)

            @block.vector
            def _(dve):
                dve.sem_inc(used, 2)

                def take(b, s, use, tiles, columns):
                    dve.wait_ge(product, b + 3)
                    alone(dve)
                    for c, at, n in halves(columns):
                        dve.bn_stats(stats[:, bass.ds(2 * b + c, 1), :].rearrange("p a b -> p (a b)"), ps[s][:, c, 0:n])
                    dve.tensor_scalar(feat_block(feat, b, columns), banks(ps[s], columns), vecs[:, bias:bias + 1], None,
                                      ALU.add).then_inc(used, 1)
                over_blocks(dve, take)
                dve.wait_ge(used, 2 + BLOCKS + 1)
                batch_scale(dve, root, var, Chain(dve, vec, 0, 5), stats, mv, scale, vecs, gamma, beta, bias)


def write_table(nc, feat, scale, ident, table):
    with ExitStack() as ctx:
        new = ctx.enter_context(sbuf(nc, "new", [P, 2, BLOCK], F32))
        rows = ctx.enter_context(sbuf(nc, "rows", [P, 2, T, C], F32))
        ps = [ctx.enter_context(psum(nc, f"ps_turn{s}", [P, 2, BANK], F32)) for s in range(2)]
        with phase(nc, "made kept turned rows_made written0 written1") as \
                (block, made, kept, turned, rows_made, written0, written1):
            written = (written0, written1)

            @block.scalar
            def _(act):
                def make(b, s, use, tiles, columns):
                    act.wait_ge(turned, b + 1)
                    act.wait_ge(kept, b + 1)
                    alone(act)
                    act.activation(new[:, s, 0:columns], feat[:, bass.ds(b * BLOCK, columns)], ACT.Relu,
                                   bias=scale[:, 1:2], scale=scale[:, 0:1]).then_inc(made, 1)
                over_blocks(act, make)

            @block.gpsimd
            def _(pool):
                pool.sem_inc(kept, 2)

                def copy(b, s, use, tiles, columns):
                    pool.wait_ge(made, b + 1)
                    alone(pool)
                    pool.tensor_copy(feat[:, bass.ds(b * BLOCK, columns)], new[:, s, 0:columns]).then_inc(kept, 1)
                over_blocks(pool, copy)

            @block.tensor
            def _(pe):
                pe.sem_inc(turned, 2)

                def turn(b, s, use, tiles, columns):
                    pe.wait_ge(rows_made, b + 1)
                    pe.wait_ge(made, b + 1)
                    n = P if columns == BLOCK else columns
                    for j in range(tiles):
                        last = pe.transpose(tile_in_banks(ps[s], j, n, P), new[:, s, j * P:j * P + n], ident[:, :])
                    last.then_inc(turned, 1)
                over_blocks(pe, turn)

            @block.vector
            def _(dve):
                dve.sem_inc(rows_made, 2)

                def store(b, s, use, tiles, columns):
                    dve.wait_ge(turned, b + 3)
                    if not first(b):
                        dve.wait_ge(written[s], use * 16)
                    rows_of(dve.tensor_copy, rows, s, ps[s], columns).then_inc(rows_made, 1)
                over_blocks(dve, store)

            @block.sync
            def _(sp):
                def write(b, s, use, tiles, columns):
                    sp.wait_ge(rows_made, b + 3)
                    alone(sp)
                    sp.dma_start(node_block(table, b, columns), node_slot(rows, s, columns)).then_inc(written[s], 16)
                over_blocks(sp, write)
                for s in range(2):
                    sp.wait_ge(written[s], 16 * (PAIRS + 1))


def rows_of(copy, rows, s, ps, columns):
    if columns == BLOCK:
        return copy(rows[:, s, :, :].rearrange("p (a j) c -> p a (j c)", a=2), ps[:, :, 0:HALF])
    return copy(rows[0:columns, s, 0, :], ps[0:columns, 0, 0:C])


def layer_norm(nc, feat, scale, ident, skip, out, also):
    with ExitStack() as ctx:
        sb = lambda name, shape, dt=F32: ctx.enter_context(sbuf(nc, name, shape, dt))
        normed = sb("normed", [P, 2, BLOCK])
        rows = sb("rows", [P, 2, T, C])
        stats = sb("row_stats", [P, T, 6])
        mv = sb("row_mv", [P, T, 2])
        root, rec = sb("row_root", [P, T]), sb("row_rec", [P, T])
        ps = [ctx.enter_context(psum(nc, f"ps_turn{s}", [P, 2, BANK], F32)) for s in range(2)]
        back = [ctx.enter_context(psum(nc, f"ps_back{s}", [P, 2, BANK], F32)) for s in range(2)]
        stores = 2 if also is not None else 1
        with phase(nc, "made turned loaded0 loaded1 summed var_made root_made rows_made turned_back feat_stored written0 written1 vec") as \
                (block, made, turned, loaded0, loaded1, summed, var_made, root_made, rows_made, turned_back,
                 feat_stored, written0, written1, vec):
            loaded, written = (loaded0, loaded1), (written0, written1)

            @block.sync
            def _(sp):
                def load(b, s, use, tiles, columns):
                    if not first(b):
                        sp.wait_ge(written[s], use * 16 * stores)
                        alone(sp)
                    if also is not None:
                        sp.wait_ge(turned_back, b + 1)
                        alone(sp)
                    sp.dma_start(node_slot(rows, s, columns), node_block(skip, b, columns)).then_inc(loaded[s], 16)
                over_blocks(sp, load)

            @block.scalar
            def _(act):
                act.sem_inc(feat_stored, 2)

                def make(b, s, use, tiles, columns):
                    act.wait_ge(turned, b + 1)
                    alone(act)
                    act.activation(normed[:, s, 0:columns], feat[:, bass.ds(b * BLOCK, columns)], ACT.Identity,
                                   bias=scale[:, 1:2], scale=scale[:, 0:1]).then_inc(made, 1)
                    act.wait_ge(var_made, b + 1)
                    act.activation(root[:, 0:tiles], mv[:, 0:tiles, 1], ACT.Sqrt).then_inc(root_made, 1)
                    if also is not None:
                        act.wait_ge(turned_back, b + 3)
                        alone(act)
                        act.activation(feat_block(feat, b, columns), banks(back[s], columns), ACT.Copy).then_inc(feat_stored, 1)
                over_blocks(act, make)

            @block.tensor
            def _(pe):
                pe.sem_inc(turned, 2)
                pe.sem_inc(turned_back, 2)

                def turn(b, s, use, tiles, columns):
                    pe.wait_ge(summed, b + 1)
                    pe.wait_ge(made, b + 1)
                    n = P if columns == BLOCK else columns
                    for j in range(tiles):
                        last = pe.transpose(tile_in_banks(ps[s], j, n, P), normed[:, s, j * P:j * P + n], ident[:, :])
                    last.then_inc(turned, 1)
                    if also is not None:
                        pe.wait_ge(feat_stored, b + 1)
                        pe.wait_ge(rows_made, b + 1)
                        for j in range(tiles):
                            last = pe.transpose(tile_in_banks(back[s], j, P, n), rows[0:n, s, j, :], ident[0:n, 0:n])
                        last.then_inc(turned_back, 1)
                over_blocks(pe, turn)

            @block.vector
            def _(dve):
                dve.sem_inc(summed, 2)

                def norm(b, s, use, tiles, columns):
                    n = P if columns == BLOCK else columns
                    ch = Chain(dve, vec, b, 4)
                    dve.wait_ge(loaded[s], use * 16 + 16)
                    dve.wait_ge(turned, b + 3)
                    add = lambda o, i: dve.tensor_tensor(o, o, i, ALU.add)
                    rows_of(add, rows, s, ps[s], columns).then_inc(summed, 1)
                    dve.wait_ge(summed, b + 3)
                    for j in range(tiles):
                        last = dve.bn_stats(stats[0:n, j, :], rows[0:n, s, j, :])
                    ch.then(last)
                    alone(dve)
                    for j in range(tiles):
                        last = dve.bn_aggr(mv[0:n, j, :], stats[0:n, j, :])
                    ch.then(last)
                    dve.tensor_scalar(mv[0:n, 0:tiles, 1], mv[0:n, 0:tiles, 1], EPS, None, ALU.add).then_inc(var_made, 1)
                    dve.wait_ge(root_made, b + 1)
                    ch.then(dve.reciprocal(rec[0:n, 0:tiles], root[0:n, 0:tiles]))
                    for j in range(tiles):
                        last = dve.tensor_scalar(rows[0:n, s, j, :], rows[0:n, s, j, :], mv[0:n, j, 0:1], rec[0:n, j:j + 1],
                                                 ALU.subtract, ALU.mult)
                    ch.then(last)
                    dve.sem_inc(rows_made, 1)
                    ch.end()
                over_blocks(dve, norm)

            @block.gpsimd
            def _(pool):
                def write(b, s, use, tiles, columns):
                    pool.wait_ge(rows_made, b + 1)
                    alone(pool)
                    pool.dma_start(node_block(out, b, columns), node_slot(rows, s, columns)).then_inc(written[s], 16)
                    if also is not None:
                        pool.dma_start(node_block(also, b, columns), node_slot(rows, s, columns)).then_inc(written[s], 16)
                over_blocks(pool, write)
                for s in range(2):
                    pool.wait_ge(written[s], 16 * stores * (PAIRS + 1))


def kernel(**inputs):
    import numpy as _np
    import concourse.bacc as _bacc
    from concourse import mybir as _mybir
    from concourse.bass_utils import run_bass_kernel_spmd as _run

    get = lambda name: _np.asarray(inputs[name])
    both = _np.concatenate([get("L0_gnn_W_f"), get("L0_gnn_W_s")], axis=0).T
    biases = _np.concatenate([get("L0_gnn_b_f"), get("L0_gnn_b_s")])[None, :]
    vectors = [get("L0_gnn_gamma"), get("L0_gnn_beta")]
    for l in range(LAYERS):
        vectors += [get(f"L1_gnn_{n}")[l] for n in ("b1", "g_mlp", "be_mlp", "b2", "g_out", "be_out")]
    arrays = {
        "x": get("x"), "src": get("src"), "dst": get("dst"),
        "edge128": get("edge_attr_128"), "edge64": get("edge_attr_64"),
        "w_src": both[C:2 * C], "w_dst": both[0:C], "w_edge": _np.concatenate([both[2 * C:], biases], axis=0),
        "vectors": _np.stack(vectors, axis=1), "w1": get("L1_gnn_W1"), "w2": get("L1_gnn_W2"),
    }
    arrays = {f"in_{k}": _np.ascontiguousarray(v) for k, v in arrays.items()}
    nc = _bacc.Bacc("TRN2", target_bir_lowering=False, num_devices=1, dynamic_dma_scratch_size=8192)
    args = [nc.dram_tensor(k, v.shape, _mybir.dt.from_np(v.dtype), kind="ExternalInput").ap() for k, v in arrays.items()]
    out = nc.dram_tensor("out", [N, C], F32, kind="ExternalOutput").ap()
    gnn_kernel(nc, *args, out)
    r = _run(nc, [arrays], core_ids=[0])
    return r.results[0]["out"]
```

```python
import concourse.bass as bass
from concourse import mybir
from contextlib import ExitStack, contextmanager

F32 = mybir.dt.float32
I32 = mybir.dt.int32
I16 = mybir.dt.int16
ALU = mybir.AluOpType
ACT = mybir.ActivationFunctionType

P = 128
N = 50000
E = 50000
C = 128
D0 = 64
LAYERS = 3
EPS = 1e-5
T = 6
BLOCK = T * P
HALF = BLOCK // 2
BLOCKS = N // BLOCK
PAIRS = BLOCKS // 2
TILES = N // P
TAIL = N - TILES * P
CHUNKS = 2 * BLOCKS + 1
BANK = 512
AGG = C + 4
AGG_ROWS = N + P

WINDOWS = [(0, 192), (64, 288), (160, 352), (256, 384), (384, 416), (480, 448)]
SPAN = 928
WIDEST = max(w for _, w in WINDOWS)
NODES = N + 336
LN_EXP_TABLE = 6
LAG = 3

assert all(first + width <= SPAN <= 2 * BANK for first, width in WINDOWS)
assert N == E and N == BLOCKS * BLOCK + TAIL and BLOCKS % 2 == 1 and TILES == BLOCKS * T


def sbuf(nc, name, shape, dt):
    return nc.sbuf_tensor(f"{name}_{nc.next_id()}", shape, dt)


def psum(nc, name, shape, dt):
    return nc.psum_tensor(f"{name}_{nc.next_id()}", shape, dt)


class Taken:

    def __init__(self, block, flag, want):
        self.block, self.flag, self.want = block, flag, want

    def _under(self, place):
        def wrap(program):
            def guarded(eng):
                with eng.If(eng.value_load(self.flag[0:1, 0:1], min_val=0, max_val=1) == self.want):
                    program(eng)
            place(guarded)
            return program
        return wrap

    sync = property(lambda self: self._under(self.block.sync))
    gpsimd = property(lambda self: self._under(self.block.gpsimd))
    scalar = property(lambda self: self._under(self.block.scalar))
    vector = property(lambda self: self._under(self.block.vector))
    tensor = property(lambda self: self._under(self.block.tensor))


@contextmanager
def phase(nc, names, when=None):
    sems = [nc.alloc_semaphore(f"{n}_{nc.next_id()}") for n in names.split()]
    with nc.Block() as block:
        yield (Taken(block, *when) if when else block, *sems)
    nc.clear_and_free_semaphores(sems)
    nc.all_engine_barrier()


class Chain:

    def __init__(self, eng, sem, at, per):
        self.eng, self.sem, self.base, self.per, self.n = eng, sem, at * per, per, 0

    def mark(self, instruction):
        instruction.then_inc(self.sem, 1)
        self.n += 1

    def wait(self):
        self.eng.wait_ge(self.sem, self.base + self.n)

    def then(self, instruction):
        self.mark(instruction)
        self.wait()

    def end(self):
        assert self.n == self.per, (self.n, self.per)


def alone(eng):
    eng.nop(nofuse=True)


def over_blocks(eng, body, ahead=1):
    for pair in range(ahead):
        body(2 * pair, 0, pair, T, BLOCK)
        body(2 * pair + 1, 1, pair, T, BLOCK)
    with eng.Fori(ahead, PAIRS) as pair:
        body(2 * pair, 0, pair, T, BLOCK)
        body(2 * pair + 1, 1, pair, T, BLOCK)
    body(BLOCKS - 1, 0, PAIRS, T, BLOCK)
    body(BLOCKS, 1, PAIRS, 1, TAIL)


def over_tiles(eng, body):
    with eng.Fori(0, TILES) as tile:
        body(tile, P)
    body(TILES, TAIL)


def first(b):
    return isinstance(b, int) and b < 2


def halves(columns):
    return [(0, 0, HALF), (1, HALF, HALF)] if columns == BLOCK else [(0, 0, columns)]


def feat_block(feat, b, columns):
    v = feat[:, bass.ds(b * BLOCK, columns)]
    return v.rearrange("p (a c) -> p a c", a=2) if columns == BLOCK else v


def banks(ps, columns):
    return ps[:, :, 0:HALF] if columns == BLOCK else ps[:, 0, 0:columns]


def tile_in_banks(ps, j, rows, width):
    return ps[0:rows, j // 3, (j % 3) * P:(j % 3) * P + width]


def node_block(dram, b, columns):
    rows = dram[bass.ds(b * BLOCK, columns), :]
    return rows.rearrange("(t p) c -> p t c", p=P) if columns == BLOCK else rows


def node_slot(buf, s, columns):
    return buf[:, s, :, :] if columns == BLOCK else buf[0:columns, s, 0, :]


def gnn_kernel(nc, x, x_t, src, dst, edge128, edge64, edge64_t, w_src, w_dst, w_edge, vectors, w1, w2, out):
    ctx = ExitStack()
    with ctx:
        keep = lambda name, shape, dt=F32: ctx.enter_context(sbuf(nc, name, shape, dt))
        ident = keep("ident", [P, P])
        src_ix = keep("src_ix", [P, TILES + 1], I32)
        dst_ix = keep("dst_ix", [P, TILES + 1], I32)
        place = keep("place", [P, TILES + 1], I16)
        base = keep("base", [1, BLOCKS + 1], I32)
        flag = keep("flag", [1, 1], I32)
        vecs = keep("vecs", [P, vectors.shape[1]])
        scale = keep("scale", [P, 2])
        table = nc.dram_tensor("table", [N, C], F32).ap()
        resid = nc.dram_tensor("resid", [N, C], F32).ap()
        agg0 = nc.dram_tensor("agg0", [AGG_ROWS, AGG], F32).ap()
        spans = nc.dram_tensor("spans", [BLOCKS + 1, P, SPAN], F32).ap()
        agg1 = nc.dram_tensor("agg1", [AGG_ROWS, C], F32).ap()

        GAMMA0, BETA0 = 0, 1
        B1, GM, BM, B2, GO, BO = (lambda l, k=k: 2 + 6 * l + k for k in range(6))

        load_constants(nc, src, dst, vectors, ident, src_ix, dst_ix, vecs, place, base, flag)
        gates = (w_src, w_dst, w_edge)
        gated_messages(nc, x, dst, edge64_t, gates, ident, src_ix, dst_ix, place, spans, (flag, 1))
        scatter_messages(nc, x, edge64, gates, ident, src_ix, dst_ix, agg0, (flag, 0))
        feat = keep("feat", [P, NODES])
        assemble(nc, x_t, spans, base, feat, vecs, scale, GAMMA0, BETA0, (flag, 1))
        load_nodes(nc, x_t, feat, (flag, 0))
        add_sums(nc, agg0, feat, ident, True, (flag, 0))
        norm_stats(nc, feat, vecs, scale, GAMMA0, BETA0, (flag, 0))
        layer_norm(nc, feat, scale, ident, x, table, resid)
        for l in range(LAYERS):
            last = l == LAYERS - 1
            sorted_messages(nc, table, edge128, src_ix, place, base, w1[l], feat, vecs, scale,
                            B1(l), GM(l), BM(l), (flag, 1))
            scatter_messages(nc, table, edge128, None, ident, src_ix, dst_ix, agg1, (flag, 0))
            add_sums(nc, agg1, feat, ident, False, (flag, 0))
            first_product(nc, w1[l], feat, vecs, scale, B1(l), GM(l), BM(l), (flag, 0))
            second_product(nc, w2[l], feat, vecs, scale, B2(l), GO(l), BO(l))
            if not last:
                write_table(nc, feat, scale, ident, table)
        layer_norm(nc, feat, scale, ident, resid, out, None)


def load_constants(nc, src, dst, vectors, ident, src_ix, dst_ix, vecs, place, base, flag):
    groups = [(g, min(P, TILES - g)) for g in range(0, TILES, P)]
    G = len(groups) + 1
    NB = BLOCKS + 1
    with ExitStack() as ctx:
        sb = lambda name, shape, dt=F32: ctx.enter_context(sbuf(nc, name, shape, dt))
        raw, rawf = sb("raw", [P, 3, G, P], I32), sb("rawf", [P, 3, G, P])
        dst_f, bad_t, bad = sb("dst_f", [P, TILES + 1]), sb("bad_t", [P, 6 * P]), sb("bad", [P, 16])
        place_f = sb("place_f", [P, TILES + 1])
        ones, row, spans = sb("ones", [P, P]), sb("row", [1, 2 * NB]), sb("spans", [P, NB])
        base_f = sb("base_f", [1, NB])
        block_ix = sb("block_ix", [1, NB], I32)
        ps = ctx.enter_context(psum(nc, "ps_ix", [P, 2, BANK], F32))
        ps_b = ctx.enter_context(psum(nc, "ps_base", [P, BANK], F32))
        ps_f = ctx.enter_context(psum(nc, "ps_bad", [P, BANK], F32))
        with phase(nc, "zeroed ones_done loaded rawf_done turned copied bases_out bads bads_summed vec") as \
                (block, zeroed, ones_done, loaded, rawf_done, turned, copied, bases_out, bads, bads_summed, vec):
            loads = 3 * G + 1

            @block.sync
            def _(sp):
                sp.wait_ge(zeroed, 1)
                for k, (a, off) in enumerate(((src, 0), (dst, 0), (dst, 1))):
                    for g, (first_tile, tiles) in enumerate(groups):
                        at = first_tile * P + off
                        sp.dma_start(raw[0:tiles, k, g, :],
                                     a[at:at + tiles * P].rearrange("(t p) -> t p", p=P)).then_inc(loaded, 16)
                    sp.dma_start(raw[0:1, k, G - 1, 0:TAIL - off],
                                 a[TILES * P + off:N].rearrange("(a p) -> a p", a=1)).then_inc(loaded, 16)
                sp.dma_start(vecs[:, :], vectors).then_inc(loaded, 16)
                sp.wait_ge(loaded, 16 * loads)

            @block.gpsimd
            def _(pool):
                pool.memset(ident[:, :], 0.0).then_inc(ones_done, 1)
                pool.memset(ones[:, :], 1.0).then_inc(ones_done, 1)
                pool.iota(block_ix[:, :], [[BLOCK, NB]], base=0, channel_multiplier=0).then_inc(ones_done, 1)
                pool.wait_ge(ones_done, 3)
                pool.affine_select(out=ident[:, :], in_=ident[:, :], compare_op=ALU.not_equal, fill=1.0,
                                   base=0, pattern=[[-1, P]], channel_multiplier=1).then_inc(ones_done, 1)

            @block.vector
            def _(dve):
                dve.memset(bad[:, :], 0.0)
                dve.memset(raw[:, :, :, :], 0).then_inc(zeroed, 1)
                ch = Chain(dve, vec, 0, 32)
                dve.wait_ge(loaded, 16 * loads)
                dve.wait_ge(zeroed, 1)
                dve.tensor_copy(rawf[:, :, :, :], raw[:, :, :, :]).then_inc(rawf_done, 1)
                dve.wait_ge(rawf_done, 1)
                for g in range(G):
                    tiles, n = (groups[g][1], P) if g < G - 1 else (1, TAIL - 1)
                    ch.then(dve.tensor_tensor(bad_t[0:tiles, 0:n], rawf[0:tiles, 1, g, 0:n], rawf[0:tiles, 2, g, 0:n], ALU.is_gt))
                    ch.then(dve.reduce_sum(bad[0:tiles, g:g + 1], bad_t[0:tiles, 0:n], axis=mybir.AxisListType.X))
                dve.wait_ge(turned, 1)
                dve.tensor_copy(src_ix[:, :], ps[:, 0, 0:TILES + 1])
                dve.tensor_copy(dst_ix[:, :], ps[:, 1, 0:TILES + 1])
                dve.tensor_copy(dst_f[:, :], ps[:, 1, 0:TILES + 1]).then_inc(copied, 1)
                dve.wait_ge(copied, 1)
                ch.then(dve.tensor_tensor(bad_t[:, 0:TILES - 1], dst_f[:, 1:TILES], dst_f[:, 0:TILES - 1], ALU.is_le))
                ch.then(dve.reduce_sum(bad[:, 4:5], bad_t[:, 0:TILES - 1], axis=mybir.AxisListType.X))
                ch.then(dve.tensor_tensor(bad[0:TAIL, 5:6], dst_f[0:TAIL, TILES:TILES + 1], dst_f[0:TAIL, TILES - 1:TILES], ALU.is_le))
                dve.wait_ge(bases_out, 1)
                ch.then(dve.tensor_copy(spans[:, :], ps_b[:, 0:NB]))
                dve.tensor_copy(base[:, :], spans[0:1, :])
                ch.then(dve.tensor_copy(base_f[:, :], spans[0:1, :]))
                for j, (at, width) in enumerate(WINDOWS):
                    nb = NB if j == 0 else NB - 1
                    here = place_f[:, j:TILES + 1:T]
                    ch.then(dve.scalar_tensor_tensor(out=here, in0=dst_f[:, j:TILES + 1:T], scalar=float(-at), in1=spans[:, 0:nb],
                                                     op0=ALU.add, op1=ALU.subtract))
                dve.tensor_copy(place[:, :], place_f[:, :])
                ch.then(dve.tensor_scalar(bad_t[:, 0:TILES], place_f[:, 0:TILES], 0.0, None, ALU.is_lt))
                ch.then(dve.reduce_sum(bad[:, 6:7], bad_t[:, 0:TILES], axis=mybir.AxisListType.X))
                ch.then(dve.tensor_scalar(bad[0:TAIL, 7:8], place_f[0:TAIL, TILES:TILES + 1], 0.0, None, ALU.is_lt))
                for j, (at, width) in enumerate(WINDOWS):
                    dve.tensor_scalar(bad_t[:, j * P:j * P + BLOCKS], place_f[:, j:TILES:T], float(width), None, ALU.is_ge)
                ch.then(dve.tensor_scalar(bad[0:TAIL, 8:9], place_f[0:TAIL, TILES:TILES + 1], float(WINDOWS[0][1]), None, ALU.is_ge))
                ch.then(dve.reduce_sum(bad[:, 9:10], bad_t[:, :].rearrange("p (j b) -> p j b", j=6)[:, :, 0:BLOCKS], axis=mybir.AxisListType.XY))
                dve.wait_ge(ones_done, 3)
                ch.then(dve.tensor_tensor(row[:, 0:NB], base_f[:, :], block_ix[:, :], ALU.subtract))
                dve.tensor_scalar(row[:, NB:2 * NB], row[:, 0:NB], float(BLOCK), None, ALU.is_gt)
                ch.then(dve.tensor_scalar(row[:, 0:NB], row[:, 0:NB], float(-BLOCK), None, ALU.is_lt))
                ch.then(dve.reduce_sum(bad[0:1, 10:11], row[:, :], axis=mybir.AxisListType.X))
                ch.mark(dve.tensor_scalar(bad[0:1, 11:12], base_f[:, BLOCKS - 1:BLOCKS], float(NODES - SPAN), None, ALU.is_gt))
                ch.wait()
                dve.sem_inc(bads, 1)
                dve.wait_ge(bads_summed, 1)
                ch.then(dve.reduce_sum(row[:, 0:1], ps_f[0:1, 0:16], axis=mybir.AxisListType.X))
                ch.then(dve.tensor_scalar(flag[:, :], row[:, 0:1], 0.0, None, ALU.is_equal))
                ch.end()

            @block.tensor
            def _(pe):
                pe.wait_ge(rawf_done, 1)
                pe.wait_ge(ones_done, 4)
                for k in range(2):
                    for g, (first_tile, tiles) in enumerate(groups + [(TILES, 1)]):
                        last = pe.transpose(ps[:, k, first_tile:first_tile + tiles], rawf[0:tiles, k, g, :], ident[0:tiles, 0:tiles])
                last.then_inc(turned, 1)
                pe.wait_ge(copied, 1)
                pe.matmul(ps_b[:, 0:NB], ones[0:1, :], dst_f[0:1, 0:TILES + 1:T], start=True, stop=True).then_inc(bases_out, 1)
                pe.wait_ge(bads, 1)
                pe.matmul(ps_f[:, 0:16], ones[:, :], bad[:, :], start=True, stop=True).then_inc(bads_summed, 1)


def gated_messages(nc, x, dst, edge_t, gates, ident, src_ix, dst_ix, place, spans, when):
    with ExitStack() as ctx:
        sb = lambda name, shape, dt=F32: ctx.enter_context(sbuf(nc, name, shape, dt))
        weights = sb("gate_w", [P, 3, 2 * C])
        ends = sb("ends", [P, 4, 3, 2, C])
        turned_ends = sb("turned_ends", [P, 2, 3, 2, P])
        edge = sb("edge_t", [D0 + 1, 2, BLOCK])
        dst_row = sb("dst_row", [P, 2, BLOCK + 2 * P], I32)
        equal = sb("equal", [P, 3, 3 * P])
        logs_, exponent, value = sb("logs", [P, 2, 3, 2, C]), sb("exponent", [P, 2, 3, C]), sb("value", [P, 2, 3, C])
        msg, match = sb("msg", [P, 2, 3, C]), sb("match", [P, 2, 3, WIDEST])
        count = sb("count", [P, WIDEST], I16)
        src_here, dst_here = sb("src_here", [P, 2, T], I32), sb("dst_here", [P, 2, T], I32)
        dst_f, place_f, share = sb("dst_f", [P, 2, T]), sb("place_f", [P, 2, T]), sb("share", [P, 2, T])
        span_out = sb("span_out", [P, 2, SPAN])
        ps_t = ctx.enter_context(psum(nc, "ps_ends", [P, 2 * BANK], F32))
        ps_z = [ctx.enter_context(psum(nc, f"ps_z{s}", [P, 2 * BANK], F32)) for s in range(2)]
        ps_span = ctx.enter_context(psum(nc, "ps_span", [P, 2 * BANK], F32))
        names = ("w_loaded counted ready indexed placed gathered0 gathered1 gathered2 gathered3 edge0 edge1 row0 row1 turned "
                 "evacuated product logs exponents values gated made matched used copied written0 written1 act_chain counted_edges")
        with phase(nc, names, when) as (block, w_loaded, counted, ready, indexed, placed, g0, g1, g2, g3, e0, e1, r0, r1, turned,
                                        evacuated, product, logs, exponents, values, gated, made, matched, used, copied,
                                        wr0, wr1, act_chain, counted_edges):
            gathered, edge_loaded, row_loaded, written = (g0, g1, g2, g3), (e0, e1), (r0, r1), (wr0, wr1)

            def units(b, s, tiles):
                return [(h, 2 * b + h, 2 * s + h, 3, P) for h in range(2)] if tiles == T else [(0, 2 * b, 2 * s, 1, TAIL)]

            def before(b, h, s):
                return (b, 0, s) if h else (b - 1, 1, 1 - s)

            def from_(n, k):
                return not isinstance(n, int) or n >= k

            def width_of(tile, tiles):
                return SPAN if tiles == T else WINDOWS[0][1]

            @block.sync
            def _(sp):
                sp.dma_start(weights[:, 0, :], gates[0]).then_inc(w_loaded, 16)
                sp.dma_start(weights[:, 1, :], gates[1]).then_inc(w_loaded, 16)
                sp.dma_start(weights[0:D0 + 1, 2, :], gates[2]).then_inc(w_loaded, 16)

                def store(b, s, width):
                    sp.wait_ge(copied, b + 1)
                    alone(sp)
                    sp.dma_start(spans[bass.ds(b, 1), :, 0:width].rearrange("a p c -> (a p) c"), span_out[:, s, 0:width]).then_inc(written[s], 16)

                def load(b, s, use, tiles, columns):
                    if from_(b, 2):
                        sp.wait_ge(product, 2 * b - 2)
                        alone(sp)
                        sp.wait_ge(counted_edges, 4 * b - 4)
                        alone(sp)
                    sp.dma_start(edge[0:D0, s, 0:columns], edge_t[:, bass.ds(b * BLOCK, columns)]).then_inc(edge_loaded[s], 16)
                    first_col = P if isinstance(b, int) and b == 0 else 0
                    last_col = min(BLOCK + 2 * P, N - (b * BLOCK - P)) if isinstance(b, int) else BLOCK + 2 * P
                    sp.dma_start(dst_row[:, s, first_col:last_col],
                                 dst[bass.ds(b * BLOCK + first_col - P, last_col - first_col)].partition_broadcast(P)).then_inc(row_loaded[s], 16)
                    if from_(b, 3):
                        store(b - 3, 1 - s, SPAN)
                over_blocks(sp, load, 2)
                store(BLOCKS - 2, 1, SPAN)
                store(BLOCKS - 1, 0, SPAN)
                store(BLOCKS, 1, WINDOWS[0][1])
                for s in range(2):
                    sp.wait_ge(written[s], 16 * (PAIRS + 1))

            @block.gpsimd
            def _(pool):
                pool.iota(count[:, :], [[1, WIDEST]], base=0, channel_multiplier=0).then_inc(counted, 1)

                def gather(b, s, use, tiles, columns):
                    pool.wait_ge(indexed, b + 1)
                    alone(pool)
                    for h, u, q, k, n in units(b, s, tiles):
                        if from_(u, 4):
                            pool.wait_ge(turned, u - 3)
                            alone(pool)
                        for j in range(k):
                            for e, ix in enumerate((src_here, dst_here)):
                                pool.indirect_dma_start(ends[0:n, q, j, e, :], None, x, bass.IndirectOffsetOnAxis(
                                    ap=ix[0:n, s, 3 * h + j:3 * h + j + 1], axis=0)).then_inc(gathered[q], 16)
                over_blocks(pool, gather, 2)

            @block.tensor
            def _(pe):
                pe.wait_ge(w_loaded, 48)
                pe.wait_ge(ready, 2)

                def sum_up(b, h, k, n):
                    u = 2 * b + h
                    if h == 0 and from_(b, 1):
                        pe.wait_ge(copied, b)
                    pe.wait_ge(made, u + 1)
                    pe.wait_ge(matched, u + 1)
                    for j in range(3 * h, 3 * h + k):
                        first_col, width = WINDOWS[j]
                        for lo, hi in bank_parts(first_col, width):
                            last = pe.matmul(ps_span[:, lo:hi], msg[0:n, h, j % 3, :],
                                             match[0:n, h, j % 3, lo - first_col:hi - first_col],
                                             start=j == 0 or (j == 3 and lo >= BANK), stop=True, skip_group_check=True)
                    last.then_inc(used, 1)

                def step(b, s, use, tiles, columns):
                    for h, u, q, k, n in units(b, s, tiles):
                        pe.wait_ge(gathered[q], use * 96 + 32 * k)
                        if from_(u, 1):
                            pe.wait_ge(evacuated, u)
                        for j in range(k):
                            for e in range(2):
                                last = pe.transpose(ps_t[:, (2 * j + e) * P:(2 * j + e) * P + n], ends[0:n, q, j, e, :], ident[0:n, 0:n])
                        last.then_inc(turned, 1)
                        if from_(b, 1):
                            sum_up(b - 1, h, 3, P)
                        pe.wait_ge(evacuated, u + 1)
                        pe.wait_ge(edge_loaded[s], use * 16 + 16)
                        if from_(u, 2):
                            pe.wait_ge(values, u - 1)
                        for j in range(k):
                            z = ps_z[h][0:n, j * 2 * C:(j + 1) * 2 * C]
                            pe.matmul(z, turned_ends[:, h, j, 0, 0:n], weights[:, 0, :], start=True, stop=False)
                            pe.matmul(z, turned_ends[:, h, j, 1, 0:n], weights[:, 1, :], start=False, stop=False)
                            at = (3 * h + j) * P
                            last = pe.matmul(z, edge[0:D0 + 1, s, at:at + n], weights[0:D0 + 1, 2, :], start=False, stop=True)
                        last.then_inc(product, 1)
                over_blocks(pe, step, 2)
                sum_up(BLOCKS - 1, 1, 3, P)
                sum_up(BLOCKS, 0, 1, TAIL)

            def z_part(h, k, n, part):
                return ps_z[h][0:n, 0:2 * C * k].rearrange("p (j e c) -> p j e c", e=2, c=C)[:, :, part, :]

            @block.scalar
            def _(act):
                act.add_instruction(mybir.InstLoadActFuncSet(
                    name=f"I-{nc.next_id()}", act_func_set_id=LN_EXP_TABLE, engine=mybir.EngineType.Activation, ins=[], outs=[]))

                def copy_span(b, s, use, width):
                    act.wait_ge(used, min(2 * b + 2, 2 * BLOCKS + 1) if isinstance(b, int) else 2 * b + 2)
                    alone(act)
                    if from_(b, 2):
                        act.wait_ge(written[s], use * 16)
                    act.activation(span_out[:, s, 0:width], ps_span[:, 0:width], ACT.Copy).then_inc(copied, 1)

                def gate(b, h, k, n):
                    u = 2 * b + h
                    act.wait_ge(product, u + 1)
                    if from_(u, 2):
                        act.wait_ge(values, u - 1)
                    e = logs_[0:n, h, 0:k, :, :].rearrange("p j e c -> p (j e c)")
                    act.activation(e, ps_z[h][0:n, 0:2 * C * k], ACT.Abs).then_inc(act_chain, 1)
                    act.wait_ge(act_chain, 2 * u + 1)
                    act.activation(e, e, ACT.Exp, scale=-1.0).then_inc(act_chain, 1)
                    act.wait_ge(act_chain, 2 * u + 2)
                    act.activation(e, e, ACT.Ln, bias=1.0).then_inc(logs, 1)
                    act.wait_ge(exponents, u + 1)
                    act.activation(exponent[0:n, h, 0:k, :], exponent[0:n, h, 0:k, :], ACT.Exp).then_inc(gated, 1)

                def step(b, s, use, tiles, columns):
                    for h, u, q, k, n in units(b, s, tiles):
                        act.wait_ge(turned, u + 1)
                        if from_(u, 2):
                            act.wait_ge(product, u - 1)
                        for j in range(0, k, 2):
                            m = min(2, k - j)
                            last = act.activation(turned_ends[:, h, j:j + m, :, 0:n].rearrange("p j e c -> p (j e) c"),
                                                  ps_t[:, j * 2 * P:(j + m) * 2 * P].rearrange("p (j c) -> p j c", c=P)[:, :, 0:n], ACT.Copy)
                        last.then_inc(evacuated, 1)
                        b_, h_, s_ = before(b, h, s)
                        if from_(b_, 0):
                            gate(b_, h_, 3, P)
                        if h == 1 and from_(b, 1):
                            copy_span(b - 1, 1 - s, (b - 1 - (1 - s)) // 2 if isinstance(b, int) else use - (1 - s), SPAN)
                over_blocks(act, step, 2)
                gate(BLOCKS, 0, 1, TAIL)
                copy_span(BLOCKS - 1, 0, PAIRS, SPAN)
                copy_span(BLOCKS, 1, PAIRS, WINDOWS[0][1])

            @block.vector
            def _(dve):
                dve.memset(dst_row[:, 0, 0:P], -1).then_inc(ready, 1)
                dve.memset(edge[D0:D0 + 1, :, :], 1.0).then_inc(ready, 1)
                dve.wait_ge(ready, 2)
                dve.wait_ge(counted, 1)

                def index(b, s, tiles):
                    dve.tensor_copy(src_here[:, s, 0:tiles], src_ix[:, bass.ds(b * T, tiles)])
                    dve.tensor_copy(dst_here[:, s, 0:tiles], dst_ix[:, bass.ds(b * T, tiles)]).then_inc(indexed, 1)

                def put_places(b, s, tiles):
                    dve.tensor_copy(dst_f[:, s, 0:tiles], dst_ix[:, bass.ds(b * T, tiles)])
                    dve.tensor_copy(place_f[:, s, 0:tiles], place[:, bass.ds(b * T, tiles)]).then_inc(placed, 1)

                def shares(b, h, s, k, n):
                    ch = Chain(dve, counted_edges, 2 * b + h, 2)
                    for j in range(3 * h, 3 * h + k):
                        width = 3 * P
                        if isinstance(b, int):
                            width = min(width, N - (b * BLOCK + (j - 1) * P))
                        last = dve.tensor_scalar(equal[0:n, j % 3, 0:width], dst_row[0:n, s, j * P:j * P + width], dst_f[0:n, s, j:j + 1],
                                                 None, ALU.is_equal, op1=ALU.add, accum_out=share[0:n, s, j:j + 1])
                    ch.then(last)
                    ch.then(dve.reciprocal(share[0:n, s, 3 * h:3 * h + k], share[0:n, s, 3 * h:3 * h + k]))
                    ch.end()

                def message(b, h, s, k, n):
                    u = 2 * b + h
                    dve.wait_ge(logs, u + 1)
                    if from_(u, 2):
                        dve.wait_ge(made, u - 1)
                    logs_of = lambda part: logs_[0:n, h, 0:k, part, :]
                    dve.scalar_tensor_tensor(out=exponent[0:n, h, 0:k, :], in0=z_part(h, k, n, 0), scalar=0.0, in1=logs_of(0),
                                             op0=ALU.min, op1=ALU.subtract).then_inc(exponents, 1)
                    dve.scalar_tensor_tensor(out=value[0:n, h, 0:k, :], in0=z_part(h, k, n, 1), scalar=0.0, in1=logs_of(1),
                                             op0=ALU.max, op1=ALU.add).then_inc(values, 1)
                    if from_(u, 2):
                        dve.wait_ge(used, u - 1)
                    for j in range(3 * h, 3 * h + k):
                        width = WINDOWS[j][1]
                        last = dve.tensor_scalar(match[0:n, h, j % 3, 0:width], count[0:n, 0:width], place_f[0:n, s, j:j + 1], None,
                                                 ALU.is_equal)
                    last.then_inc(matched, 1)
                    dve.wait_ge(values, u + 1)
                    dve.wait_ge(gated, u + 1)
                    for j in range(k):
                        last = dve.scalar_tensor_tensor(out=msg[0:n, h, j, :], in0=exponent[0:n, h, j, :], scalar=share[0:n, s, 3 * h + j:3 * h + j + 1],
                                                        in1=value[0:n, h, j, :], op0=ALU.mult, op1=ALU.mult)
                    last.then_inc(made, 1)

                def step(b, s, use, tiles, columns):
                    following = 1 if isinstance(b, int) and b == BLOCKS - 1 else T
                    dve.wait_ge(placed, b + 1)
                    dve.wait_ge(row_loaded[s], use * 16 + 16)
                    for h, u, q, k, n in units(b, s, tiles):
                        if h == 0 and tiles == T:
                            if from_(b, 1):
                                dve.wait_ge(turned, 2 * b)
                                alone(dve)
                            index(b + 1, 1 - s, following)
                        shares(b, h, s, k, n)
                        b_, h_, s_ = before(b, h, s)
                        if from_(b_, 0):
                            message(b_, h_, s_, 3, P)
                        if h == 0 and tiles == T:
                            if from_(b, 1):
                                dve.wait_ge(matched, 2 * b)
                                dve.wait_ge(made, 2 * b)
                                alone(dve)
                            put_places(b + 1, 1 - s, following)

                index(0, 0, T)
                put_places(0, 0, T)
                over_blocks(dve, step, 2)
                message(BLOCKS, 0, 1, 1, TAIL)


def assemble(nc, x_t, spans, base, feat, vecs, scale, gamma, beta, when):
    with ExitStack() as ctx:
        span = ctx.enter_context(sbuf(nc, "span", [P, 2, SPAN], F32))
        mv = ctx.enter_context(sbuf(nc, "mv", [P, 4], F32))
        stats = ctx.enter_context(psum(nc, "stats", [P, 2 * BANK], F32))
        with phase(nc, "nodes0 nodes1 span0 span1 added taken root var vec", when) as \
                (block, nodes0, nodes1, span0, span1, added, taken, root, var, vec):
            nodes_loaded, span_loaded = (nodes0, nodes1), (span0, span1)

            @block.sync
            def _(sp):
                def nodes(b, s, columns):
                    sp.dma_start(feat[:, bass.ds(b * BLOCK, columns)], x_t[:, bass.ds(b * BLOCK, columns)]).then_inc(nodes_loaded[s], 16)

                def sums(b, s, width):
                    sp.dma_start(span[:, s, 0:width], spans[bass.ds(b, 1), :, 0:width].rearrange("a p c -> (a p) c")).then_inc(span_loaded[s], 16)

                def load(b, s, use, tiles, columns):
                    if not isinstance(b, int) or b >= 3:
                        sp.wait_ge(added, b - 1)
                        alone(sp)
                    if tiles == T:
                        nodes(b + 1, 1 - s, TAIL if isinstance(b, int) and b == BLOCKS - 1 else BLOCK)
                    if not isinstance(b, int) or b >= 1:
                        sums(b - 1, 1 - s, SPAN)

                nodes(0, 0, BLOCK)
                over_blocks(sp, load, 2)
                sp.wait_ge(added, BLOCKS)
                alone(sp)
                sums(BLOCKS, 1, WINDOWS[0][1])

            @block.scalar
            def _(act):
                root_of(act, root, var, mv)

            @block.vector
            def _(dve):
                dve.memset(feat[:, N:NODES], 0.0).then_inc(added, 1)

                def add_span(b, s, use, width):
                    at = dve.value_load(base[0:1, bass.ds(b, 1)], min_val=0, max_val=NODES - width)
                    dve.wait_ge(span_loaded[s], use * 16 + 16)
                    dve.wait_ge(added, b + 1)
                    here = feat[:, bass.ds(at, width)]
                    dve.tensor_tensor(here, here, span[:, s, 0:width], ALU.add).then_inc(added, 1)

                def statistics(b, columns, spans_added):
                    dve.wait_ge(added, spans_added)
                    alone(dve)
                    for c, at, n in halves(columns):
                        last = dve.bn_stats(stats[:, bass.ds((2 * b + c) * 6, 6)], feat[:, bass.ds(b * BLOCK + at, n)])
                    last.then_inc(taken, 1)

                def step(b, s, use, tiles, columns):
                    if tiles == T:
                        dve.wait_ge(nodes_loaded[1 - s], (use + s) * 16 + 16)
                    if not isinstance(b, int) or b >= 1:
                        add_span(b - 1, 1 - s, use + s - 1, SPAN)
                    if not isinstance(b, int) or b >= 3:
                        statistics(b - 3, BLOCK, b)
                dve.wait_ge(nodes_loaded[0], 16)
                over_blocks(dve, step, 2)
                add_span(BLOCKS, 1, PAIRS, WINDOWS[0][1])
                for b in range(BLOCKS - 2, BLOCKS + 1):
                    statistics(b, BLOCK if b < BLOCKS else TAIL, BLOCKS + 2)
                dve.wait_ge(taken, BLOCKS + 1)
                batch_scale(dve, root, var, Chain(dve, vec, 0, 4), stats[:, 0:CHUNKS * 6], mv, scale, vecs, gamma, beta)


def load_nodes(nc, x_t, feat, when):
    with phase(nc, "loaded", when) as (block, loaded):
        @block.sync
        def _(sp):
            sp.dma_start(feat[:, 0:N], x_t).then_inc(loaded, 16)
            sp.wait_ge(loaded, 16)

        @block.vector
        def _(dve):
            dve.memset(feat[:, N:NODES], 0.0)


def zero_rows(nc, agg, when):
    rows, width = agg.shape
    words = rows * width // 16
    piece = 1
    for k in range(1, 3001):
        if words % k == 0:
            piece = k
    flat = agg.rearrange("r w -> (r w)").rearrange("(a n) -> a n", a=16)
    with ExitStack() as ctx:
        zeros = ctx.enter_context(sbuf(nc, "zeros", [16, piece], F32))
        with phase(nc, "zeros_set zeroed", when) as (block, zeros_set, zeroed):
            @block.vector
            def _(dve):
                dve.memset(zeros[:, :], 0.0).then_inc(zeros_set, 1)

            @block.sync
            def _(sp):
                sp.wait_ge(zeros_set, 1)
                with sp.Fori(0, words // piece) as k:
                    sp.dma_start(flat[:, bass.ds(k * piece, piece)], zeros[:, :]).then_inc(zeroed, 16)
                sp.wait_ge(zeroed, words // piece * 16)


def scatter_messages(nc, table, edges, gates, ident, src_ix, dst_ix, agg, when):
    zero_rows(nc, agg, when)
    width = agg.shape[1]
    d = edges.shape[1]
    with ExitStack() as ctx:
        sb = lambda name, shape, dt=F32: ctx.enter_context(sbuf(nc, name, shape, dt))
        six, dix, gix = (sb(n, [P, 1], I32) for n in ("six", "dix", "gix"))
        ds_, spare, low, to, tof = (sb(n, [P, 1]) for n in ("dst_here", "spare", "low", "to", "tof"))
        same, tmp, lower = sb("same", [P, P]), sb("tmp", [P, P]), sb("lower", [P, P])
        xs, ed, msg, total = sb("xs", [P, C]), sb("ed", [P, d]), sb("msg", [P, width]), sb("total", [P, width])
        if gates:
            xd, tT = sb("xd", [P, C]), sb("tT", [P, 3, P])
            weights = sb("gate_w", [P, 3, 2 * C])
            e1, e2 = sb("e1", [P, C]), sb("e2", [P, C])
        ps_d = ctx.enter_context(psum(nc, "ps_dst", [P, BANK], F32))
        ps_m = ctx.enter_context(psum(nc, "ps_total", [P, BANK], F32))
        ps_t = ctx.enter_context(psum(nc, "ps_turned", [P, 3, P], F32))
        ps_z = ctx.enter_context(psum(nc, "ps_z", [P, 2 * C], F32))
        names = "ready wloaded indexed dst_turned edge_loaded gathered added index_made msg_made summed total_made turned turned_copied gated gate_vals vec"
        with phase(nc, names, when) as (block, ready, wloaded, indexed, dst_turned, edge_loaded, gathered, added, index_made,
                                  msg_made, summed, total_made, turned, turned_copied, gated, gate_vals, vec):
            @block.sync
            def _(sp):
                if gates:
                    sp.dma_start(weights[:, 0, :], gates[0]).then_inc(wloaded, 16)
                    sp.dma_start(weights[:, 1, :], gates[1]).then_inc(wloaded, 16)
                    sp.dma_start(weights[0:D0 + 1, 2, :], gates[2]).then_inc(wloaded, 16)

                def load(t, rows):
                    sp.wait_ge(indexed, t + 1)
                    alone(sp)
                    sp.dma_start(ed[0:rows, :], edges[bass.ds(t * P, rows), :]).then_inc(edge_loaded, 16)
                over_tiles(sp, load)

            @block.gpsimd
            def _(pool):
                pool.iota(gix[:, :], [[0, 1]], base=N, channel_multiplier=1).then_inc(ready, 1)
                pool.memset(lower[:, :], 1.0).then_inc(ready, 1)
                pool.wait_ge(ready, 2)
                pool.affine_select(out=lower[:, :], in_=lower[:, :], compare_op=ALU.is_gt, fill=0.0,
                                   base=0, pattern=[[-1, P]], channel_multiplier=1).then_inc(ready, 1)

                def tile(t, rows):
                    pool.wait_ge(indexed, t + 1)
                    alone(pool)
                    pool.indirect_dma_start(xs[0:rows, :], None, table,
                                            bass.IndirectOffsetOnAxis(ap=six[0:rows, 0:1], axis=0)).then_inc(gathered, 16)
                    if gates:
                        pool.indirect_dma_start(xd[0:rows, :], None, table,
                                                bass.IndirectOffsetOnAxis(ap=dix[0:rows, 0:1], axis=0)).then_inc(gathered, 16)
                    pool.wait_ge(total_made, t + 1)
                    alone(pool)
                    pool.indirect_dma_start(agg, bass.IndirectOffsetOnAxis(ap=dix[0:rows, 0:1], axis=0),
                                            total[0:rows, :], None, compute_op=ALU.add).then_inc(added, 16)
                over_tiles(pool, tile)

            @block.tensor
            def _(pe):
                if gates:
                    pe.wait_ge(wloaded, 48)

                def tile(t, rows):
                    pe.wait_ge(indexed, t + 1)
                    pe.transpose(ps_d[0:rows, 0:rows], ds_[0:rows, 0:1].to_broadcast([rows, rows]),
                                 ident[0:rows, 0:rows]).then_inc(dst_turned, 1)
                    if gates:
                        pe.wait_ge(gathered, 32 * t + 32)
                        pe.wait_ge(edge_loaded, 16 * t + 16)
                        pe.transpose(ps_t[:, 0, 0:rows], xs[0:rows, :], ident[0:rows, 0:rows])
                        pe.transpose(ps_t[:, 1, 0:rows], xd[0:rows, :], ident[0:rows, 0:rows])
                        pe.transpose(ps_t[0:D0, 2, 0:rows], ed[0:rows, :], ident[0:rows, 0:rows]).then_inc(turned, 1)
                        pe.wait_ge(turned_copied, t + 1)
                        pe.matmul(ps_z[0:rows, :], tT[:, 0, 0:rows], weights[:, 0, :], start=True, stop=False)
                        pe.matmul(ps_z[0:rows, :], tT[:, 1, 0:rows], weights[:, 1, :], start=False, stop=False)
                        pe.matmul(ps_z[0:rows, :], tT[0:D0 + 1, 2, 0:rows], weights[0:D0 + 1, 2, :],
                                  start=False, stop=True).then_inc(gated, 1)
                    pe.wait_ge(msg_made, t + 1)
                    pe.matmul(ps_m[0:rows, 0:width], same[0:rows, 0:rows], msg[0:rows, :],
                              start=True, stop=True).then_inc(summed, 1)
                over_tiles(pe, tile)

            if gates:
                @block.scalar
                def _(act):
                    def tile(t, rows):
                        act.wait_ge(turned, t + 1)
                        act.activation(tT[:, 0:2, 0:rows], ps_t[:, 0:2, 0:rows], ACT.Copy)
                        act.activation(tT[0:D0, 2, 0:rows], ps_t[0:D0, 2, 0:rows], ACT.Copy).then_inc(turned_copied, 1)
                        act.wait_ge(gated, t + 1)
                        act.activation(e1[0:rows, :], ps_z[0:rows, 0:C], ACT.Exp, scale=-1.0)
                        act.activation(e2[0:rows, :], ps_z[0:rows, C:2 * C], ACT.Abs).then_inc(gate_vals, 1)
                        act.wait_ge(gate_vals, 3 * t + 1)
                        act.activation(e2[0:rows, :], e2[0:rows, :], ACT.Exp, scale=-1.0).then_inc(gate_vals, 1)
                        act.wait_ge(gate_vals, 3 * t + 2)
                        act.activation(e2[0:rows, :], e2[0:rows, :], ACT.Ln, bias=1.0).then_inc(gate_vals, 1)
                    over_tiles(act, tile)

            @block.vector
            def _(dve):
                dve.wait_ge(ready, 3)
                dve.tensor_copy(spare[:, :], gix[:, :]).then_inc(ready, 1)
                dve.wait_ge(ready, 4)
                if gates:
                    dve.memset(tT[D0:D0 + 1, 2, :], 1.0)
                    dve.memset(msg[:, C:AGG], 1.0).then_inc(ready, 1)
                    dve.wait_ge(ready, 5)

                def tile(t, rows):
                    ch = Chain(dve, vec, t, 7 if gates else 6)
                    r = slice(0, rows)
                    dve.tensor_copy(six[r, :], src_ix[r, bass.ds(t, 1)])
                    dve.tensor_copy(dix[r, :], dst_ix[r, bass.ds(t, 1)])
                    dve.tensor_copy(ds_[r, :], dst_ix[r, bass.ds(t, 1)]).then_inc(indexed, 1)
                    dve.wait_ge(dst_turned, t + 1)
                    dve.wait_ge(indexed, t + 1)
                    ch.then(dve.tensor_scalar(same[r, r], ps_d[r, r], ds_[r, 0:1], None, ALU.is_equal))
                    ch.then(dve.tensor_tensor_reduce(out=tmp[r, r], in0=same[r, r], in1=lower[r, r], scale=1.0, scalar=0.0,
                                                     op0=ALU.mult, op1=ALU.add, accum_out=low[r, :]))
                    ch.then(dve.tensor_tensor(to[r, :], spare[r, :], ds_[r, :], ALU.subtract))
                    ch.then(dve.scalar_tensor_tensor(out=tof[r, :], in0=low[r, :], scalar=0.0, in1=to[r, :],
                                                     op0=ALU.is_gt, op1=ALU.mult))
                    if gates:
                        dve.wait_ge(gate_vals, 3 * t + 3)
                        ch.then(dve.scalar_tensor_tensor(out=e2[r, :], in0=ps_z[r, C:2 * C], scalar=0.0, in1=e2[r, :],
                                                         op0=ALU.max, op1=ALU.add))
                        ch.then(dve.tensor_scalar(e1[r, :], e1[r, :], 1.0, None, ALU.add))
                        ch.then(dve.reciprocal(e1[r, :], e1[r, :]))
                        dve.tensor_tensor(msg[r, 0:C], e2[r, :], e1[r, :], ALU.mult).then_inc(msg_made, 1)
                    else:
                        dve.wait_ge(gathered, 16 * t + 16)
                        dve.wait_ge(edge_loaded, 16 * t + 16)
                        ch.then(dve.tensor_tensor(tmp[r, 0:C], xs[r, :], ed[r, :], ALU.add))
                        ch.mark(dve.tensor_scalar(msg[r, :], tmp[r, 0:C], 0.0, None, ALU.max))
                        ch.wait()
                        dve.sem_inc(msg_made, 1)
                    dve.wait_ge(summed, t + 1)
                    dve.tensor_copy(total[r, :], ps_m[r, 0:width])
                    dve.tensor_tensor(dix[r, :], tof[r, :], ds_[r, :], ALU.add).then_inc(total_made, 1)
                    dve.wait_ge(added, 16 * t + 16)
                    ch.end()
                over_tiles(dve, tile)


def sorted_messages(nc, table, edges, src_ix, place, base, w, feat, vecs, scale, bias, gamma, beta, when):
    with ExitStack() as ctx:
        sb = lambda name, shape, dt=F32: ctx.enter_context(sbuf(nc, name, shape, dt))
        msg = sb("msg", [P, 4, 3, C])
        edge = sb("edge", [P, 2, 3, C])
        match = sb("match", [P, 2, WIDEST])
        count = sb("count", [P, WIDEST], I16)
        index = sb("index", [P, 2, T], I32)
        at_ = sb("place_here", [P, 2, T])
        w_sb, mv = sb("w_sb", [P, C]), sb("mv", [P, 4])
        span = [ctx.enter_context(psum(nc, f"ps_span{s}", [P, 2 * BANK], F32)) for s in range(2)]
        ps = ctx.enter_context(psum(nc, "ps_h", [P, 2, BANK], F32))
        stats = ctx.enter_context(psum(nc, "stats", [P, 2 * BANK], F32))
        names = ("w_loaded counted indexed gathered0 gathered1 gathered2 gathered3 edge0 edge1 summed made matched "
                 "tile_used added product stored taken root var vec")
        with phase(nc, names, when) as (block, w_loaded, counted, indexed, g0, g1, g2, g3, e0, e1, summed, made, matched,
                                        tile_used, added, product, stored, taken, root, var, vec):
            gathered, edge_loaded = (g0, g1, g2, g3), (e0, e1)
            last_step = BLOCKS + 1

            def units(b, s, tiles):
                return [(h, 2 * b + h, 2 * s + h, 3) for h in range(2)] if tiles == T else [(0, 2 * b, 2 * s, 1)]

            @block.sync
            def _(sp):
                sp.dma_start(w_sb[:, :], w).then_inc(w_loaded, 16)

                def load(b, s, use, tiles, columns):
                    for h, u, _, n in units(b, s, tiles):
                        sp.wait_ge(summed, u + 1)
                        alone(sp)
                        if tiles == T:
                            rows = edges[bass.ds(b * BLOCK + h * HALF, HALF), :].rearrange("(t p) c -> p t c", p=P)
                            sp.dma_start(edge[:, h, :, :], rows).then_inc(edge_loaded[h], 16)
                        else:
                            sp.dma_start(edge[0:columns, h, 0, :], edges[N - columns:N, :]).then_inc(edge_loaded[h], 16)
                over_blocks(sp, load, 2)

            @block.gpsimd
            def _(pool):
                pool.iota(count[:, :], [[1, WIDEST]], base=0, channel_multiplier=0).then_inc(counted, 1)

                def gather(b, s, use, tiles, columns):
                    pool.wait_ge(indexed, b + 1)
                    alone(pool)
                    n = P if tiles == T else columns
                    for h, u, q, k in units(b, s, tiles):
                        if not isinstance(u, int) or u >= 4:
                            pool.wait_ge(tile_used, b * T + (3 * h - 7))
                            alone(pool)
                        for j in range(k):
                            pool.indirect_dma_start(msg[0:n, q, j, :], None, table, bass.IndirectOffsetOnAxis(
                                ap=index[0:n, s, 3 * h + j:3 * h + j + 1], axis=0)).then_inc(gathered[q], 16)
                over_blocks(pool, gather, 2)

            @block.scalar
            def _(act):
                act.sem_inc(stored, 1)

                def store(b, columns):
                    act.wait_ge(product, b + 1)
                    alone(act)
                    act.activation(feat_block(feat, b, columns), banks(ps, columns), ACT.Identity,
                                   bias=vecs[:, bias:bias + 1]).then_inc(stored, 1)

                def step(b, s, use, tiles, columns):
                    n = P if tiles == T else columns
                    for h, u, q, k in units(b, s, tiles):
                        act.wait_ge(summed, u + 3)
                        act.activation(msg[0:n, q, 0:k, :], msg[0:n, q, 0:k, :], ACT.Relu).then_inc(made, 1)
                    if not isinstance(b, int) or b >= LAG:
                        store(b - LAG, BLOCK)
                over_blocks(act, step, 2)
                for b in range(last_step - LAG, last_step):
                    store(b, BLOCK if b < BLOCKS else TAIL)
                root_of(act, root, var, mv)

            @block.vector
            def _(dve):
                dve.sem_inc(summed, 2)
                dve.wait_ge(counted, 1)

                def indices(b, s, tiles):
                    dve.tensor_copy(index[:, s, 0:tiles], src_ix[:, bass.ds(b * T, tiles)])
                    dve.tensor_copy(at_[:, s, 0:tiles], place[:, bass.ds(b * T, tiles)]).then_inc(indexed, 1)

                def add_span(b, s, width, tiles=T):
                    at = dve.value_load(base[0:1, bass.ds(b, 1)], min_val=0, max_val=NODES - width)
                    dve.wait_ge(tile_used, b * T + (tiles + 2))
                    dve.wait_ge(added, b + 1)
                    here = feat[:, bass.ds(at, width)]
                    dve.tensor_tensor(here, here, span[s][:, 0:width], ALU.add).then_inc(added, 1)

                def statistics(b, columns):
                    dve.wait_ge(stored, b + 2)
                    alone(dve)
                    for c, at, n in halves(columns):
                        last = dve.bn_stats(stats[:, bass.ds((2 * b + c) * 6, 6)], feat[:, bass.ds(b * BLOCK + at, n)])
                    last.then_inc(taken, 1)

                def step(b, s, use, tiles, columns):
                    n = P if tiles == T else columns
                    if not isinstance(b, int) or b >= 1:
                        dve.wait_ge(matched, b * T)
                    if tiles == T:
                        indices(b + 1, 1 - s, 1 if isinstance(b, int) and b == BLOCKS - 1 else T)
                    for h, u, q, k in units(b, s, tiles):
                        dve.wait_ge(gathered[q], (use * 3 + k) * 16)
                        dve.wait_ge(edge_loaded[h], b * 16 + 16)
                        dve.tensor_tensor(msg[0:n, q, 0:k, :], msg[0:n, q, 0:k, :], edge[0:n, h, 0:k, :], ALU.add).then_inc(summed, 1)
                        for j in range(3 * h, 3 * h + k):
                            width = WINDOWS[j][1]
                            dve.wait_ge(tile_used, b * T + j + 1)
                            dve.tensor_scalar(match[0:n, j % 2, 0:width], count[0:n, 0:width], at_[0:n, s, j:j + 1], None,
                                              ALU.is_equal).then_inc(matched, 1)
                    if not isinstance(b, int) or b >= 1:
                        add_span(b - 1, 1 - s, SPAN)
                    if not isinstance(b, int) or b > LAG:
                        statistics(b - LAG - 1, BLOCK)

                dve.sem_inc(added, 1)
                indices(0, 0, T)
                dve.wait_ge(indexed, 1)
                over_blocks(dve, step, 2)
                add_span(BLOCKS, 1, WINDOWS[0][1], 1)
                for b in range(last_step - LAG - 1, last_step):
                    statistics(b, BLOCK if b < BLOCKS else TAIL)
                dve.wait_ge(taken, BLOCKS + 1)
                batch_scale(dve, root, var, Chain(dve, vec, 0, 4), stats[:, 0:CHUNKS * 6], mv, scale, vecs, gamma, beta)

            @block.tensor
            def _(pe):
                pe.wait_ge(w_loaded, 16)
                pe.sem_inc(tile_used, 2)

                def multiply(b, columns, spans_added):
                    pe.wait_ge(added, spans_added)
                    pe.wait_ge(stored, b + 1)
                    for c, at, n in halves(columns):
                        last = pe.matmul(ps[:, c, 0:n], w_sb[:, :], feat[:, bass.ds(b * BLOCK + at, n)], start=True, stop=True)
                    last.then_inc(product, 1)

                def step(b, s, use, tiles, columns):
                    n = P if tiles == T else columns
                    if not isinstance(b, int) or b >= LAG:
                        multiply(b - LAG, BLOCK, b)
                    if not isinstance(b, int) or b >= 2:
                        pe.wait_ge(added, b)
                    for h, u, q, k in units(b, s, tiles):
                        pe.wait_ge(made, u + 1)
                        for j in range(3 * h, 3 * h + k):
                            first_col, width = WINDOWS[j]
                            pe.wait_ge(matched, b * T + j + 1)
                            for lo, hi in bank_parts(first_col, width):
                                last = pe.matmul(span[s][:, lo:hi], msg[0:n, q, j % 3, :],
                                                 match[0:n, j % 2, lo - first_col:hi - first_col],
                                                 start=j == 0 or (j == 3 and lo >= BANK), stop=True, skip_group_check=True)
                            last.then_inc(tile_used, 1)
                over_blocks(pe, step, 2)
                for b in range(last_step - LAG, last_step):
                    multiply(b, BLOCK if b < BLOCKS else TAIL, last_step + 1)


def bank_parts(first_col, width):
    end = first_col + width
    if first_col < BANK < end:
        return [(first_col, BANK), (BANK, end)]
    return [(first_col, end)]


def add_sums(nc, agg, feat, ident, mean, when):
    width = agg.shape[1]
    with ExitStack() as ctx:
        sb = lambda name, shape, dt=F32: ctx.enter_context(sbuf(nc, name, shape, dt))
        rows_ = sb("sum_rows", [P, width])
        cnt, rec = sb("cnt", [P, 1]), sb("rec", [P, 1])
        ps = ctx.enter_context(psum(nc, "ps_sums", [P, P], F32))
        with phase(nc, "loaded scaled turned added vec", when) as (block, loaded, scaled, turned, added, vec):
            @block.sync
            def _(sp):
                sp.sem_inc(added, 1)

                def load(t, rows):
                    sp.wait_ge(added, t + 1)
                    alone(sp)
                    sp.dma_start(rows_[0:rows, :], agg[bass.ds(t * P, rows), :]).then_inc(loaded, 16)
                over_tiles(sp, load)

            @block.tensor
            def _(pe):
                def tile(t, rows):
                    pe.wait_ge(scaled, t + 1)
                    pe.transpose(ps[:, 0:rows], rows_[0:rows, 0:C], ident[0:rows, 0:rows]).then_inc(turned, 1)
                over_tiles(pe, tile)

            @block.vector
            def _(dve):
                def tile(t, rows):
                    r = slice(0, rows)
                    dve.wait_ge(loaded, 16 * t + 16)
                    if mean:
                        ch = Chain(dve, vec, t, 3)
                        ch.then(dve.tensor_scalar(cnt[r, :], rows_[r, C:C + 1], 1.0, None, ALU.max))
                        ch.then(dve.reciprocal(rec[r, :], cnt[r, :]))
                        ch.then(dve.tensor_scalar(rows_[r, 0:C], rows_[r, 0:C], rec[r, 0:1], None, ALU.mult))
                        ch.end()
                    dve.sem_inc(scaled, 1)
                    dve.wait_ge(turned, t + 1)
                    here = feat[:, bass.ds(t * P, rows)]
                    dve.tensor_tensor(here, here, ps[:, 0:rows], ALU.add).then_inc(added, 1)
                over_tiles(dve, tile)


def batch_scale(dve, act_sem, var_sem, chain, stats, mv, scale, vecs, gamma, beta, bias=None):
    chain.then(dve.bn_aggr(mv[:, 0:2], stats))
    dve.tensor_scalar(mv[:, 1:2], mv[:, 1:2], EPS, None, ALU.add).then_inc(var_sem, 1)
    dve.wait_ge(act_sem, 1)
    chain.then(dve.reciprocal(mv[:, 3:4], mv[:, 2:3]))
    chain.then(dve.tensor_tensor(scale[:, 0:1], mv[:, 3:4], vecs[:, gamma:gamma + 1], ALU.mult))
    if bias is not None:
        chain.then(dve.tensor_tensor(mv[:, 0:1], mv[:, 0:1], vecs[:, bias:bias + 1], ALU.add))
    chain.then(dve.tensor_tensor(mv[:, 3:4], mv[:, 0:1], scale[:, 0:1], ALU.mult))
    dve.tensor_tensor(scale[:, 1:2], vecs[:, beta:beta + 1], mv[:, 3:4], ALU.subtract)


def root_of(act, act_sem, var_sem, mv):
    act.wait_ge(var_sem, 1)
    act.activation(mv[:, 2:3], mv[:, 1:2], ACT.Sqrt).then_inc(act_sem, 1)


def norm_stats(nc, feat, vecs, scale, gamma, beta, when):
    with ExitStack() as ctx:
        stats = ctx.enter_context(sbuf(nc, "stats", [P, CHUNKS, 6], F32))
        mv = ctx.enter_context(sbuf(nc, "mv", [P, 4], F32))
        with phase(nc, "taken root var vec", when) as (block, taken, root, var, vec):
            @block.vector
            def _(dve):
                def take(b, s, use, tiles, columns):
                    for c, at, w in halves(columns):
                        dve.bn_stats(stats[:, bass.ds(2 * b + c, 1), :].rearrange("p a b -> p (a b)"),
                                     feat[:, bass.ds(b * BLOCK + at, w)]).then_inc(taken, 1)
                over_blocks(dve, take)
                dve.wait_ge(taken, CHUNKS)
                batch_scale(dve, root, var, Chain(dve, vec, 0, 4), stats[:, :, :].rearrange("p a b -> p (a b)"), mv, scale, vecs, gamma, beta)

            @block.scalar
            def _(act):
                root_of(act, root, var, mv)


def first_product(nc, w, feat, vecs, scale, bias, gamma, beta, when):
    with ExitStack() as ctx:
        stats = ctx.enter_context(sbuf(nc, "stats", [P, CHUNKS, 6], F32))
        mv = ctx.enter_context(sbuf(nc, "mv", [P, 4], F32))
        w_sb = ctx.enter_context(sbuf(nc, "w_sb", [P, C], F32))
        ps = [ctx.enter_context(psum(nc, f"ps_h{s}", [P, 2, BANK], F32)) for s in range(2)]
        with phase(nc, "w_loaded product taken stored root var vec", when) as (block, w_loaded, product, taken, stored, root, var, vec):
            @block.sync
            def _(sp):
                sp.dma_start(w_sb[:, :], w).then_inc(w_loaded, 16)

            @block.tensor
            def _(pe):
                pe.wait_ge(w_loaded, 16)

                def multiply(b, s, use, tiles, columns):
                    pe.wait_ge(stored, b + 1)
                    for c, at, n in halves(columns):
                        last = pe.matmul(ps[s][:, c, 0:n], w_sb[:, :], feat[:, bass.ds(b * BLOCK + at, n)], start=True, stop=True)
                    last.then_inc(product, 1)
                over_blocks(pe, multiply)

            @block.scalar
            def _(act):
                act.sem_inc(stored, 2)

                def store(b, s, use, tiles, columns):
                    act.wait_ge(product, b + 1)
                    alone(act)
                    act.activation(feat_block(feat, b, columns), banks(ps[s], columns), ACT.Identity,
                                   bias=vecs[:, bias:bias + 1]).then_inc(stored, 1)
                over_blocks(act, store)
                root_of(act, root, var, mv)

            @block.vector
            def _(dve):
                def take(b, s, use, tiles, columns):
                    dve.wait_ge(stored, b + 3)
                    alone(dve)
                    for c, at, n in halves(columns):
                        last = dve.bn_stats(stats[:, bass.ds(2 * b + c, 1), :].rearrange("p a b -> p (a b)"),
                                            feat[:, bass.ds(b * BLOCK + at, n)])
                    last.then_inc(taken, 1)
                over_blocks(dve, take)
                dve.wait_ge(taken, BLOCKS + 1)
                batch_scale(dve, root, var, Chain(dve, vec, 0, 4), stats[:, :, :].rearrange("p a b -> p (a b)"), mv, scale, vecs, gamma, beta)


def second_product(nc, w, feat, vecs, scale, bias, gamma, beta):
    with ExitStack() as ctx:
        stats = ctx.enter_context(sbuf(nc, "stats", [P, CHUNKS, 6], F32))
        mv = ctx.enter_context(sbuf(nc, "mv", [P, 4], F32))
        w_sb = ctx.enter_context(sbuf(nc, "w_sb", [P, C], F32))
        hidden = ctx.enter_context(sbuf(nc, "hidden", [P, 2, BLOCK], F32))
        ps = [ctx.enter_context(psum(nc, f"ps_h{s}", [P, 2, BANK], F32)) for s in range(2)]
        with phase(nc, "w_loaded made product used root var vec") as (block, w_loaded, made, product, used, root, var, vec):
            @block.sync
            def _(sp):
                sp.dma_start(w_sb[:, :], w).then_inc(w_loaded, 16)

            @block.scalar
            def _(act):
                def make(b, s, use, tiles, columns):
                    act.wait_ge(product, b + 1)
                    alone(act)
                    act.activation(hidden[:, s, 0:columns], feat[:, bass.ds(b * BLOCK, columns)], ACT.Relu,
                                   bias=scale[:, 1:2], scale=scale[:, 0:1]).then_inc(made, 1)
                over_blocks(act, make)
                root_of(act, root, var, mv)

            @block.tensor
            def _(pe):
                pe.wait_ge(w_loaded, 16)
                pe.sem_inc(product, 2)

                def multiply(b, s, use, tiles, columns):
                    pe.wait_ge(used, b + 1)
                    pe.wait_ge(made, b + 1)
                    for c, at, n in halves(columns):
                        last = pe.matmul(ps[s][:, c, 0:n], w_sb[:, :], hidden[:, s, at:at + n], start=True, stop=True)
                    last.then_inc(product, 1)
                over_blocks(pe, multiply)

            @block.vector
            def _(dve):
                dve.sem_inc(used, 2)

                def take(b, s, use, tiles, columns):
                    dve.wait_ge(product, b + 3)
                    alone(dve)
                    for c, at, n in halves(columns):
                        dve.bn_stats(stats[:, bass.ds(2 * b + c, 1), :].rearrange("p a b -> p (a b)"), ps[s][:, c, 0:n])
                    dve.tensor_scalar(feat_block(feat, b, columns), banks(ps[s], columns), vecs[:, bias:bias + 1], None,
                                      ALU.add).then_inc(used, 1)
                over_blocks(dve, take)
                dve.wait_ge(used, 2 + BLOCKS + 1)
                batch_scale(dve, root, var, Chain(dve, vec, 0, 5), stats[:, :, :].rearrange("p a b -> p (a b)"), mv, scale, vecs, gamma, beta, bias)


def write_table(nc, feat, scale, ident, table):
    with ExitStack() as ctx:
        new = ctx.enter_context(sbuf(nc, "new", [P, 2, BLOCK], F32))
        rows = ctx.enter_context(sbuf(nc, "rows", [P, 2, T, C], F32))
        ps = [ctx.enter_context(psum(nc, f"ps_turn{s}", [P, 2, BANK], F32)) for s in range(2)]
        with phase(nc, "made kept turned rows_made written0 written1") as \
                (block, made, kept, turned, rows_made, written0, written1):
            written = (written0, written1)

            @block.scalar
            def _(act):
                def make(b, s, use, tiles, columns):
                    act.wait_ge(turned, b + 1)
                    act.wait_ge(kept, b + 1)
                    alone(act)
                    act.activation(new[:, s, 0:columns], feat[:, bass.ds(b * BLOCK, columns)], ACT.Relu,
                                   bias=scale[:, 1:2], scale=scale[:, 0:1]).then_inc(made, 1)
                over_blocks(act, make)

            @block.gpsimd
            def _(pool):
                pool.sem_inc(kept, 2)

                def copy(b, s, use, tiles, columns):
                    pool.wait_ge(made, b + 1)
                    alone(pool)
                    pool.tensor_copy(feat[:, bass.ds(b * BLOCK, columns)], new[:, s, 0:columns]).then_inc(kept, 1)
                over_blocks(pool, copy)

            @block.tensor
            def _(pe):
                pe.sem_inc(turned, 2)

                def turn(b, s, use, tiles, columns):
                    pe.wait_ge(rows_made, b + 1)
                    pe.wait_ge(made, b + 1)
                    n = P if columns == BLOCK else columns
                    for j in range(tiles):
                        last = pe.transpose(tile_in_banks(ps[s], j, n, P), new[:, s, j * P:j * P + n], ident[:, :])
                    last.then_inc(turned, 1)
                over_blocks(pe, turn)

            @block.vector
            def _(dve):
                dve.sem_inc(rows_made, 2)

                def store(b, s, use, tiles, columns):
                    dve.wait_ge(turned, b + 3)
                    if not first(b):
                        dve.wait_ge(written[s], use * 16)
                    rows_of(dve.tensor_copy, rows, s, ps[s], columns).then_inc(rows_made, 1)
                over_blocks(dve, store)

            @block.sync
            def _(sp):
                def write(b, s, use, tiles, columns):
                    sp.wait_ge(rows_made, b + 3)
                    alone(sp)
                    sp.dma_start(node_block(table, b, columns), node_slot(rows, s, columns)).then_inc(written[s], 16)
                over_blocks(sp, write)
                for s in range(2):
                    sp.wait_ge(written[s], 16 * (PAIRS + 1))


def rows_of(copy, rows, s, ps, columns):
    if columns == BLOCK:
        return copy(rows[:, s, :, :].rearrange("p (a j) c -> p a (j c)", a=2), ps[:, :, 0:HALF])
    return copy(rows[0:columns, s, 0, :], ps[0:columns, 0, 0:C])


def layer_norm(nc, feat, scale, ident, skip, out, also):
    with ExitStack() as ctx:
        sb = lambda name, shape, dt=F32: ctx.enter_context(sbuf(nc, name, shape, dt))
        normed = sb("normed", [P, 2, BLOCK])
        rows = sb("rows", [P, 2, T, C])
        stats = sb("row_stats", [P, T, 6])
        mv = sb("row_mv", [P, T, 2])
        root, rec = sb("row_root", [P, T]), sb("row_rec", [P, T])
        ps = [ctx.enter_context(psum(nc, f"ps_turn{s}", [P, 2, BANK], F32)) for s in range(2)]
        back = [ctx.enter_context(psum(nc, f"ps_back{s}", [P, 2, BANK], F32)) for s in range(2)]
        stores = 2 if also is not None else 1
        with phase(nc, "made turned loaded0 loaded1 summed var_made root_made rows_made turned_back feat_stored written0 written1 vec") as \
                (block, made, turned, loaded0, loaded1, summed, var_made, root_made, rows_made, turned_back,
                 feat_stored, written0, written1, vec):
            loaded, written = (loaded0, loaded1), (written0, written1)

            @block.sync
            def _(sp):
                def load(b, s, use, tiles, columns):
                    if not first(b):
                        sp.wait_ge(written[s], use * 16 * stores)
                        alone(sp)
                    if also is not None:
                        sp.wait_ge(turned_back, b + 1)
                        alone(sp)
                    sp.dma_start(node_slot(rows, s, columns), node_block(skip, b, columns)).then_inc(loaded[s], 16)
                over_blocks(sp, load)

            @block.scalar
            def _(act):
                act.sem_inc(feat_stored, 2)

                def make(b, s, use, tiles, columns):
                    act.wait_ge(turned, b + 1)
                    alone(act)
                    act.activation(normed[:, s, 0:columns], feat[:, bass.ds(b * BLOCK, columns)], ACT.Identity,
                                   bias=scale[:, 1:2], scale=scale[:, 0:1]).then_inc(made, 1)
                    act.wait_ge(var_made, b + 1)
                    act.activation(root[:, 0:tiles], mv[:, 0:tiles, 1], ACT.Sqrt).then_inc(root_made, 1)
                    if also is not None:
                        act.wait_ge(turned_back, b + 3)
                        alone(act)
                        act.activation(feat_block(feat, b, columns), banks(back[s], columns), ACT.Copy).then_inc(feat_stored, 1)
                over_blocks(act, make)

            @block.tensor
            def _(pe):
                pe.sem_inc(turned, 2)
                pe.sem_inc(turned_back, 2)

                def turn(b, s, use, tiles, columns):
                    pe.wait_ge(summed, b + 1)
                    pe.wait_ge(made, b + 1)
                    n = P if columns == BLOCK else columns
                    for j in range(tiles):
                        last = pe.transpose(tile_in_banks(ps[s], j, n, P), normed[:, s, j * P:j * P + n], ident[:, :])
                    last.then_inc(turned, 1)
                    if also is not None:
                        pe.wait_ge(feat_stored, b + 1)
                        pe.wait_ge(rows_made, b + 1)
                        for j in range(tiles):
                            last = pe.transpose(tile_in_banks(back[s], j, P, n), rows[0:n, s, j, :], ident[0:n, 0:n])
                        last.then_inc(turned_back, 1)
                over_blocks(pe, turn)

            @block.vector
            def _(dve):
                dve.sem_inc(summed, 2)

                def norm(b, s, use, tiles, columns):
                    n = P if columns == BLOCK else columns
                    ch = Chain(dve, vec, b, 4)
                    dve.wait_ge(loaded[s], use * 16 + 16)
                    dve.wait_ge(turned, b + 3)
                    add = lambda o, i: dve.tensor_tensor(o, o, i, ALU.add)
                    rows_of(add, rows, s, ps[s], columns).then_inc(summed, 1)
                    dve.wait_ge(summed, b + 3)
                    for j in range(tiles):
                        last = dve.bn_stats(stats[0:n, j, :], rows[0:n, s, j, :])
                    ch.then(last)
                    alone(dve)
                    for j in range(tiles):
                        last = dve.bn_aggr(mv[0:n, j, :], stats[0:n, j, :])
                    ch.then(last)
                    dve.tensor_scalar(mv[0:n, 0:tiles, 1], mv[0:n, 0:tiles, 1], EPS, None, ALU.add).then_inc(var_made, 1)
                    dve.wait_ge(root_made, b + 1)
                    ch.then(dve.reciprocal(rec[0:n, 0:tiles], root[0:n, 0:tiles]))
                    for j in range(tiles):
                        last = dve.tensor_scalar(rows[0:n, s, j, :], rows[0:n, s, j, :], mv[0:n, j, 0:1], rec[0:n, j:j + 1],
                                                 ALU.subtract, ALU.mult)
                    ch.then(last)
                    dve.sem_inc(rows_made, 1)
                    ch.end()
                over_blocks(dve, norm)

            @block.gpsimd
            def _(pool):
                def write(b, s, use, tiles, columns):
                    pool.wait_ge(rows_made, b + 1)
                    alone(pool)
                    pool.dma_start(node_block(out, b, columns), node_slot(rows, s, columns)).then_inc(written[s], 16)
                    if also is not None:
                        pool.dma_start(node_block(also, b, columns), node_slot(rows, s, columns)).then_inc(written[s], 16)
                over_blocks(pool, write)
                for s in range(2):
                    pool.wait_ge(written[s], 16 * stores * (PAIRS + 1))


def kernel(**inputs):
    import numpy as _np
    import concourse.bacc as _bacc
    from concourse import mybir as _mybir
    from concourse.bass_utils import run_bass_kernel_spmd as _run

    get = lambda name: _np.asarray(inputs[name])
    both = _np.concatenate([get("L0_gnn_W_f"), get("L0_gnn_W_s")], axis=0).T
    biases = _np.concatenate([get("L0_gnn_b_f"), get("L0_gnn_b_s")])[None, :]
    vectors = [get("L0_gnn_gamma"), get("L0_gnn_beta")]
    for l in range(LAYERS):
        vectors += [get(f"L1_gnn_{n}")[l] for n in ("b1", "g_mlp", "be_mlp", "b2", "g_out", "be_out")]
    arrays = {
        "x": get("x"), "x_t": get("x").T, "src": get("src"), "dst": get("dst"),
        "edge128": get("edge_attr_128"), "edge64": get("edge_attr_64"), "edge64_t": get("edge_attr_64").T,
        "w_src": both[C:2 * C], "w_dst": both[0:C], "w_edge": _np.concatenate([both[2 * C:], biases], axis=0),
        "vectors": _np.stack(vectors, axis=1), "w1": get("L1_gnn_W1"), "w2": get("L1_gnn_W2"),
    }
    arrays = {f"in_{k}": _np.ascontiguousarray(v) for k, v in arrays.items()}
    nc = _bacc.Bacc("TRN2", target_bir_lowering=False, num_devices=1, dynamic_dma_scratch_size=8192)
    args = [nc.dram_tensor(k, v.shape, _mybir.dt.from_np(v.dtype), kind="ExternalInput").ap() for k, v in arrays.items()]
    out = nc.dram_tensor("out", [N, C], F32, kind="ExternalOutput").ap()
    gnn_kernel(nc, *args, out)
    r = _run(nc, [arrays], core_ids=[0])
    return r.results[0]["out"]
```

```python
import concourse.bass as bass
from concourse import mybir
from contextlib import ExitStack, contextmanager

F32 = mybir.dt.float32
I32 = mybir.dt.int32
I16 = mybir.dt.int16
U16 = mybir.dt.uint16
ALU = mybir.AluOpType
ACT = mybir.ActivationFunctionType

P = 128
N = 50000
E = 50000
C = 128
D0 = 64
LAYERS = 3
EPS = 1e-5
T = 6
BLOCK = T * P
HALF = BLOCK // 2
BLOCKS = N // BLOCK
PAIRS = BLOCKS // 2
TILES = N // P
TAIL = N - TILES * P
COLUMNS = (BLOCKS + 1) * T
CHUNKS = 2 * BLOCKS + 1
BANK = 512
AGG = C + 4
AGG_ROWS = N + P

WINDOWS = [(0, 192), (68, 272), (172, 312), (280, 348), (392, 376), (512, 400)]
SPAN = 912
WIDEST = max(w for _, w in WINDOWS)
NODES = N + 336
LN_EXP_TABLE = 6
NEAR = 44
LAG = 3

assert all(first + width <= SPAN <= 2 * BANK for first, width in WINDOWS)
assert N <= 1 << 16
assert NEAR % 4 == 0 and NEAR >= 8
assert N == E and N == BLOCKS * BLOCK + TAIL and BLOCKS % 2 == 1 and TILES == BLOCKS * T


def sbuf(nc, name, shape, dt):
    return nc.sbuf_tensor(f"{name}_{nc.next_id()}", shape, dt)


def psum(nc, name, shape, dt):
    return nc.psum_tensor(f"{name}_{nc.next_id()}", shape, dt)


class Taken:

    def __init__(self, block, flag, want):
        self.block, self.flag, self.want = block, flag, want

    def _under(self, place):
        def wrap(program):
            def guarded(eng):
                with eng.If(eng.value_load(self.flag[0:1, 0:1], min_val=0, max_val=1) == self.want):
                    program(eng)
            place(guarded)
            return program
        return wrap

    sync = property(lambda self: self._under(self.block.sync))
    gpsimd = property(lambda self: self._under(self.block.gpsimd))
    scalar = property(lambda self: self._under(self.block.scalar))
    vector = property(lambda self: self._under(self.block.vector))
    tensor = property(lambda self: self._under(self.block.tensor))


@contextmanager
def phase(nc, names, when=None):
    sems = [nc.alloc_semaphore(f"{n}_{nc.next_id()}") for n in names.split()]
    with nc.Block() as block:
        yield (Taken(block, *when) if when else block, *sems)
    nc.clear_and_free_semaphores(sems)
    nc.all_engine_barrier()


class Chain:

    def __init__(self, eng, sem, at, per):
        self.eng, self.sem, self.base, self.per, self.n = eng, sem, at * per, per, 0

    def mark(self, instruction):
        instruction.then_inc(self.sem, 1)
        self.n += 1

    def wait(self):
        self.eng.wait_ge(self.sem, self.base + self.n)

    def then(self, instruction):
        self.mark(instruction)
        self.wait()

    def end(self):
        assert self.n == self.per, (self.n, self.per)


def alone(eng):
    eng.nop(nofuse=True)


def over_blocks(eng, body, ahead=1):
    for pair in range(ahead):
        body(2 * pair, 0, pair, T, BLOCK)
        body(2 * pair + 1, 1, pair, T, BLOCK)
    with eng.Fori(ahead, PAIRS) as pair:
        body(2 * pair, 0, pair, T, BLOCK)
        body(2 * pair + 1, 1, pair, T, BLOCK)
    body(BLOCKS - 1, 0, PAIRS, T, BLOCK)
    body(BLOCKS, 1, PAIRS, 1, TAIL)


def over_blocks_by_four(eng, body, start=0):
    for b in range(start, start + 4):
        body(b, b % 4, 0, T, BLOCK)
    with eng.Fori(1, (BLOCKS - start) // 4) as turn:
        for q in range(4):
            body(4 * turn + (start + q), q, turn, T, BLOCK)
    for b in range(BLOCKS // 4 * 4, BLOCKS + 1):
        body(b, b % 4, (b - start) // 4, *((T, BLOCK) if b < BLOCKS else (1, TAIL)))


def over_near_and_far(eng, body):
    def pair(k, near):
        body(2 * k, 0, k, T, BLOCK, near)
        body(2 * k + 1, 1, k, T, BLOCK, near)
    pair(0, None)
    pair(1, None)
    with eng.Fori(2, NEAR // 2) as k:
        pair(k, True)
    pair(NEAR // 2, None)
    pair(NEAR // 2 + 1, None)
    with eng.Fori(NEAR // 2 + 2, PAIRS) as k:
        pair(k, False)
    body(BLOCKS - 1, 0, PAIRS, T, BLOCK, None)
    body(BLOCKS, 1, PAIRS, 1, TAIL, None)


def over_tiles(eng, body):
    with eng.Fori(0, TILES) as tile:
        body(tile, P)
    body(TILES, TAIL)


def first(b):
    return isinstance(b, int) and b < 2


def halves(columns):
    return [(0, 0, HALF), (1, HALF, HALF)] if columns == BLOCK else [(0, 0, columns)]


def feat_block(feat, b, columns):
    v = feat[:, bass.ds(b * BLOCK, columns)]
    return v.rearrange("p (a c) -> p a c", a=2) if columns == BLOCK else v


def banks(ps, columns):
    return ps[:, :, 0:HALF] if columns == BLOCK else ps[:, 0, 0:columns]


def tile_in_banks(ps, j, rows, width):
    return ps[0:rows, j // 3, (j % 3) * P:(j % 3) * P + width]


def node_block(dram, b, columns):
    rows = dram[bass.ds(b * BLOCK, columns), :]
    return rows.rearrange("(t p) c -> p t c", p=P) if columns == BLOCK else rows


def node_slot(buf, s, columns):
    return buf[:, s, :, :] if columns == BLOCK else buf[0:columns, s, 0, :]


def gnn_kernel(nc, x, x_t, src, dst, edge128, edge64, edge64_t, w_src, w_dst, w_edge, vectors, w1, w2, out):
    ctx = ExitStack()
    with ctx:
        keep = lambda name, shape, dt=F32: ctx.enter_context(sbuf(nc, name, shape, dt))
        ident = keep("ident", [P, P])
        src_ix = keep("src_ix", [P, COLUMNS], U16)
        dst_ix = keep("dst_ix", [P, COLUMNS], U16)
        place = keep("place", [P, COLUMNS], I16)
        base = keep("base", [1, BLOCKS + 1], I32)
        flag = keep("flag", [1, 1], I32)
        vecs = keep("vecs", [P, vectors.shape[1]])
        scale = keep("scale", [P, 2])
        tables = [nc.dram_tensor(f"table{l}", [N, C], F32).ap() for l in range(LAYERS)]
        agg0 = nc.dram_tensor("agg0", [AGG_ROWS, AGG], F32).ap()
        spans = nc.dram_tensor("spans", [BLOCKS + 1, P, SPAN], F32).ap()
        agg1 = nc.dram_tensor("agg1", [AGG_ROWS, C], F32).ap()

        GAMMA0, BETA0 = 0, 1
        B1, GM, BM, B2, GO, BO = (lambda l, k=k: 2 + 6 * l + k for k in range(6))

        load_constants(nc, src, dst, vectors, ident, src_ix, dst_ix, vecs, place, base, flag)
        gates = (w_src, w_dst, w_edge)
        scatter_messages(nc, x, edge64, gates, ident, src_ix, dst_ix, agg0, (flag, 0))
        feat = keep("feat", [P, NODES])
        gated_messages(nc, x, x_t, dst, edge64_t, gates, ident, src_ix, dst_ix, place, base, feat, spans, (flag, 1))
        assemble(nc, x_t, spans, base, feat, vecs, scale, GAMMA0, BETA0, (flag, 1))
        load_nodes(nc, x_t, feat, (flag, 0))
        add_sums(nc, agg0, feat, ident, True, (flag, 0))
        norm_stats(nc, feat, vecs, scale, GAMMA0, BETA0, (flag, 0))
        layer_norm(nc, feat, scale, ident, x_t, tables[0], True)
        for l in range(LAYERS):
            last = l == LAYERS - 1
            sorted_messages(nc, tables[l], edge128, src_ix, place, base, w1[l], feat, vecs, scale,
                            B1(l), GM(l), BM(l), (flag, 1))
            scatter_messages(nc, tables[l], edge128, None, ident, src_ix, dst_ix, agg1, (flag, 0))
            add_sums(nc, agg1, feat, ident, False, (flag, 0))
            first_product(nc, w1[l], feat, vecs, scale, B1(l), GM(l), BM(l), (flag, 0))
            second_product(nc, w2[l], feat, vecs, scale, B2(l), GO(l), BO(l))
            if not last:
                write_table(nc, feat, scale, ident, tables[l + 1])
        layer_norm(nc, feat, scale, ident, tables[0], out, False)


def load_constants(nc, src, dst, vectors, ident, src_ix, dst_ix, vecs, place, base, flag):
    groups = [(g, min(P, TILES - g)) for g in range(0, TILES, P)]
    G = len(groups) + 1
    NB = BLOCKS + 1
    with ExitStack() as ctx:
        sb = lambda name, shape, dt=F32: ctx.enter_context(sbuf(nc, name, shape, dt))
        raw, rawf = sb("raw", [P, 3, G, P], I32), sb("rawf", [P, 3, G, P])
        dst_f, bad_t, bad = sb("dst_f", [P, TILES + 1]), sb("bad_t", [P, 6 * P]), sb("bad", [P, 16])
        place_f = sb("place_f", [P, TILES + 1])
        ones, row, spans = sb("ones", [P, P]), sb("row", [1, 2 * NB]), sb("spans", [P, NB])
        base_f = sb("base_f", [1, NB])
        block_ix = sb("block_ix", [1, NB], I32)
        ps = ctx.enter_context(psum(nc, "ps_ix", [P, 2, BANK], F32))
        ps_b = ctx.enter_context(psum(nc, "ps_base", [P, BANK], F32))
        ps_f = ctx.enter_context(psum(nc, "ps_bad", [P, BANK], F32))
        with phase(nc, "zeroed ones_done loaded rawf_done turned copied bases_out bads bads_summed vec") as \
                (block, zeroed, ones_done, loaded, rawf_done, turned, copied, bases_out, bads, bads_summed, vec):
            loads = 3 * G + 1

            @block.sync
            def _(sp):
                sp.wait_ge(zeroed, 1)
                for k, (a, off) in enumerate(((src, 0), (dst, 0), (dst, 1))):
                    for g, (first_tile, tiles) in enumerate(groups):
                        at = first_tile * P + off
                        sp.dma_start(raw[0:tiles, k, g, :],
                                     a[at:at + tiles * P].rearrange("(t p) -> t p", p=P)).then_inc(loaded, 16)
                    sp.dma_start(raw[0:1, k, G - 1, 0:TAIL - off],
                                 a[TILES * P + off:N].rearrange("(a p) -> a p", a=1)).then_inc(loaded, 16)
                sp.dma_start(vecs[:, :], vectors).then_inc(loaded, 16)
                sp.wait_ge(loaded, 16 * loads)

            @block.gpsimd
            def _(pool):
                pool.memset(ident[:, :], 0.0).then_inc(ones_done, 1)
                pool.memset(ones[:, :], 1.0).then_inc(ones_done, 1)
                pool.iota(block_ix[:, :], [[BLOCK, NB]], base=0, channel_multiplier=0).then_inc(ones_done, 1)
                pool.wait_ge(ones_done, 3)
                pool.affine_select(out=ident[:, :], in_=ident[:, :], compare_op=ALU.not_equal, fill=1.0,
                                   base=0, pattern=[[-1, P]], channel_multiplier=1).then_inc(ones_done, 1)

            @block.vector
            def _(dve):
                dve.memset(bad[:, :], 0.0)
                for ix in (src_ix, dst_ix, place):
                    dve.memset(ix[:, TILES + 1:COLUMNS], 0)
                dve.memset(raw[:, :, :, :], 0).then_inc(zeroed, 1)
                ch = Chain(dve, vec, 0, 32)
                dve.wait_ge(loaded, 16 * loads)
                dve.wait_ge(zeroed, 1)
                dve.tensor_copy(rawf[:, :, :, :], raw[:, :, :, :]).then_inc(rawf_done, 1)
                dve.wait_ge(rawf_done, 1)
                for g in range(G):
                    tiles, n = (groups[g][1], P) if g < G - 1 else (1, TAIL - 1)
                    ch.then(dve.tensor_tensor(bad_t[0:tiles, 0:n], rawf[0:tiles, 1, g, 0:n], rawf[0:tiles, 2, g, 0:n], ALU.is_gt))
                    ch.then(dve.reduce_sum(bad[0:tiles, g:g + 1], bad_t[0:tiles, 0:n], axis=mybir.AxisListType.X))
                dve.wait_ge(turned, 1)
                dve.tensor_copy(src_ix[:, 0:TILES + 1], ps[:, 0, 0:TILES + 1])
                dve.tensor_copy(dst_ix[:, 0:TILES + 1], ps[:, 1, 0:TILES + 1])
                dve.tensor_copy(dst_f[:, :], ps[:, 1, 0:TILES + 1]).then_inc(copied, 1)
                dve.wait_ge(copied, 1)
                ch.then(dve.tensor_tensor(bad_t[:, 0:TILES - 1], dst_f[:, 1:TILES], dst_f[:, 0:TILES - 1], ALU.is_le))
                ch.then(dve.reduce_sum(bad[:, 4:5], bad_t[:, 0:TILES - 1], axis=mybir.AxisListType.X))
                ch.then(dve.tensor_tensor(bad[0:TAIL, 5:6], dst_f[0:TAIL, TILES:TILES + 1], dst_f[0:TAIL, TILES - 1:TILES], ALU.is_le))
                dve.wait_ge(bases_out, 1)
                ch.then(dve.tensor_copy(spans[:, :], ps_b[:, 0:NB]))
                dve.tensor_copy(base[:, :], spans[0:1, :])
                ch.then(dve.tensor_copy(base_f[:, :], spans[0:1, :]))
                for j, (at, width) in enumerate(WINDOWS):
                    nb = NB if j == 0 else NB - 1
                    here = place_f[:, j:TILES + 1:T]
                    ch.then(dve.scalar_tensor_tensor(out=here, in0=dst_f[:, j:TILES + 1:T], scalar=float(-at), in1=spans[:, 0:nb],
                                                     op0=ALU.add, op1=ALU.subtract))
                dve.tensor_copy(place[:, 0:TILES + 1], place_f[:, :])
                ch.then(dve.tensor_scalar(bad_t[:, 0:TILES], place_f[:, 0:TILES], 0.0, None, ALU.is_lt))
                ch.then(dve.reduce_sum(bad[:, 6:7], bad_t[:, 0:TILES], axis=mybir.AxisListType.X))
                ch.then(dve.tensor_scalar(bad[0:TAIL, 7:8], place_f[0:TAIL, TILES:TILES + 1], 0.0, None, ALU.is_lt))
                for j, (at, width) in enumerate(WINDOWS):
                    dve.tensor_scalar(bad_t[:, j * P:j * P + BLOCKS], place_f[:, j:TILES:T], float(width), None, ALU.is_ge)
                ch.then(dve.tensor_scalar(bad[0:TAIL, 8:9], place_f[0:TAIL, TILES:TILES + 1], float(WINDOWS[0][1]), None, ALU.is_ge))
                ch.then(dve.reduce_sum(bad[:, 9:10], bad_t[:, :].rearrange("p (j b) -> p j b", j=6)[:, :, 0:BLOCKS], axis=mybir.AxisListType.XY))
                dve.wait_ge(ones_done, 3)
                ch.then(dve.tensor_tensor(row[:, 0:NB], base_f[:, :], block_ix[:, :], ALU.subtract))
                dve.tensor_scalar(row[:, NB:2 * NB], row[:, 0:NB], float(BLOCK), None, ALU.is_gt)
                ch.then(dve.tensor_scalar(row[:, 0:NB], row[:, 0:NB], float(-BLOCK), None, ALU.is_lt))
                ch.then(dve.reduce_sum(bad[0:1, 10:11], row[:, :], axis=mybir.AxisListType.X))
                ch.mark(dve.tensor_scalar(bad[0:1, 11:12], base_f[:, BLOCKS - 1:BLOCKS], float(NODES - SPAN), None, ALU.is_gt))
                ch.wait()
                dve.sem_inc(bads, 1)
                dve.wait_ge(bads_summed, 1)
                ch.then(dve.reduce_sum(row[:, 0:1], ps_f[0:1, 0:16], axis=mybir.AxisListType.X))
                ch.then(dve.tensor_scalar(flag[:, :], row[:, 0:1], 0.0, None, ALU.is_equal))
                ch.end()

            @block.tensor
            def _(pe):
                pe.wait_ge(rawf_done, 1)
                pe.wait_ge(ones_done, 4)
                for k in range(2):
                    for g, (first_tile, tiles) in enumerate(groups + [(TILES, 1)]):
                        last = pe.transpose(ps[:, k, first_tile:first_tile + tiles], rawf[0:tiles, k, g, :], ident[0:tiles, 0:tiles])
                last.then_inc(turned, 1)
                pe.wait_ge(copied, 1)
                pe.matmul(ps_b[:, 0:NB], ones[0:1, :], dst_f[0:1, 0:TILES + 1:T], start=True, stop=True).then_inc(bases_out, 1)
                pe.wait_ge(bads, 1)
                pe.matmul(ps_f[:, 0:16], ones[:, :], bad[:, :], start=True, stop=True).then_inc(bads_summed, 1)


def gated_messages(nc, x, x_t, dst, edge_t, gates, ident, src_ix, dst_ix, place, base, feat, spans, when):
    with ExitStack() as ctx:
        sb = lambda name, shape, dt=F32: ctx.enter_context(sbuf(nc, name, shape, dt))
        free = (NEAR + 2) * BLOCK

        def carve(*shape, dt=F32):
            nonlocal free
            size = 1
            for k in shape:
                size *= k
            v = feat[:, free:free + size]
            free += size
            assert free <= NODES
            v = v if dt == F32 else v.bitcast(dt)
            letters = "abcd"[:len(shape)]
            return v.rearrange(f"p ({' '.join(letters)}) -> p {' '.join(letters)}", **dict(zip(letters, shape)))

        weights = sb("gate_w", [P, 3, 2 * C])
        ends = carve(4, 3, 2, C)
        turned_ends = carve(2, 3, 2, P)
        edge = carve(2, BLOCK)
        dst_row = carve(2, BLOCK + 2 * P, dt=I32)
        equal = carve(3, 3 * P)
        logs_, exponent, value, msg = carve(2, 3, 2, C), carve(2, 3, C), carve(2, 3, C), carve(2, 3, C)
        span_out = carve(2, SPAN)
        match = sb("match", [P, 2, 3, WIDEST])
        count = sb("count", [P, WIDEST], I16)
        src_here, dst_here = sb("src_here", [P, 2, T], I32), sb("dst_here", [P, 2, T], I32)
        dst_f, place_f, share = sb("dst_f", [P, 2, T]), sb("place_f", [P, 2, T]), sb("share", [P, 2, T])
        ps_t = ctx.enter_context(psum(nc, "ps_ends", [P, 2 * BANK], F32))
        ps_z = [ctx.enter_context(psum(nc, f"ps_z{s}", [P, 2 * BANK], F32)) for s in range(2)]
        ps_span = ctx.enter_context(psum(nc, "ps_span", [P, 2 * BANK], F32))
        names = ("nodes0 nodes1 joined w_loaded counted ready indexed placed gathered0 gathered1 gathered2 gathered3 edge0 edge1 row0 row1 turned "
                 "evacuated product logs exponents values gated made matched used copied written0 written1 act_chain counted_edges")
        with phase(nc, names, when) as (block, n0, n1, joined, w_loaded, counted, ready, indexed, placed, g0, g1, g2, g3, e0, e1, r0, r1, turned,
                                        evacuated, product, logs, exponents, values, gated, made, matched, used, copied,
                                        wr0, wr1, act_chain, counted_edges):
            gathered, edge_loaded, row_loaded, written = (g0, g1, g2, g3), (e0, e1), (r0, r1), (wr0, wr1)
            nodes_loaded = (n0, n1)

            def is_near(b, lag, near):
                return b - lag < NEAR if isinstance(b, int) else near

            def units(b, s, tiles):
                return [(h, 2 * b + h, 2 * s + h, 3, P) for h in range(2)] if tiles == T else [(0, 2 * b, 2 * s, 1, TAIL)]

            def before(b, h, s):
                return (b, 0, s) if h else (b - 1, 1, 1 - s)

            def from_(n, k):
                return not isinstance(n, int) or n >= k

            @block.sync
            def _(sp):
                sp.dma_start(weights[:, 0, :], gates[0]).then_inc(w_loaded, 16)
                sp.dma_start(weights[:, 1, :], gates[1]).then_inc(w_loaded, 16)
                sp.dma_start(weights[0:D0 + 1, 2, :], gates[2]).then_inc(w_loaded, 16)

                def store(b, s, width):
                    sp.wait_ge(copied, b + 1)
                    alone(sp)
                    sp.dma_start(spans[bass.ds(b, 1), :, 0:width].rearrange("a p c -> (a p) c"), span_out[:, s, 0:width]).then_inc(written[s], 16)

                def nodes(b, s):
                    sp.dma_start(feat[:, bass.ds(b * BLOCK, BLOCK)], x_t[:, bass.ds(b * BLOCK, BLOCK)]).then_inc(nodes_loaded[s], 16)

                def load(b, s, use, tiles, columns, near_):
                    if from_(b, 2):
                        sp.wait_ge(product, 2 * b - 2)
                        alone(sp)
                        sp.wait_ge(counted_edges, 4 * b - 4)
                        alone(sp)
                    sp.dma_start(edge[0:D0, s, 0:columns], edge_t[:, bass.ds(b * BLOCK, columns)]).then_inc(edge_loaded[s], 16)
                    first_col = P if isinstance(b, int) and b == 0 else 0
                    last_col = min(BLOCK + 2 * P, N - (b * BLOCK - P)) if isinstance(b, int) else BLOCK + 2 * P
                    sp.dma_start(dst_row[:, s, first_col:last_col],
                                 dst[bass.ds(b * BLOCK + first_col - P, last_col - first_col)].partition_broadcast(P)).then_inc(row_loaded[s], 16)
                    if is_near(b, 0, near_):
                        sp.wait_ge(nodes_loaded[s], use * 16 + 16)
                        alone(sp)
                        nodes(b + 2, s)
                    if not is_near(b, 3, near_):
                        store(b - 3, 1 - s, SPAN)
                nodes(0, 0)
                nodes(1, 1)
                over_near_and_far(sp, load)
                store(BLOCKS - 2, 1, SPAN)
                store(BLOCKS - 1, 0, SPAN)
                store(BLOCKS, 1, WINDOWS[0][1])
                for s in range(2):
                    sp.wait_ge(written[s], 16 * (PAIRS + 1 - NEAR // 2))

            @block.gpsimd
            def _(pool):
                pool.iota(count[:, :], [[1, WIDEST]], base=0, channel_multiplier=0).then_inc(counted, 1)

                def gather(b, s, use, tiles, columns):
                    pool.wait_ge(indexed, b + 1)
                    alone(pool)
                    for h, u, q, k, n in units(b, s, tiles):
                        if from_(u, 4):
                            pool.wait_ge(turned, u - 3)
                            alone(pool)
                        for j in range(k):
                            for e, ix in enumerate((src_here, dst_here)):
                                pool.indirect_dma_start(ends[0:n, q, j, e, :], None, x, bass.IndirectOffsetOnAxis(
                                    ap=ix[0:n, s, 3 * h + j:3 * h + j + 1], axis=0)).then_inc(gathered[q], 16)
                over_blocks(pool, gather, 2)

            @block.tensor
            def _(pe):
                pe.wait_ge(w_loaded, 48)
                pe.wait_ge(ready, 2)

                def sum_up(b, h, k, n):
                    u = 2 * b + h
                    if h == 0 and from_(b, 1):
                        pe.wait_ge(copied, b)
                    pe.wait_ge(made, u + 1)
                    pe.wait_ge(matched, u + 1)
                    for j in range(3 * h, 3 * h + k):
                        first_col, width = WINDOWS[j]
                        for lo, hi in bank_parts(first_col, width):
                            last = pe.matmul(ps_span[:, lo:hi], msg[0:n, h, j % 3, :],
                                             match[0:n, h, j % 3, lo - first_col:hi - first_col],
                                             start=j == 0 or (j == 3 and lo >= BANK), stop=True, skip_group_check=True)
                    last.then_inc(used, 1)

                def step(b, s, use, tiles, columns):
                    for h, u, q, k, n in units(b, s, tiles):
                        pe.wait_ge(gathered[q], use * 96 + 32 * k)
                        if from_(u, 1):
                            pe.wait_ge(evacuated, u)
                        for j in range(k):
                            for e in range(2):
                                last = pe.transpose(ps_t[:, (2 * j + e) * P:(2 * j + e) * P + n], ends[0:n, q, j, e, :], ident[0:n, 0:n])
                        last.then_inc(turned, 1)
                        if from_(b, 1):
                            sum_up(b - 1, h, 3, P)
                        pe.wait_ge(evacuated, u + 1)
                        pe.wait_ge(edge_loaded[s], use * 16 + 16)
                        if from_(u, 2):
                            pe.wait_ge(values, u - 1)
                        for j in range(k):
                            z = ps_z[h][0:n, j * 2 * C:(j + 1) * 2 * C]
                            pe.matmul(z, turned_ends[:, h, j, 0, 0:n], weights[:, 0, :], start=True, stop=False)
                            pe.matmul(z, turned_ends[:, h, j, 1, 0:n], weights[:, 1, :], start=False, stop=False)
                            at = (3 * h + j) * P
                            last = pe.matmul(z, edge[0:D0 + 1, s, at:at + n], weights[0:D0 + 1, 2, :], start=False, stop=True)
                        last.then_inc(product, 1)
                over_blocks(pe, step, 2)
                sum_up(BLOCKS - 1, 1, 3, P)
                sum_up(BLOCKS, 0, 1, TAIL)

            def z_part(h, k, n, part):
                return ps_z[h][0:n, 0:2 * C * k].rearrange("p (j e c) -> p j e c", e=2, c=C)[:, :, part, :]

            @block.scalar
            def _(act):
                act.add_instruction(mybir.InstLoadActFuncSet(
                    name=f"I-{nc.next_id()}", act_func_set_id=LN_EXP_TABLE, engine=mybir.EngineType.Activation, ins=[], outs=[]))

                def copy_span(b, s, use, width, near_=None):
                    act.wait_ge(used, min(2 * b + 2, 2 * BLOCKS + 1) if isinstance(b, int) else 2 * b + 2)
                    alone(act)
                    if not is_near(b, 2, near_):
                        act.wait_ge(written[s], (use - NEAR // 2) * 16)
                    elif from_(b, 2):
                        act.wait_ge(joined, b - 1)
                    act.activation(span_out[:, s, 0:width], ps_span[:, 0:width], ACT.Copy).then_inc(copied, 1)

                def gate(b, h, k, n):
                    u = 2 * b + h
                    act.wait_ge(product, u + 1)
                    if from_(u, 2):
                        act.wait_ge(values, u - 1)
                    e = logs_[0:n, h, 0:k, :, :].rearrange("p j e c -> p (j e c)")
                    act.activation(e, ps_z[h][0:n, 0:2 * C * k], ACT.Abs).then_inc(act_chain, 1)
                    act.wait_ge(act_chain, 2 * u + 1)
                    act.activation(e, e, ACT.Exp, scale=-1.0).then_inc(act_chain, 1)
                    act.wait_ge(act_chain, 2 * u + 2)
                    act.activation(e, e, ACT.Ln, bias=1.0).then_inc(logs, 1)
                    act.wait_ge(exponents, u + 1)
                    act.activation(exponent[0:n, h, 0:k, :], exponent[0:n, h, 0:k, :], ACT.Exp).then_inc(gated, 1)

                def step(b, s, use, tiles, columns, near_):
                    for h, u, q, k, n in units(b, s, tiles):
                        act.wait_ge(turned, u + 1)
                        if from_(u, 2):
                            act.wait_ge(product, u - 1)
                        for j in range(0, k, 2):
                            m = min(2, k - j)
                            last = act.activation(turned_ends[:, h, j:j + m, :, 0:n].rearrange("p j e c -> p (j e) c"),
                                                  ps_t[:, j * 2 * P:(j + m) * 2 * P].rearrange("p (j c) -> p j c", c=P)[:, :, 0:n], ACT.Copy)
                        last.then_inc(evacuated, 1)
                        b_, h_, s_ = before(b, h, s)
                        if from_(b_, 0):
                            gate(b_, h_, 3, P)
                        if h == 1 and from_(b, 1):
                            copy_span(b - 1, 1 - s, (b - 1 - (1 - s)) // 2 if isinstance(b, int) else use - (1 - s), SPAN, near_)
                over_near_and_far(act, step)
                gate(BLOCKS, 0, 1, TAIL)
                copy_span(BLOCKS - 1, 0, PAIRS, SPAN)
                copy_span(BLOCKS, 1, PAIRS, WINDOWS[0][1])

            @block.vector
            def _(dve):
                dve.memset(dst_row[:, 0, 0:P], -1).then_inc(ready, 1)
                dve.memset(edge[D0:D0 + 1, :, :], 1.0).then_inc(ready, 1)
                dve.wait_ge(ready, 2)
                dve.wait_ge(counted, 1)

                def index(b, s):
                    dve.tensor_copy(src_here[:, s, :], src_ix[:, bass.ds(b * T, T)])
                    dve.tensor_copy(dst_here[:, s, :], dst_ix[:, bass.ds(b * T, T)]).then_inc(indexed, 1)

                def put_places(b, s):
                    dve.tensor_copy(dst_f[:, s, :], dst_ix[:, bass.ds(b * T, T)])
                    dve.tensor_copy(place_f[:, s, :], place[:, bass.ds(b * T, T)]).then_inc(placed, 1)

                def shares(b, h, s, k, n):
                    ch = Chain(dve, counted_edges, 2 * b + h, 2)
                    for j in range(3 * h, 3 * h + k):
                        width = 3 * P
                        if isinstance(b, int):
                            width = min(width, N - (b * BLOCK + (j - 1) * P))
                        last = dve.tensor_scalar(equal[0:n, j % 3, 0:width], dst_row[0:n, s, j * P:j * P + width], dst_f[0:n, s, j:j + 1],
                                                 None, ALU.is_equal, op1=ALU.add, accum_out=share[0:n, s, j:j + 1])
                    ch.then(last)
                    ch.then(dve.reciprocal(share[0:n, s, 3 * h:3 * h + k], share[0:n, s, 3 * h:3 * h + k]))
                    ch.end()

                def message(b, h, s, k, n):
                    u = 2 * b + h
                    dve.wait_ge(logs, u + 1)
                    if from_(u, 2):
                        dve.wait_ge(made, u - 1)
                    logs_of = lambda part: logs_[0:n, h, 0:k, part, :]
                    dve.scalar_tensor_tensor(out=exponent[0:n, h, 0:k, :], in0=z_part(h, k, n, 0), scalar=0.0, in1=logs_of(0),
                                             op0=ALU.min, op1=ALU.subtract).then_inc(exponents, 1)
                    dve.scalar_tensor_tensor(out=value[0:n, h, 0:k, :], in0=z_part(h, k, n, 1), scalar=0.0, in1=logs_of(1),
                                             op0=ALU.max, op1=ALU.add).then_inc(values, 1)
                    if from_(u, 2):
                        dve.wait_ge(used, u - 1)
                    for j in range(3 * h, 3 * h + k):
                        width = WINDOWS[j][1]
                        last = dve.tensor_scalar(match[0:n, h, j % 3, 0:width], count[0:n, 0:width], place_f[0:n, s, j:j + 1], None,
                                                 ALU.is_equal)
                    last.then_inc(matched, 1)
                    dve.wait_ge(values, u + 1)
                    dve.wait_ge(gated, u + 1)
                    for j in range(k):
                        last = dve.scalar_tensor_tensor(out=msg[0:n, h, j, :], in0=exponent[0:n, h, j, :], scalar=share[0:n, s, 3 * h + j:3 * h + j + 1],
                                                        in1=value[0:n, h, j, :], op0=ALU.mult, op1=ALU.mult)
                    last.then_inc(made, 1)

                def add_span(b, s):
                    at = dve.value_load(base[0:1, bass.ds(b, 1)], min_val=0, max_val=(NEAR + 2) * BLOCK - SPAN)
                    dve.wait_ge(copied, b + 1)
                    if from_(b, 1):
                        dve.wait_ge(joined, b)
                    here = feat[:, bass.ds(at, SPAN)]
                    dve.tensor_tensor(here, here, span_out[:, s, 0:SPAN], ALU.add).then_inc(joined, 1)

                def step(b, s, use, tiles, columns, near_):
                    dve.wait_ge(placed, b + 1)
                    dve.wait_ge(row_loaded[s], use * 16 + 16)
                    for h, u, q, k, n in units(b, s, tiles):
                        shares(b, h, s, k, n)
                        b_, h_, s_ = before(b, h, s)
                        if from_(b_, 0):
                            message(b_, h_, s_, 3, P)
                        if h == 0 and tiles == T:
                            if from_(b, 1):
                                dve.wait_ge(matched, 2 * b)
                                dve.wait_ge(made, 2 * b)
                                alone(dve)
                            put_places(b + 1, 1 - s)
                        if h == 1 and (not isinstance(b, int) or b + 2 <= BLOCKS):
                            dve.wait_ge(turned, 2 * b + 2)
                            alone(dve)
                            index(b + 2, s)
                        if h == 0 and from_(b, 2) and is_near(b, 2, near_):
                            if isinstance(b, int) and b == 2:
                                dve.wait_ge(nodes_loaded[1], 16)
                            dve.wait_ge(nodes_loaded[s], use * 16 + 16)
                            add_span(b - 2, s)

                index(0, 0)
                index(1, 1)
                put_places(0, 0)
                over_near_and_far(dve, step)
                message(BLOCKS, 0, 1, 1, TAIL)


def assemble(nc, x_t, spans, base, feat, vecs, scale, gamma, beta, when):
    with ExitStack() as ctx:
        span = ctx.enter_context(sbuf(nc, "span", [P, 4, SPAN], F32))
        mv = ctx.enter_context(sbuf(nc, "mv", [P, 4], F32))
        stats = ctx.enter_context(psum(nc, "stats", [P, 2 * BANK], F32))
        with phase(nc, "nodes0 nodes1 nodes2 nodes3 span0 span1 span2 span3 added taken root var vec", when) as \
                (block, n0, n1, n2, n3, s0, s1, s2, s3, added, taken, root, var, vec):
            nodes_loaded, span_loaded = (n0, n1, n2, n3), (s0, s1, s2, s3)

            @block.sync
            def _(sp):
                def nodes(b, s, columns):
                    sp.dma_start(feat[:, bass.ds(b * BLOCK, columns)], x_t[:, bass.ds(b * BLOCK, columns)]).then_inc(nodes_loaded[s], 16)

                def sums(b, s, width):
                    sp.dma_start(span[:, s, 0:width], spans[bass.ds(b, 1), :, 0:width].rearrange("a p c -> (a p) c")).then_inc(span_loaded[s], 16)

                def load(b, q, use, tiles, columns):
                    if not isinstance(b, int) or b >= NEAR + 5:
                        sp.wait_ge(added, b - (NEAR + 3))
                        alone(sp)
                    if tiles == T and not (isinstance(b, int) and b == NEAR):
                        nodes(b + 1, (q + 1) % 4, TAIL if isinstance(b, int) and b == BLOCKS - 1 else BLOCK)
                    if not isinstance(b, int) or b > NEAR:
                        sums(b - 1, (q + 3) % 4, SPAN)

                for q in range(2):
                    sp.sem_inc(nodes_loaded[q], 16)
                over_blocks_by_four(sp, load, NEAR)
                sp.wait_ge(added, BLOCKS - NEAR - 2)
                alone(sp)
                sums(BLOCKS, BLOCKS % 4, WINDOWS[0][1])

            @block.scalar
            def _(act):
                root_of(act, root, var, mv)

            @block.vector
            def _(dve):
                dve.memset(feat[:, N:NODES], 0.0).then_inc(added, 1)

                def add_span(b, s, use, width):
                    at = dve.value_load(base[0:1, bass.ds(b, 1)], min_val=0, max_val=NODES - width)
                    dve.wait_ge(span_loaded[s], use * 16 + 16)
                    dve.wait_ge(added, b - (NEAR - 1))
                    here = feat[:, bass.ds(at, width)]
                    dve.tensor_tensor(here, here, span[:, s, 0:width], ALU.add).then_inc(added, 1)

                def statistics(b, columns, spans_added):
                    dve.wait_ge(added, spans_added)
                    alone(dve)
                    for c, at, n in halves(columns):
                        last = dve.bn_stats(stats[:, bass.ds((2 * b + c) * 6, 6)], feat[:, bass.ds(b * BLOCK + at, n)])
                    last.then_inc(taken, 1)

                def step(b, q, use, tiles, columns):
                    if tiles == T:
                        dve.wait_ge(nodes_loaded[(q + 1) % 4], (use + (q == 3)) * 16 + 16)
                    if not isinstance(b, int) or b > NEAR:
                        add_span(b - 1, (q + 3) % 4, use - (q == 0), SPAN)
                    statistics(b - 3, BLOCK, max(1, b - NEAR) if isinstance(b, int) else b - NEAR)
                with dve.Fori(0, NEAR - 3) as b:
                    statistics(b, BLOCK, 1)
                over_blocks_by_four(dve, step, NEAR)
                add_span(BLOCKS, BLOCKS % 4, (BLOCKS - NEAR) // 4, WINDOWS[0][1])
                for b in range(BLOCKS - 2, BLOCKS + 1):
                    statistics(b, BLOCK if b < BLOCKS else TAIL, BLOCKS - NEAR + 2)
                dve.wait_ge(taken, BLOCKS + 1)
                batch_scale(dve, root, var, Chain(dve, vec, 0, 4), stats[:, 0:CHUNKS * 6], mv, scale, vecs, gamma, beta)


def load_nodes(nc, x_t, feat, when):
    with phase(nc, "loaded", when) as (block, loaded):
        @block.sync
        def _(sp):
            sp.dma_start(feat[:, 0:N], x_t).then_inc(loaded, 16)
            sp.wait_ge(loaded, 16)

        @block.vector
        def _(dve):
            dve.memset(feat[:, N:NODES], 0.0)


def zero_rows(nc, agg, when):
    rows, width = agg.shape
    words = rows * width // 16
    piece = 1
    for k in range(1, 3001):
        if words % k == 0:
            piece = k
    flat = agg.rearrange("r w -> (r w)").rearrange("(a n) -> a n", a=16)
    with ExitStack() as ctx:
        zeros = ctx.enter_context(sbuf(nc, "zeros", [16, piece], F32))
        with phase(nc, "zeros_set zeroed", when) as (block, zeros_set, zeroed):
            @block.vector
            def _(dve):
                dve.memset(zeros[:, :], 0.0).then_inc(zeros_set, 1)

            @block.sync
            def _(sp):
                sp.wait_ge(zeros_set, 1)
                with sp.Fori(0, words // piece) as k:
                    sp.dma_start(flat[:, bass.ds(k * piece, piece)], zeros[:, :]).then_inc(zeroed, 16)
                sp.wait_ge(zeroed, words // piece * 16)


def scatter_messages(nc, table, edges, gates, ident, src_ix, dst_ix, agg, when):
    zero_rows(nc, agg, when)
    width = agg.shape[1]
    d = edges.shape[1]
    with ExitStack() as ctx:
        sb = lambda name, shape, dt=F32: ctx.enter_context(sbuf(nc, name, shape, dt))
        six, dix, gix = (sb(n, [P, 1], I32) for n in ("six", "dix", "gix"))
        ds_, spare, low, to, tof = (sb(n, [P, 1]) for n in ("dst_here", "spare", "low", "to", "tof"))
        same, tmp, lower = sb("same", [P, P]), sb("tmp", [P, P]), sb("lower", [P, P])
        xs, ed, msg, total = sb("xs", [P, C]), sb("ed", [P, d]), sb("msg", [P, width]), sb("total", [P, width])
        if gates:
            xd, tT = sb("xd", [P, C]), sb("tT", [P, 3, P])
            weights = sb("gate_w", [P, 3, 2 * C])
            e1, e2 = sb("e1", [P, C]), sb("e2", [P, C])
        ps_d = ctx.enter_context(psum(nc, "ps_dst", [P, BANK], F32))
        ps_m = ctx.enter_context(psum(nc, "ps_total", [P, BANK], F32))
        ps_t = ctx.enter_context(psum(nc, "ps_turned", [P, 3, P], F32))
        ps_z = ctx.enter_context(psum(nc, "ps_z", [P, 2 * C], F32))
        names = "ready wloaded indexed dst_turned edge_loaded gathered added index_made msg_made summed total_made turned turned_copied gated gate_vals vec"
        with phase(nc, names, when) as (block, ready, wloaded, indexed, dst_turned, edge_loaded, gathered, added, index_made,
                                  msg_made, summed, total_made, turned, turned_copied, gated, gate_vals, vec):
            @block.sync
            def _(sp):
                if gates:
                    sp.dma_start(weights[:, 0, :], gates[0]).then_inc(wloaded, 16)
                    sp.dma_start(weights[:, 1, :], gates[1]).then_inc(wloaded, 16)
                    sp.dma_start(weights[0:D0 + 1, 2, :], gates[2]).then_inc(wloaded, 16)

                def load(t, rows):
                    sp.wait_ge(indexed, t + 1)
                    alone(sp)
                    sp.dma_start(ed[0:rows, :], edges[bass.ds(t * P, rows), :]).then_inc(edge_loaded, 16)
                over_tiles(sp, load)

            @block.gpsimd
            def _(pool):
                pool.iota(gix[:, :], [[0, 1]], base=N, channel_multiplier=1).then_inc(ready, 1)
                pool.memset(lower[:, :], 1.0).then_inc(ready, 1)
                pool.wait_ge(ready, 2)
                pool.affine_select(out=lower[:, :], in_=lower[:, :], compare_op=ALU.is_gt, fill=0.0,
                                   base=0, pattern=[[-1, P]], channel_multiplier=1).then_inc(ready, 1)

                def tile(t, rows):
                    pool.wait_ge(indexed, t + 1)
                    alone(pool)
                    pool.indirect_dma_start(xs[0:rows, :], None, table,
                                            bass.IndirectOffsetOnAxis(ap=six[0:rows, 0:1], axis=0)).then_inc(gathered, 16)
                    if gates:
                        pool.indirect_dma_start(xd[0:rows, :], None, table,
                                                bass.IndirectOffsetOnAxis(ap=dix[0:rows, 0:1], axis=0)).then_inc(gathered, 16)
                    pool.wait_ge(total_made, t + 1)
                    alone(pool)
                    pool.indirect_dma_start(agg, bass.IndirectOffsetOnAxis(ap=dix[0:rows, 0:1], axis=0),
                                            total[0:rows, :], None, compute_op=ALU.add).then_inc(added, 16)
                over_tiles(pool, tile)

            @block.tensor
            def _(pe):
                if gates:
                    pe.wait_ge(wloaded, 48)

                def tile(t, rows):
                    pe.wait_ge(indexed, t + 1)
                    pe.transpose(ps_d[0:rows, 0:rows], ds_[0:rows, 0:1].to_broadcast([rows, rows]),
                                 ident[0:rows, 0:rows]).then_inc(dst_turned, 1)
                    if gates:
                        pe.wait_ge(gathered, 32 * t + 32)
                        pe.wait_ge(edge_loaded, 16 * t + 16)
                        pe.transpose(ps_t[:, 0, 0:rows], xs[0:rows, :], ident[0:rows, 0:rows])
                        pe.transpose(ps_t[:, 1, 0:rows], xd[0:rows, :], ident[0:rows, 0:rows])
                        pe.transpose(ps_t[0:D0, 2, 0:rows], ed[0:rows, :], ident[0:rows, 0:rows]).then_inc(turned, 1)
                        pe.wait_ge(turned_copied, t + 1)
                        pe.matmul(ps_z[0:rows, :], tT[:, 0, 0:rows], weights[:, 0, :], start=True, stop=False)
                        pe.matmul(ps_z[0:rows, :], tT[:, 1, 0:rows], weights[:, 1, :], start=False, stop=False)
                        pe.matmul(ps_z[0:rows, :], tT[0:D0 + 1, 2, 0:rows], weights[0:D0 + 1, 2, :],
                                  start=False, stop=True).then_inc(gated, 1)
                    pe.wait_ge(msg_made, t + 1)
                    pe.matmul(ps_m[0:rows, 0:width], same[0:rows, 0:rows], msg[0:rows, :],
                              start=True, stop=True).then_inc(summed, 1)
                over_tiles(pe, tile)

            if gates:
                @block.scalar
                def _(act):
                    def tile(t, rows):
                        act.wait_ge(turned, t + 1)
                        act.activation(tT[:, 0:2, 0:rows], ps_t[:, 0:2, 0:rows], ACT.Copy)
                        act.activation(tT[0:D0, 2, 0:rows], ps_t[0:D0, 2, 0:rows], ACT.Copy).then_inc(turned_copied, 1)
                        act.wait_ge(gated, t + 1)
                        act.activation(e1[0:rows, :], ps_z[0:rows, 0:C], ACT.Exp, scale=-1.0)
                        act.activation(e2[0:rows, :], ps_z[0:rows, C:2 * C], ACT.Abs).then_inc(gate_vals, 1)
                        act.wait_ge(gate_vals, 3 * t + 1)
                        act.activation(e2[0:rows, :], e2[0:rows, :], ACT.Exp, scale=-1.0).then_inc(gate_vals, 1)
                        act.wait_ge(gate_vals, 3 * t + 2)
                        act.activation(e2[0:rows, :], e2[0:rows, :], ACT.Ln, bias=1.0).then_inc(gate_vals, 1)
                    over_tiles(act, tile)

            @block.vector
            def _(dve):
                dve.wait_ge(ready, 3)
                dve.tensor_copy(spare[:, :], gix[:, :]).then_inc(ready, 1)
                dve.wait_ge(ready, 4)
                if gates:
                    dve.memset(tT[D0:D0 + 1, 2, :], 1.0)
                    dve.memset(msg[:, C:AGG], 1.0).then_inc(ready, 1)
                    dve.wait_ge(ready, 5)

                def tile(t, rows):
                    ch = Chain(dve, vec, t, 7 if gates else 6)
                    r = slice(0, rows)
                    dve.tensor_copy(six[r, :], src_ix[r, bass.ds(t, 1)])
                    dve.tensor_copy(dix[r, :], dst_ix[r, bass.ds(t, 1)])
                    dve.tensor_copy(ds_[r, :], dst_ix[r, bass.ds(t, 1)]).then_inc(indexed, 1)
                    dve.wait_ge(dst_turned, t + 1)
                    dve.wait_ge(indexed, t + 1)
                    ch.then(dve.tensor_scalar(same[r, r], ps_d[r, r], ds_[r, 0:1], None, ALU.is_equal))
                    ch.then(dve.tensor_tensor_reduce(out=tmp[r, r], in0=same[r, r], in1=lower[r, r], scale=1.0, scalar=0.0,
                                                     op0=ALU.mult, op1=ALU.add, accum_out=low[r, :]))
                    ch.then(dve.tensor_tensor(to[r, :], spare[r, :], ds_[r, :], ALU.subtract))
                    ch.then(dve.scalar_tensor_tensor(out=tof[r, :], in0=low[r, :], scalar=0.0, in1=to[r, :],
                                                     op0=ALU.is_gt, op1=ALU.mult))
                    if gates:
                        dve.wait_ge(gate_vals, 3 * t + 3)
                        ch.then(dve.scalar_tensor_tensor(out=e2[r, :], in0=ps_z[r, C:2 * C], scalar=0.0, in1=e2[r, :],
                                                         op0=ALU.max, op1=ALU.add))
                        ch.then(dve.tensor_scalar(e1[r, :], e1[r, :], 1.0, None, ALU.add))
                        ch.then(dve.reciprocal(e1[r, :], e1[r, :]))
                        dve.tensor_tensor(msg[r, 0:C], e2[r, :], e1[r, :], ALU.mult).then_inc(msg_made, 1)
                    else:
                        dve.wait_ge(gathered, 16 * t + 16)
                        dve.wait_ge(edge_loaded, 16 * t + 16)
                        ch.then(dve.tensor_tensor(tmp[r, 0:C], xs[r, :], ed[r, :], ALU.add))
                        ch.mark(dve.tensor_scalar(msg[r, :], tmp[r, 0:C], 0.0, None, ALU.max))
                        ch.wait()
                        dve.sem_inc(msg_made, 1)
                    dve.wait_ge(summed, t + 1)
                    dve.tensor_copy(total[r, :], ps_m[r, 0:width])
                    dve.tensor_tensor(dix[r, :], tof[r, :], ds_[r, :], ALU.add).then_inc(total_made, 1)
                    dve.wait_ge(added, 16 * t + 16)
                    ch.end()
                over_tiles(dve, tile)


def sorted_messages(nc, table, edges, src_ix, place, base, w, feat, vecs, scale, bias, gamma, beta, when):
    with ExitStack() as ctx:
        sb = lambda name, shape, dt=F32: ctx.enter_context(sbuf(nc, name, shape, dt))
        msg = sb("msg", [P, 4, 3, C])
        edge = sb("edge", [P, 2, 3, C])
        match = [sb(f"match{j}", [P, width]) for j, (_, width) in enumerate(WINDOWS)]
        count = sb("count", [P, WIDEST], I16)
        index = sb("index", [P, 2, T], I32)
        at_ = sb("place_here", [P, 2, T])
        w_sb, mv = sb("w_sb", [P, C]), sb("mv", [P, 4])
        span = [ctx.enter_context(psum(nc, f"ps_span{s}", [P, 2 * BANK], F32)) for s in range(2)]
        ps = ctx.enter_context(psum(nc, "ps_h", [P, 2, BANK], F32))
        stats = ctx.enter_context(psum(nc, "stats", [P, 2 * BANK], F32))
        names = ("w_loaded counted indexed placed gathered0 gathered1 gathered2 gathered3 edge0 edge1 summed made matched "
                 "tile_used added product stored taken root var vec")
        with phase(nc, names, when) as (block, w_loaded, counted, indexed, placed, g0, g1, g2, g3, e0, e1, summed, made, matched,
                                        tile_used, added, product, stored, taken, root, var, vec):
            gathered, edge_loaded = (g0, g1, g2, g3), (e0, e1)
            last_step = BLOCKS + 1

            def units(b, s, tiles):
                return [(h, 2 * b + h, 2 * s + h, 3) for h in range(2)] if tiles == T else [(0, 2 * b, 2 * s, 1)]

            @block.sync
            def _(sp):
                sp.dma_start(w_sb[:, :], w).then_inc(w_loaded, 16)

                def load(b, s, use, tiles, columns):
                    for h, u, _, n in units(b, s, tiles):
                        sp.wait_ge(summed, u + 1)
                        alone(sp)
                        if tiles == T:
                            rows = edges[bass.ds(b * BLOCK + h * HALF, HALF), :].rearrange("(t p) c -> p t c", p=P)
                            sp.dma_start(edge[:, h, :, :], rows).then_inc(edge_loaded[h], 16)
                        else:
                            sp.dma_start(edge[0:columns, h, 0, :], edges[N - columns:N, :]).then_inc(edge_loaded[h], 16)
                over_blocks(sp, load, 2)

            @block.gpsimd
            def _(pool):
                pool.iota(count[:, :], [[1, WIDEST]], base=0, channel_multiplier=0).then_inc(counted, 1)

                def gather(b, s, use, tiles, columns):
                    pool.wait_ge(indexed, b + 1)
                    alone(pool)
                    n = P if tiles == T else columns
                    for h, u, q, k in units(b, s, tiles):
                        if not isinstance(u, int) or u >= 4:
                            pool.wait_ge(tile_used, b * T + (3 * h - 7))
                            alone(pool)
                        for j in range(k):
                            pool.indirect_dma_start(msg[0:n, q, j, :], None, table, bass.IndirectOffsetOnAxis(
                                ap=index[0:n, s, 3 * h + j:3 * h + j + 1], axis=0)).then_inc(gathered[q], 16)
                over_blocks(pool, gather, 2)

            @block.scalar
            def _(act):
                act.sem_inc(stored, 1)

                def store(b, columns):
                    act.wait_ge(product, b + 1)
                    alone(act)
                    act.activation(feat_block(feat, b, columns), banks(ps, columns), ACT.Identity,
                                   bias=vecs[:, bias:bias + 1]).then_inc(stored, 1)

                def step(b, s, use, tiles, columns):
                    n = P if tiles == T else columns
                    for h, u, q, k in units(b, s, tiles):
                        act.wait_ge(summed, u + 3)
                        act.activation(msg[0:n, q, 0:k, :], msg[0:n, q, 0:k, :], ACT.Relu).then_inc(made, 1)
                    if not isinstance(b, int) or b >= LAG:
                        store(b - LAG, BLOCK)
                over_blocks(act, step, 2)
                for b in range(last_step - LAG, last_step):
                    store(b, BLOCK if b < BLOCKS else TAIL)
                root_of(act, root, var, mv)

            @block.vector
            def _(dve):
                dve.sem_inc(summed, 2)
                dve.wait_ge(counted, 1)

                def put_index(b, s):
                    dve.tensor_copy(index[:, s, :], src_ix[:, bass.ds(b * T, T)]).then_inc(indexed, 1)

                def put_places(b, s):
                    dve.tensor_copy(at_[:, s, :], place[:, bass.ds(b * T, T)]).then_inc(placed, 1)

                def add_span(b, s, width, tiles=T):
                    at = dve.value_load(base[0:1, bass.ds(b, 1)], min_val=0, max_val=NODES - width)
                    dve.wait_ge(tile_used, b * T + (tiles + 2))
                    dve.wait_ge(added, b + 1)
                    here = feat[:, bass.ds(at, width)]
                    dve.tensor_tensor(here, here, span[s][:, 0:width], ALU.add).then_inc(added, 1)

                def statistics(b, columns):
                    dve.wait_ge(stored, b + 2)
                    alone(dve)
                    for c, at, n in halves(columns):
                        last = dve.bn_stats(stats[:, bass.ds((2 * b + c) * 6, 6)], feat[:, bass.ds(b * BLOCK + at, n)])
                    last.then_inc(taken, 1)

                def step(b, s, use, tiles, columns):
                    n = P if tiles == T else columns
                    more = not isinstance(b, int) or b + 2 <= BLOCKS
                    dve.wait_ge(placed, b + 1)
                    for h, u, q, k in units(b, s, tiles):
                        dve.wait_ge(gathered[q], (use * 3 + k) * 16)
                        if h == 1 and more:
                            alone(dve)
                            put_index(b + 2, s)
                        dve.wait_ge(edge_loaded[h], b * 16 + 16)
                        dve.tensor_tensor(msg[0:n, q, 0:k, :], msg[0:n, q, 0:k, :], edge[0:n, h, 0:k, :], ALU.add).then_inc(summed, 1)
                        for j in range(3 * h, 3 * h + k):
                            width = WINDOWS[j][1]
                            if not isinstance(b, int) or b >= 1:
                                dve.wait_ge(tile_used, b * T + (j + 3 - T))
                            dve.tensor_scalar(match[j][0:n, :], count[0:n, 0:width], at_[0:n, s, j:j + 1], None,
                                              ALU.is_equal).then_inc(matched, 1)
                    if more:
                        dve.wait_ge(matched, b * T + T)
                        alone(dve)
                        put_places(b + 2, s)
                    if not isinstance(b, int) or b >= 1:
                        add_span(b - 1, 1 - s, SPAN)
                    if not isinstance(b, int) or b > LAG:
                        statistics(b - LAG - 1, BLOCK)

                dve.sem_inc(added, 1)
                for b in range(2):
                    put_index(b, b)
                    put_places(b, b)
                over_blocks(dve, step, 2)
                add_span(BLOCKS, 1, WINDOWS[0][1], 1)
                for b in range(last_step - LAG - 1, last_step):
                    statistics(b, BLOCK if b < BLOCKS else TAIL)
                dve.wait_ge(taken, BLOCKS + 1)
                batch_scale(dve, root, var, Chain(dve, vec, 0, 4), stats[:, 0:CHUNKS * 6], mv, scale, vecs, gamma, beta)

            @block.tensor
            def _(pe):
                pe.wait_ge(w_loaded, 16)
                pe.sem_inc(tile_used, 2)

                def multiply(b, columns, spans_added):
                    pe.wait_ge(added, spans_added)
                    pe.wait_ge(stored, b + 1)
                    for c, at, n in halves(columns):
                        last = pe.matmul(ps[:, c, 0:n], w_sb[:, :], feat[:, bass.ds(b * BLOCK + at, n)], start=True, stop=True)
                    last.then_inc(product, 1)

                def step(b, s, use, tiles, columns):
                    n = P if tiles == T else columns
                    if not isinstance(b, int) or b >= LAG:
                        multiply(b - LAG, BLOCK, b)
                    if not isinstance(b, int) or b >= 2:
                        pe.wait_ge(added, b)
                    for h, u, q, k in units(b, s, tiles):
                        pe.wait_ge(made, u + 1)
                        for j in range(3 * h, 3 * h + k):
                            first_col, width = WINDOWS[j]
                            pe.wait_ge(matched, b * T + j + 1)
                            for lo, hi in bank_parts(first_col, width):
                                last = pe.matmul(span[s][:, lo:hi], msg[0:n, q, j % 3, :],
                                                 match[j][0:n, lo - first_col:hi - first_col],
                                                 start=j == 0 or (j == 3 and lo >= BANK), stop=True, skip_group_check=True)
                            last.then_inc(tile_used, 1)
                over_blocks(pe, step, 2)
                for b in range(last_step - LAG, last_step):
                    multiply(b, BLOCK if b < BLOCKS else TAIL, last_step + 1)


def bank_parts(first_col, width):
    end = first_col + width
    if first_col < BANK < end:
        return [(first_col, BANK), (BANK, end)]
    return [(first_col, end)]


def add_sums(nc, agg, feat, ident, mean, when):
    width = agg.shape[1]
    with ExitStack() as ctx:
        sb = lambda name, shape, dt=F32: ctx.enter_context(sbuf(nc, name, shape, dt))
        rows_ = sb("sum_rows", [P, width])
        cnt, rec = sb("cnt", [P, 1]), sb("rec", [P, 1])
        ps = ctx.enter_context(psum(nc, "ps_sums", [P, P], F32))
        with phase(nc, "loaded scaled turned added vec", when) as (block, loaded, scaled, turned, added, vec):
            @block.sync
            def _(sp):
                sp.sem_inc(added, 1)

                def load(t, rows):
                    sp.wait_ge(added, t + 1)
                    alone(sp)
                    sp.dma_start(rows_[0:rows, :], agg[bass.ds(t * P, rows), :]).then_inc(loaded, 16)
                over_tiles(sp, load)

            @block.tensor
            def _(pe):
                def tile(t, rows):
                    pe.wait_ge(scaled, t + 1)
                    pe.transpose(ps[:, 0:rows], rows_[0:rows, 0:C], ident[0:rows, 0:rows]).then_inc(turned, 1)
                over_tiles(pe, tile)

            @block.vector
            def _(dve):
                def tile(t, rows):
                    r = slice(0, rows)
                    dve.wait_ge(loaded, 16 * t + 16)
                    if mean:
                        ch = Chain(dve, vec, t, 3)
                        ch.then(dve.tensor_scalar(cnt[r, :], rows_[r, C:C + 1], 1.0, None, ALU.max))
                        ch.then(dve.reciprocal(rec[r, :], cnt[r, :]))
                        ch.then(dve.tensor_scalar(rows_[r, 0:C], rows_[r, 0:C], rec[r, 0:1], None, ALU.mult))
                        ch.end()
                    dve.sem_inc(scaled, 1)
                    dve.wait_ge(turned, t + 1)
                    here = feat[:, bass.ds(t * P, rows)]
                    dve.tensor_tensor(here, here, ps[:, 0:rows], ALU.add).then_inc(added, 1)
                over_tiles(dve, tile)


def batch_scale(dve, act_sem, var_sem, chain, stats, mv, scale, vecs, gamma, beta, bias=None):
    chain.then(dve.bn_aggr(mv[:, 0:2], stats))
    dve.tensor_scalar(mv[:, 1:2], mv[:, 1:2], EPS, None, ALU.add).then_inc(var_sem, 1)
    dve.wait_ge(act_sem, 1)
    chain.then(dve.reciprocal(mv[:, 3:4], mv[:, 2:3]))
    chain.then(dve.tensor_tensor(scale[:, 0:1], mv[:, 3:4], vecs[:, gamma:gamma + 1], ALU.mult))
    if bias is not None:
        chain.then(dve.tensor_tensor(mv[:, 0:1], mv[:, 0:1], vecs[:, bias:bias + 1], ALU.add))
    chain.then(dve.tensor_tensor(mv[:, 3:4], mv[:, 0:1], scale[:, 0:1], ALU.mult))
    dve.tensor_tensor(scale[:, 1:2], vecs[:, beta:beta + 1], mv[:, 3:4], ALU.subtract)


def root_of(act, act_sem, var_sem, mv):
    act.wait_ge(var_sem, 1)
    act.activation(mv[:, 2:3], mv[:, 1:2], ACT.Sqrt).then_inc(act_sem, 1)


def norm_stats(nc, feat, vecs, scale, gamma, beta, when):
    with ExitStack() as ctx:
        stats = ctx.enter_context(sbuf(nc, "stats", [P, CHUNKS, 6], F32))
        mv = ctx.enter_context(sbuf(nc, "mv", [P, 4], F32))
        with phase(nc, "taken root var vec", when) as (block, taken, root, var, vec):
            @block.vector
            def _(dve):
                def take(b, s, use, tiles, columns):
                    for c, at, w in halves(columns):
                        dve.bn_stats(stats[:, bass.ds(2 * b + c, 1), :].rearrange("p a b -> p (a b)"),
                                     feat[:, bass.ds(b * BLOCK + at, w)]).then_inc(taken, 1)
                over_blocks(dve, take)
                dve.wait_ge(taken, CHUNKS)
                batch_scale(dve, root, var, Chain(dve, vec, 0, 4), stats[:, :, :].rearrange("p a b -> p (a b)"), mv, scale, vecs, gamma, beta)

            @block.scalar
            def _(act):
                root_of(act, root, var, mv)


def first_product(nc, w, feat, vecs, scale, bias, gamma, beta, when):
    with ExitStack() as ctx:
        stats = ctx.enter_context(sbuf(nc, "stats", [P, CHUNKS, 6], F32))
        mv = ctx.enter_context(sbuf(nc, "mv", [P, 4], F32))
        w_sb = ctx.enter_context(sbuf(nc, "w_sb", [P, C], F32))
        ps = [ctx.enter_context(psum(nc, f"ps_h{s}", [P, 2, BANK], F32)) for s in range(2)]
        with phase(nc, "w_loaded product taken stored root var vec", when) as (block, w_loaded, product, taken, stored, root, var, vec):
            @block.sync
            def _(sp):
                sp.dma_start(w_sb[:, :], w).then_inc(w_loaded, 16)

            @block.tensor
            def _(pe):
                pe.wait_ge(w_loaded, 16)

                def multiply(b, s, use, tiles, columns):
                    pe.wait_ge(stored, b + 1)
                    for c, at, n in halves(columns):
                        last = pe.matmul(ps[s][:, c, 0:n], w_sb[:, :], feat[:, bass.ds(b * BLOCK + at, n)], start=True, stop=True)
                    last.then_inc(product, 1)
                over_blocks(pe, multiply)

            @block.scalar
            def _(act):
                act.sem_inc(stored, 2)

                def store(b, s, use, tiles, columns):
                    act.wait_ge(product, b + 1)
                    alone(act)
                    act.activation(feat_block(feat, b, columns), banks(ps[s], columns), ACT.Identity,
                                   bias=vecs[:, bias:bias + 1]).then_inc(stored, 1)
                over_blocks(act, store)
                root_of(act, root, var, mv)

            @block.vector
            def _(dve):
                def take(b, s, use, tiles, columns):
                    dve.wait_ge(stored, b + 3)
                    alone(dve)
                    for c, at, n in halves(columns):
                        last = dve.bn_stats(stats[:, bass.ds(2 * b + c, 1), :].rearrange("p a b -> p (a b)"),
                                            feat[:, bass.ds(b * BLOCK + at, n)])
                    last.then_inc(taken, 1)
                over_blocks(dve, take)
                dve.wait_ge(taken, BLOCKS + 1)
                batch_scale(dve, root, var, Chain(dve, vec, 0, 4), stats[:, :, :].rearrange("p a b -> p (a b)"), mv, scale, vecs, gamma, beta)


def second_product(nc, w, feat, vecs, scale, bias, gamma, beta):
    with ExitStack() as ctx:
        stats = ctx.enter_context(sbuf(nc, "stats", [P, CHUNKS, 6], F32))
        mv = ctx.enter_context(sbuf(nc, "mv", [P, 4], F32))
        w_sb = ctx.enter_context(sbuf(nc, "w_sb", [P, C], F32))
        hidden = ctx.enter_context(sbuf(nc, "hidden", [P, 2, BLOCK], F32))
        ps = [ctx.enter_context(psum(nc, f"ps_h{s}", [P, 2, BANK], F32)) for s in range(4)]
        with phase(nc, "w_loaded made product taken used stored root var vec") as (block, w_loaded, made, product, taken, used, stored, root, var, vec):
            @block.sync
            def _(sp):
                sp.dma_start(w_sb[:, :], w).then_inc(w_loaded, 16)

            @block.scalar
            def _(act):
                def make(b, q, use, tiles, columns):
                    if not isinstance(b, int) or b >= 2:
                        act.wait_ge(product, b - 1)
                        alone(act)
                    act.activation(hidden[:, q % 2, 0:columns], feat[:, bass.ds(b * BLOCK, columns)], ACT.Relu,
                                   bias=scale[:, 1:2], scale=scale[:, 0:1]).then_inc(made, 1)
                    if not isinstance(b, int) or b >= 2:
                        store(b - 2, (q + 2) % 4)

                def store(b, q):
                    act.wait_ge(taken, b + 1)
                    alone(act)
                    act.activation(feat[:, bass.ds(b * BLOCK + HALF, HALF)], ps[q][:, 1, 0:HALF], ACT.Identity,
                                   bias=vecs[:, bias:bias + 1]).then_inc(stored, 1)
                over_blocks_by_four(act, make)
                store(BLOCKS - 1, 0)
                root_of(act, root, var, mv)

            @block.tensor
            def _(pe):
                pe.wait_ge(w_loaded, 16)

                def multiply(b, q, use, tiles, columns):
                    if not isinstance(b, int) or b >= 4:
                        pe.wait_ge(used, b - 3)
                        pe.wait_ge(stored, b - 3)
                    pe.wait_ge(made, b + 1)
                    for c, at, n in halves(columns):
                        last = pe.matmul(ps[q][:, c, 0:n], w_sb[:, :], hidden[:, q % 2, at:at + n], start=True, stop=True)
                    last.then_inc(product, 1)
                over_blocks_by_four(pe, multiply)

            @block.vector
            def _(dve):
                def take(b, q, use, tiles, columns):
                    dve.wait_ge(product, b + 1)
                    alone(dve)
                    for c, at, n in reversed(halves(columns)):
                        last = dve.bn_stats(stats[:, bass.ds(2 * b + c, 1), :].rearrange("p a b -> p (a b)"), ps[q][:, c, 0:n])
                        if c == 1:
                            last.then_inc(taken, 1)
                    n = min(columns, HALF)
                    dve.tensor_scalar(feat[:, bass.ds(b * BLOCK, n)], ps[q][:, 0, 0:n], vecs[:, bias:bias + 1], None,
                                      ALU.add).then_inc(used, 1)
                over_blocks_by_four(dve, take)
                dve.wait_ge(used, BLOCKS + 1)
                batch_scale(dve, root, var, Chain(dve, vec, 0, 5), stats[:, :, :].rearrange("p a b -> p (a b)"), mv, scale, vecs, gamma, beta, bias)


def write_table(nc, feat, scale, ident, table):
    with ExitStack() as ctx:
        new = ctx.enter_context(sbuf(nc, "new", [P, 2, BLOCK], F32))
        rows = ctx.enter_context(sbuf(nc, "rows", [P, 4, T, C], F32))
        ps = [ctx.enter_context(psum(nc, f"ps_turn{q}", [P, 2, BANK], F32)) for q in range(4)]
        with phase(nc, "made kept turned rows_made written0 written1 written2 written3") as \
                (block, made, kept, turned, rows_made, wr0, wr1, wr2, wr3):
            written = (wr0, wr1, wr2, wr3)

            @block.scalar
            def _(act):
                def make(b, q, use, tiles, columns):
                    if not isinstance(b, int) or b >= 2:
                        act.wait_ge(turned, b - 1)
                        act.wait_ge(kept, b - 1)
                        alone(act)
                    act.activation(new[:, q % 2, 0:columns], feat[:, bass.ds(b * BLOCK, columns)], ACT.Relu,
                                   bias=scale[:, 1:2], scale=scale[:, 0:1]).then_inc(made, 1)
                over_blocks_by_four(act, make)

            @block.tensor
            def _(pe):
                def turn(b, q, use, tiles, columns):
                    if not isinstance(b, int) or b >= 4:
                        pe.wait_ge(rows_made, b - 3)
                    pe.wait_ge(made, b + 1)
                    n = P if columns == BLOCK else columns
                    for j in range(tiles):
                        last = pe.transpose(tile_in_banks(ps[q], j, n, P), new[:, q % 2, j * P:j * P + n], ident[:, :])
                    last.then_inc(turned, 1)
                over_blocks_by_four(pe, turn)

            @block.vector
            def _(dve):
                def store(b, q, use, tiles, columns):
                    dve.wait_ge(made, b + 1)
                    alone(dve)
                    dve.tensor_copy(feat[:, bass.ds(b * BLOCK, columns)], new[:, q % 2, 0:columns]).then_inc(kept, 1)
                    dve.wait_ge(turned, b + 1)
                    if not isinstance(b, int) or b >= 4:
                        dve.wait_ge(written[q], use * 16)
                    rows_of(dve.tensor_copy, rows, q, ps[q], columns).then_inc(rows_made, 1)
                over_blocks_by_four(dve, store)

            @block.sync
            def _(sp):
                def write(b, q, use, tiles, columns):
                    sp.wait_ge(rows_made, b + 1)
                    alone(sp)
                    sp.dma_start(node_block(table, b, columns), node_slot(rows, q, columns)).then_inc(written[q], 16)
                over_blocks_by_four(sp, write)
                for q in range(4):
                    sp.wait_ge(written[q], 16 * len(range(q, BLOCKS + 1, 4)))


def rows_of(copy, rows, s, ps, columns):
    if columns == BLOCK:
        return copy(rows[:, s, :, :].rearrange("p (a j) c -> p a (j c)", a=2), ps[:, :, 0:HALF])
    return copy(rows[0:columns, s, 0, :], ps[0:columns, 0, 0:C])


def layer_norm(nc, feat, scale, ident, skip, out, first_norm):
    with ExitStack() as ctx:
        sb = lambda name, shape, dt=F32: ctx.enter_context(sbuf(nc, name, shape, dt))
        normed = sb("normed", [P, 2, BLOCK])
        B = 2 if first_norm else 4
        beside = sb("beside", [P, B, BLOCK])
        rows = sb("rows", [P, 2, T, C]) if first_norm else None
        squares, centre = sb("squares", [P, 3, C], mybir.dt.bfloat16), sb("centre", [P, P])
        stats, mv = sb("row_stats", [P, 2, 3, 6]), sb("row_mv", [P, 2, T, 2])
        spread, root, rec = sb("spread", [P, 2, T]), sb("row_root", [P, 2, T]), sb("row_rec", [P, 2, T])
        ps = [ctx.enter_context(psum(nc, f"ps_rows{q}", [P, 2, BANK], F32)) for q in range(4)]
        if first_norm:
            ps, back = ps[0:2], ps[2:4]
        R = len(ps)
        with phase(nc, "centred made product loaded0 loaded1 loaded2 loaded3 spread_made taken averaged squared root_made divided rows_made turned_back feat_stored written0 written1") as \
                (block, centred, made, product, ld0, ld1, ld2, ld3, spread_made, taken, averaged, squared, root_made, divided, rows_made, turned_back,
                 feat_stored, written0, written1):
            loaded, written = (ld0, ld1, ld2, ld3), (written0, written1)

            def uses(turn, q, buffers):
                return 2 * turn + q // 2 if buffers == 2 else turn

            def earlier(b, q, lag):
                b_ = b - lag
                tiles, columns = (1, TAIL) if isinstance(b_, int) and b_ == BLOCKS else (T, BLOCK)
                return b_, (q + lag) % 2, tiles, columns, not isinstance(b_, int) or 0 <= b_ <= BLOCKS, (q - lag) % 4 % R

            def steps(eng, body, lag):
                over_blocks_by_four(eng, body)
                for b in range(BLOCKS + 1, BLOCKS + 1 + lag):
                    body(b, b % 4, b // 4, 0, 0)

            def rows_at(b, s):
                return rows[:, s, :, :] if first_norm else feat[:, bass.ds(b * BLOCK, BLOCK)].rearrange("p (t c) -> p t c", c=C)

            def tail_rows(s):
                return rows[0:TAIL, s, 0, :] if first_norm else feat[0:TAIL, BLOCKS * BLOCK:BLOCKS * BLOCK + C]

            def from_(n, k):
                return not isinstance(n, int) or n >= k

            @block.sync
            def _(sp):
                def move(b, q, turn, tiles, columns):
                    s = q % 2
                    if tiles:
                        s = q % B
                        if from_(b, B):
                            sp.wait_ge(product, b + 1 - B)
                            alone(sp)
                        if first_norm:
                            sp.dma_start(beside[:, s, 0:columns], skip[:, bass.ds(b * BLOCK, columns)]).then_inc(loaded[s], 16)
                        else:
                            sp.dma_start(node_slot(beside[:, :, :].rearrange("p s (t c) -> p s t c", c=C), s, columns),
                                         node_block(skip, b, columns)).then_inc(loaded[s], 16)
                    b_, s_, tiles_, columns_, there, r = earlier(b, q, 3)
                    if there:
                        sp.wait_ge(rows_made, b_ + 1)
                        alone(sp)
                        sp.dma_start(node_block(out, b_, columns_), rows_at(b_, s_) if tiles_ == T else tail_rows(s_)).then_inc(written[s_], 16)
                steps(sp, move, 3)
                for s in range(2):
                    sp.wait_ge(written[s], 16 * (PAIRS + 1))

            @block.scalar
            def _(act):
                def step(b, q, turn, tiles, columns):
                    s = q % 2
                    b_, s_, tiles_, columns_, there, r = earlier(b, q, 2)
                    if there:
                        n = P if tiles_ == T else TAIL
                        act.wait_ge(spread_made, b_ + 1)
                        act.activation(root[0:n, s_, 0:tiles_], spread[0:n, s_, 0:tiles_], ACT.Sqrt).then_inc(root_made, 1)
                    if tiles:
                        if from_(b, 2):
                            act.wait_ge(product, b - 1)
                            alone(act)
                        act.activation(normed[:, s, 0:columns], feat[:, bass.ds(b * BLOCK, columns)], ACT.Identity,
                                       bias=scale[:, 1:2], scale=scale[:, 0:1]).then_inc(made, 1)
                    b_, s_, tiles_, columns_, there, r = earlier(b, q, 1)
                    if there and tiles_ == T:
                        act.wait_ge(product, b_ + 1)
                        for j in range(3, T):
                            last = act.activation(squares[:, j - 3, :], tile_in_banks(ps[r], j, P, P), ACT.Square,
                                                  scale=C ** -0.5, accum_out=mv[:, s_, j, 1:2])
                        last.then_inc(squared, 1)
                    b_, s_, tiles_, columns_, there, r = earlier(b, q, 3)
                    if first_norm and there:
                        act.wait_ge(turned_back, b_ + 1)
                        alone(act)
                        act.activation(feat_block(feat, b_, columns_), banks(back[s_], columns_), ACT.Copy).then_inc(feat_stored, 1)
                steps(act, step, 3)

            @block.tensor
            def _(pe):
                pe.wait_ge(centred, 1)

                def step(b, q, turn, tiles, columns):
                    s = q % 2
                    if tiles:
                        n = P if tiles == T else TAIL
                        pe.wait_ge(loaded[q % B], uses(turn, q, B) * 16 + 16)
                        if from_(b, R):
                            pe.wait_ge(rows_made, b + 1 - R)
                        if not first_norm:
                            for c, at, m in halves(columns):
                                cols = m if tiles == T else C
                                pe.matmul(ps[q % R][0:n, c, 0:cols], ident[0:n, 0:n], beside[0:n, q % B, at:at + cols], start=True, stop=True,
                                          skip_group_check=True)
                        else:
                            for j in range(tiles):
                                pe.matmul(tile_in_banks(ps[q % R], j, n, P), beside[:, q % B, j * P:j * P + n], centre[:, :],
                                          start=j % 3 == 0, stop=True, skip_group_check=True)
                        pe.wait_ge(made, b + 1)
                        for j in range(tiles):
                            last = pe.matmul(tile_in_banks(ps[q % R], j, n, P), normed[:, s, j * P:j * P + n], centre[:, :],
                                             start=False, stop=True, skip_group_check=True)
                        last.then_inc(product, 1)
                    b_, s_, tiles_, columns_, there, r = earlier(b, q, 2)
                    if first_norm and there:
                        n = P if tiles_ == T else TAIL
                        pe.wait_ge(rows_made, b_ + 1)
                        if from_(b_, 2):
                            pe.wait_ge(feat_stored, b_ - 1)
                        for j in range(tiles_):
                            last = pe.transpose(tile_in_banks(back[s_], j, P, n), rows[0:n, s_, j, :], ident[0:n, 0:n])
                        last.then_inc(turned_back, 1)
                steps(pe, step, 2)

            @block.vector
            def _(dve):
                dve.tensor_scalar(centre[:, :], ident[:, :], -1.0 / C, None, ALU.add).then_inc(centred, 1)

                def step(b, q, turn, tiles, columns):
                    s = q % 2
                    b_, s_, tiles_, columns_, there, r = earlier(b, q, 2)
                    if there:
                        n = P if tiles_ == T else TAIL
                        dve.wait_ge(root_made, b_ + 1)
                        dve.reciprocal(rec[0:n, s_, 0:tiles_], root[0:n, s_, 0:tiles_]).then_inc(divided, 1)
                        dve.wait_ge(divided, b_ + 1)
                        if not first_norm:
                            alone(dve)
                        elif from_(b_, 2):
                            dve.wait_ge(written[s_], (uses(turn, q, 2) - 1) * 16)
                            dve.wait_ge(turned_back, b_ - 1)
                        if tiles_ == T:
                            dve.tensor_tensor(rows_at(b_, s_).rearrange("p (a j) c -> p a j c", a=2),
                                              ps[r][:, :, 0:HALF].rearrange("p a (j c) -> p a j c", c=C),
                                              rec[:, s_, :].rearrange("p (a j) -> p a j", a=2).unsqueeze(3).to_broadcast([P, 2, 3, C]),
                                              ALU.mult).then_inc(rows_made, 1)
                        else:
                            dve.tensor_scalar(tail_rows(s_), ps[r][0:n, 0, 0:C], rec[0:n, s_, 0:1], None, ALU.mult).then_inc(rows_made, 1)
                    b_, s_, tiles_, columns_, there, r = earlier(b, q, 1)
                    if there:
                        n = P if tiles_ == T else TAIL
                        dve.wait_ge(product, b_ + 1)
                        for j in range(min(3, tiles_)):
                            last = dve.bn_stats(stats[0:n, s_, j, :], tile_in_banks(ps[r], j, n, P))
                        last.then_inc(taken, 1)
                        dve.wait_ge(taken, b_ + 1)
                        alone(dve)
                        for j in range(min(3, tiles_)):
                            last = dve.bn_aggr(mv[0:n, s_, j, :], stats[0:n, s_, j, :])
                        last.then_inc(averaged, 1)
                        dve.wait_ge(averaged, b_ + 1)
                        if tiles_ == T:
                            dve.wait_ge(squared, b_ + 1)
                        dve.tensor_scalar(spread[0:n, s_, 0:tiles_], mv[0:n, s_, 0:tiles_, 1], EPS, None, ALU.add).then_inc(spread_made, 1)
                steps(dve, step, 2)


def kernel(**inputs):
    import numpy as _np
    import concourse.bacc as _bacc
    from concourse import mybir as _mybir
    from concourse.bass_utils import run_bass_kernel_spmd as _run

    get = lambda name: _np.asarray(inputs[name])
    both = _np.concatenate([get("L0_gnn_W_f"), get("L0_gnn_W_s")], axis=0).T
    biases = _np.concatenate([get("L0_gnn_b_f"), get("L0_gnn_b_s")])[None, :]
    vectors = [get("L0_gnn_gamma"), get("L0_gnn_beta")]
    for l in range(LAYERS):
        vectors += [get(f"L1_gnn_{n}")[l] for n in ("b1", "g_mlp", "be_mlp", "b2", "g_out", "be_out")]
    arrays = {
        "x": get("x"), "x_t": get("x").T, "src": get("src"), "dst": get("dst"),
        "edge128": get("edge_attr_128"), "edge64": get("edge_attr_64"), "edge64_t": get("edge_attr_64").T,
        "w_src": both[C:2 * C], "w_dst": both[0:C], "w_edge": _np.concatenate([both[2 * C:], biases], axis=0),
        "vectors": _np.stack(vectors, axis=1), "w1": get("L1_gnn_W1"), "w2": get("L1_gnn_W2"),
    }
    arrays = {f"in_{k}": _np.ascontiguousarray(v) for k, v in arrays.items()}
    nc = _bacc.Bacc("TRN2", target_bir_lowering=False, num_devices=1, dynamic_dma_scratch_size=4096)
    args = [nc.dram_tensor(k, v.shape, _mybir.dt.from_np(v.dtype), kind="ExternalInput").ap() for k, v in arrays.items()]
    out = nc.dram_tensor("out", [N, C], F32, kind="ExternalOutput").ap()
    gnn_kernel(nc, *args, out)
    r = _run(nc, [arrays], core_ids=[0])
    return r.results[0]["out"]
```
